# Optimizing a Trainium2 kernel written in Bass

```python
import numpy as np
import jax
import jax.numpy as jnp

def _softmax(x, axis=-1):
    return jax.nn.softmax(x, axis=axis)

def _gelu(x):
    return jax.nn.gelu(x, approximate=True)

def _silu(x):
    return jax.nn.silu(x)

def _sigmoid(x):
    return jax.nn.sigmoid(x)

def _layernorm(x, axis=-1, eps=1e-05):
    m = jnp.mean(x, axis=axis, keepdims=True)
    v = jnp.var(x, axis=axis, keepdims=True)
    return (x - m) / jnp.sqrt(v + eps)

def _scatter_add(tgt, idx, src, axis=0):
    return tgt.at[idx].add(src)

def _segment_sum(src, seg, n):
    return jax.ops.segment_sum(src, seg, n)
kernel_name = 'mk_gnn_preln_d4_gnn_r32_c26847'

def setup_inputs(seed: int=0):
    np.random.seed(seed)
    _w = jnp.asarray

    def _rec_inputs():
        import jax
        import jax.numpy as jnp
        _gk = jax.random.key(seed)
        x = -0.0003713 + 1 * jax.random.normal(jax.random.fold_in(_gk, 1), (50000, 128), jnp.float32)
        src = jax.random.randint(jax.random.fold_in(_gk, 2), (25000,), 0, 50000, jnp.int32)
        dst = jax.random.randint(jax.random.fold_in(_gk, 3), (25000,), 0, 50000, jnp.int32)
        _o = jnp.argsort(dst, stable=True)
        src = src[_o]
        dst = dst[_o]
        edge_attr_16 = 0.000196303 + 1.00016 * jax.random.normal(jax.random.fold_in(_gk, 12), (25000, 16), jnp.float32)
        edge_attr_64 = 0.000189758 + 1.00013 * jax.random.normal(jax.random.fold_in(_gk, 13), (25000, 64), jnp.float32)
        edge_weight = jax.random.uniform(jax.random.fold_in(_gk, 15), (25000,), jnp.float32, 0.0, 1)
        return (x, src, dst, edge_attr_16, edge_attr_64, edge_weight)
    x, src, dst, edge_attr_16, edge_attr_64, edge_weight = _rec_inputs()

    def _L0_gnn_setup():
        import jax, jax.numpy as jnp
        import numpy as np
        N_NODES = 3125
        N_EDGES = 50000
        HEADS = 4
        IN_CH = 128
        HID_CH = 128
        OUT_CH = 128
        EDGE_DIM = 16
        NEG_SLOPE = 0.2

        def gat_conv(x, src, dst, edge_attr, W, att_src, att_dst, W_edge, att_edge, bias):
            N = x.shape[0]
            H, C = att_src.shape
            E = edge_attr.shape[0]
            cnt = jax.ops.segment_sum(jnp.ones((E,), edge_attr.dtype), dst, num_segments=N)
            loop_attr = jax.ops.segment_sum(edge_attr, dst, num_segments=N) / jnp.clip(cnt, 1.0)[:, None]
            loop = jnp.arange(N)
            src_f = jnp.concatenate([src, loop])
            dst_f = jnp.concatenate([dst, loop])
            ea = jnp.concatenate([edge_attr, loop_attr], axis=0)
            xh = (x @ W).reshape(N, H, C)
            a_src = jnp.sum(xh * att_src, axis=-1)
            a_dst = jnp.sum(xh * att_dst, axis=-1)
            eh = (ea @ W_edge).reshape(-1, H, C)
            a_edge = jnp.sum(eh * att_edge, axis=-1)
            alpha = jax.nn.leaky_relu(a_src[src_f] + a_dst[dst_f] + a_edge, NEG_SLOPE)
            m = jax.ops.segment_max(alpha, dst_f, num_segments=N)
            m = jnp.where(jnp.isfinite(m), m, 0.0)
            p = jnp.exp(alpha - jax.lax.stop_gradient(m)[dst_f])
            s = jax.ops.segment_sum(p, dst_f, num_segments=N)
            alpha = p / (s[dst_f] + 1e-16)
            out = jax.ops.segment_sum(xh[src_f] * alpha[..., None], dst_f, num_segments=N)
            return out.reshape(N, H * C) + bias
        key = jax.random.key(seed)
        ks = jax.random.split(key, 16)
        C1 = HID_CH // HEADS
        C2 = OUT_CH // HEADS
        s_in = 1.0 / np.sqrt(IN_CH)
        s_hid = 1.0 / np.sqrt(HID_CH)
        s_e = 1.0 / np.sqrt(EDGE_DIM)
        return {'x': jax.random.normal(ks[0], (N_NODES, IN_CH), jnp.float32), 'edge_index': jax.random.randint(ks[1], (2, N_EDGES), 0, N_NODES, jnp.int64), 'edge_attr': jax.random.normal(ks[2], (N_EDGES, EDGE_DIM), jnp.float32), 'W1': jax.random.normal(ks[3], (IN_CH, HID_CH), jnp.float32) * s_in, 'att_src1': jax.random.normal(ks[4], (HEADS, C1), jnp.float32) * s_hid, 'att_dst1': jax.random.normal(ks[5], (HEADS, C1), jnp.float32) * s_hid, 'W_edge1': jax.random.normal(ks[6], (EDGE_DIM, HID_CH), jnp.float32) * s_e, 'att_edge1': jax.random.normal(ks[7], (HEADS, C1), jnp.float32) * s_hid, 'bias1': jnp.zeros((HID_CH,), jnp.float32), 'W2': jax.random.normal(ks[8], (HID_CH, OUT_CH), jnp.float32) * s_hid, 'att_src2': jax.random.normal(ks[9], (HEADS, C2), jnp.float32) * s_hid, 'att_dst2': jax.random.normal(ks[10], (HEADS, C2), jnp.float32) * s_hid, 'W_edge2': jax.random.normal(ks[11], (EDGE_DIM, OUT_CH), jnp.float32) * s_e, 'att_edge2': jax.random.normal(ks[12], (HEADS, C2), jnp.float32) * s_hid, 'bias2': jnp.zeros((OUT_CH,), jnp.float32)}
    _L0_gnn_all = _L0_gnn_setup()
    _L0_gnn_in = {k: v for k, v in _L0_gnn_all.items() if k in ('W1', 'att_src1', 'att_dst1', 'W_edge1', 'att_edge1', 'bias1', 'W2', 'att_src2', 'att_dst2', 'W_edge2', 'att_edge2', 'bias2')}
    del _L0_gnn_all

    def _L1_gnn_setup():
        import jax, jax.numpy as jnp
        import numpy as np
        N_NODES = 3125
        D = 128
        N_EDGES = 50000
        NUM_LAYERS = 3
        key = jax.random.key(seed)
        k1, k2, k3, k4 = jax.random.split(key, 4)
        ebds = jax.random.normal(k1, (N_NODES, D), dtype=jnp.float32)
        edge_val = jax.random.uniform(k2, (N_EDGES,), dtype=jnp.float32)
        edge_row = jax.random.randint(k3, (N_EDGES,), 0, N_NODES, dtype=jnp.int32)
        edge_col = jax.random.randint(k4, (N_EDGES,), 0, N_NODES, dtype=jnp.int32)
        return {'ebds': ebds, 'edge_val': edge_val, 'edge_row': edge_row, 'edge_col': edge_col, 'num_layers': NUM_LAYERS}
    _L1_gnn_all = _L1_gnn_setup()
    _L1_gnn_in = {k: v for k, v in _L1_gnn_all.items() if k in ()}
    del _L1_gnn_all

    def _L2_gnn_setup():
        import jax, jax.numpy as jnp
        import numpy as np
        N, E = (50000, 25000)
        NODE_DIM, EDGE_DIM, HIDDEN_DIM = (128, 64, 128)
        LN_EPS = 1e-05
        key = jax.random.key(seed)
        ks = jax.random.split(key, 14)
        s = lambda fan_in: 1.0 / np.sqrt(fan_in)
        return {'node_features': jax.random.normal(ks[0], (N, NODE_DIM), jnp.float32), 'edge_index': jax.random.randint(ks[1], (2, E), 0, N, jnp.int32), 'edge_features': jax.random.normal(ks[2], (E, EDGE_DIM), jnp.float32), 'Wm1': jax.random.uniform(ks[3], (2 * NODE_DIM + EDGE_DIM, HIDDEN_DIM), jnp.float32, -s(320), s(320)), 'bm1': jax.random.uniform(ks[4], (HIDDEN_DIM,), jnp.float32, -s(320), s(320)), 'Wm2': jax.random.uniform(ks[5], (HIDDEN_DIM, HIDDEN_DIM), jnp.float32, -s(HIDDEN_DIM), s(HIDDEN_DIM)), 'bm2': jax.random.uniform(ks[6], (HIDDEN_DIM,), jnp.float32, -s(HIDDEN_DIM), s(HIDDEN_DIM)), 'Wu1': jax.random.uniform(ks[7], (NODE_DIM + HIDDEN_DIM, HIDDEN_DIM), jnp.float32, -s(256), s(256)), 'bu1': jax.random.uniform(ks[8], (HIDDEN_DIM,), jnp.float32, -s(256), s(256)), 'Wu2': jax.random.uniform(ks[9], (HIDDEN_DIM, NODE_DIM), jnp.float32, -s(HIDDEN_DIM), s(HIDDEN_DIM)), 'bu2': jax.random.uniform(ks[10], (NODE_DIM,), jnp.float32, -s(HIDDEN_DIM), s(HIDDEN_DIM)), 'gamma': jnp.ones((NODE_DIM,), jnp.float32), 'beta': jnp.zeros((NODE_DIM,), jnp.float32)}
    _L2_gnn_all = _L2_gnn_setup()
    _L2_gnn_in = {k: v for k, v in _L2_gnn_all.items() if k in ('Wm1', 'bm1', 'Wm2', 'bm2', 'Wu1', 'bu1', 'Wu2', 'bu2', 'gamma', 'beta')}
    del _L2_gnn_all

    def _L3_gnn_setup():
        import jax, jax.numpy as jnp
        import numpy as np
        import math
        N_NODES = 3125
        N_EDGES = 50000
        IN_C = 128
        HID = 128
        OUT_C = 128
        N_LAYERS = 3
        ALPHA = 0.1
        THETA = 0.5
        key = jax.random.key(seed)
        ks = jax.random.split(key, 8)
        node_features = jax.random.normal(ks[0], (N_NODES, IN_C), dtype=jnp.float32)
        edges = jax.random.randint(ks[1], (2, N_EDGES), 0, N_NODES, dtype=jnp.int64)
        s = 1.0 / math.sqrt(HID)
        fc1_w = jax.random.uniform(ks[2], (IN_C, HID), jnp.float32, -s, s)
        fc1_b = jax.random.uniform(ks[3], (HID,), jnp.float32, -s, s)
        fc2_w = jax.random.uniform(ks[4], (HID, OUT_C), jnp.float32, -s, s)
        fc2_b = jax.random.uniform(ks[5], (OUT_C,), jnp.float32, -s, s)
        conv_w = jax.random.normal(ks[6], (N_LAYERS, HID, HID), dtype=jnp.float32) * s
        return {'node_features': node_features, 'edges': edges, 'fc1_w': fc1_w, 'fc1_b': fc1_b, 'fc2_w': fc2_w, 'fc2_b': fc2_b, 'conv_w': conv_w}
    _L3_gnn_all = _L3_gnn_setup()
    _L3_gnn_in = {k: v for k, v in _L3_gnn_all.items() if k in ('fc1_w', 'fc1_b', 'fc2_w', 'fc2_b', 'conv_w')}
    del _L3_gnn_all
    return {'x': x, 'src': src, 'dst': dst, 'edge_attr_16': edge_attr_16, 'edge_attr_64': edge_attr_64, 'edge_weight': edge_weight, 'L0_gnn_W1': _L0_gnn_in['W1'], 'L0_gnn_att_src1': _L0_gnn_in['att_src1'], 'L0_gnn_att_dst1': _L0_gnn_in['att_dst1'], 'L0_gnn_W_edge1': _L0_gnn_in['W_edge1'], 'L0_gnn_att_edge1': _L0_gnn_in['att_edge1'], 'L0_gnn_bias1': _L0_gnn_in['bias1'], 'L0_gnn_W2': _L0_gnn_in['W2'], 'L0_gnn_att_src2': _L0_gnn_in['att_src2'], 'L0_gnn_att_dst2': _L0_gnn_in['att_dst2'], 'L0_gnn_W_edge2': _L0_gnn_in['W_edge2'], 'L0_gnn_att_edge2': _L0_gnn_in['att_edge2'], 'L0_gnn_bias2': _L0_gnn_in['bias2'], 'L2_gnn_Wm1': _L2_gnn_in['Wm1'], 'L2_gnn_bm1': _L2_gnn_in['bm1'], 'L2_gnn_Wm2': _L2_gnn_in['Wm2'], 'L2_gnn_bm2': _L2_gnn_in['bm2'], 'L2_gnn_Wu1': _L2_gnn_in['Wu1'], 'L2_gnn_bu1': _L2_gnn_in['bu1'], 'L2_gnn_Wu2': _L2_gnn_in['Wu2'], 'L2_gnn_bu2': _L2_gnn_in['bu2'], 'L2_gnn_gamma': _L2_gnn_in['gamma'], 'L2_gnn_beta': _L2_gnn_in['beta'], 'L3_gnn_fc1_w': _L3_gnn_in['fc1_w'], 'L3_gnn_fc1_b': _L3_gnn_in['fc1_b'], 'L3_gnn_fc2_w': _L3_gnn_in['fc2_w'], 'L3_gnn_fc2_b': _L3_gnn_in['fc2_b'], 'L3_gnn_conv_w': _L3_gnn_in['conv_w']}

def reference(x, src, dst, edge_attr_16, edge_attr_64, edge_weight, L0_gnn_W1, L0_gnn_att_src1, L0_gnn_att_dst1, L0_gnn_W_edge1, L0_gnn_att_edge1, L0_gnn_bias1, L0_gnn_W2, L0_gnn_att_src2, L0_gnn_att_dst2, L0_gnn_W_edge2, L0_gnn_att_edge2, L0_gnn_bias2, L2_gnn_Wm1, L2_gnn_bm1, L2_gnn_Wm2, L2_gnn_bm2, L2_gnn_Wu1, L2_gnn_bu1, L2_gnn_Wu2, L2_gnn_bu2, L2_gnn_gamma, L2_gnn_beta, L3_gnn_fc1_w, L3_gnn_fc1_b, L3_gnn_fc2_w, L3_gnn_fc2_b, L3_gnn_conv_w):
    import jax
    import jax.numpy as jnp

    def _L0_gnn_ref(x, edge_index, edge_attr, W1, att_src1, att_dst1, W_edge1, att_edge1, bias1, W2, att_src2, att_dst2, W_edge2, att_edge2, bias2):
        import jax, jax.numpy as jnp
        import numpy as np
        N_NODES = 3125
        N_EDGES = 50000
        HEADS = 4
        IN_CH = 128
        HID_CH = 128
        OUT_CH = 128
        EDGE_DIM = 16
        NEG_SLOPE = 0.2

        def gat_conv(x, src, dst, edge_attr, W, att_src, att_dst, W_edge, att_edge, bias):
            N = x.shape[0]
            H, C = att_src.shape
            E = edge_attr.shape[0]
            cnt = jax.ops.segment_sum(jnp.ones((E,), edge_attr.dtype), dst, num_segments=N)
            loop_attr = jax.ops.segment_sum(edge_attr, dst, num_segments=N) / jnp.clip(cnt, 1.0)[:, None]
            loop = jnp.arange(N)
            src_f = jnp.concatenate([src, loop])
            dst_f = jnp.concatenate([dst, loop])
            ea = jnp.concatenate([edge_attr, loop_attr], axis=0)
            xh = (x @ W).reshape(N, H, C)
            a_src = jnp.sum(xh * att_src, axis=-1)
            a_dst = jnp.sum(xh * att_dst, axis=-1)
            eh = (ea @ W_edge).reshape(-1, H, C)
            a_edge = jnp.sum(eh * att_edge, axis=-1)
            alpha = jax.nn.leaky_relu(a_src[src_f] + a_dst[dst_f] + a_edge, NEG_SLOPE)
            m = jax.ops.segment_max(alpha, dst_f, num_segments=N)
            m = jnp.where(jnp.isfinite(m), m, 0.0)
            p = jnp.exp(alpha - jax.lax.stop_gradient(m)[dst_f])
            s = jax.ops.segment_sum(p, dst_f, num_segments=N)
            alpha = p / (s[dst_f] + 1e-16)
            out = jax.ops.segment_sum(xh[src_f] * alpha[..., None], dst_f, num_segments=N)
            return out.reshape(N, H * C) + bias
        src, dst = (edge_index[0], edge_index[1])
        h = gat_conv(x, src, dst, edge_attr, W1, att_src1, att_dst1, W_edge1, att_edge1, bias1)
        h = jax.nn.relu(h)
        out = gat_conv(h, src, dst, edge_attr, W2, att_src2, att_dst2, W_edge2, att_edge2, bias2)
        return out

    def _L1_gnn_ref(ebds, edge_val, edge_row, edge_col, num_layers):
        import jax, jax.numpy as jnp
        import numpy as np
        N_NODES = 3125
        D = 128
        N_EDGES = 50000
        NUM_LAYERS = 3
        'LightGCN forward: repeated SpMM with running layer-sum.\n\n            adj is COO: out[r] += val[e] * x[c] for each edge e=(r,c).\n            Equivalent to torch.spmm(adj, x) applied num_layers times,\n            summing all layer outputs (including layer 0 input).\n            '
        n = ebds.shape[0]

        def spmm(x):
            msgs = edge_val[:, None] * x[edge_col]
            return jax.ops.segment_sum(msgs, edge_row, num_segments=n)
        acc = ebds
        cur = ebds
        for _ in range(num_layers):
            cur = spmm(cur)
            acc = acc + cur
        return acc

    def _L2_gnn_ref(node_features, edge_index, edge_features, Wm1, bm1, Wm2, bm2, Wu1, bu1, Wu2, bu2, gamma, beta):
        import jax, jax.numpy as jnp
        import numpy as np
        N, E = (50000, 25000)
        NODE_DIM, EDGE_DIM, HIDDEN_DIM = (128, 64, 128)
        LN_EPS = 1e-05
        n = node_features.shape[0]
        src, dst = (edge_index[0], edge_index[1])
        msg_in = jnp.concatenate([node_features[src], node_features[dst], edge_features], axis=-1)
        messages = jax.nn.relu(msg_in @ Wm1 + bm1) @ Wm2 + bm2
        aggregated = jax.ops.segment_sum(messages, dst, num_segments=n)
        upd_in = jnp.concatenate([node_features, aggregated], axis=-1)
        updates = jax.nn.relu(upd_in @ Wu1 + bu1) @ Wu2 + bu2
        x = node_features + updates
        mu = jnp.mean(x, axis=-1, keepdims=True)
        var = jnp.mean((x - mu) ** 2, axis=-1, keepdims=True)
        return (x - mu) * jax.lax.rsqrt(var + LN_EPS) * gamma + beta

    def _L3_gnn_ref(node_features, edges, fc1_w, fc1_b, fc2_w, fc2_b, conv_w):
        import jax, jax.numpy as jnp
        import numpy as np
        import math
        N_NODES = 3125
        N_EDGES = 50000
        IN_C = 128
        HID = 128
        OUT_C = 128
        N_LAYERS = 3
        ALPHA = 0.1
        THETA = 0.5
        N = node_features.shape[0]
        loop = jnp.arange(N, dtype=edges.dtype)
        src = jnp.concatenate([edges[0], loop])
        dst = jnp.concatenate([edges[1], loop])
        deg = jax.ops.segment_sum(jnp.ones_like(dst, dtype=jnp.float32), dst, num_segments=N)
        dinv = jnp.where(deg > 0, jax.lax.rsqrt(jnp.maximum(deg, 1e-12)), 0.0)
        norm = dinv[dst] * dinv[src]
        x0 = jax.nn.relu(node_features @ fc1_w + fc1_b)
        x = x0
        for i in range(N_LAYERS):
            beta = math.log(THETA / (i + 1) + 1.0)
            h = jax.ops.segment_sum(x[src] * norm[:, None], dst, num_segments=N)
            h = (1.0 - ALPHA) * h + ALPHA * x0
            x = jax.nn.relu((1.0 - beta) * h + beta * (h @ conv_w[i]))
        return x @ fc2_w + fc2_b
    edge_index = jnp.stack([src, dst])
    h = jnp.maximum(_layernorm(x, axis=-1), 0.0)
    x = x + _L0_gnn_ref(h, edge_index, edge_attr_16, L0_gnn_W1, L0_gnn_att_src1, L0_gnn_att_dst1, L0_gnn_W_edge1, L0_gnn_att_edge1, L0_gnn_bias1, L0_gnn_W2, L0_gnn_att_src2, L0_gnn_att_dst2, L0_gnn_W_edge2, L0_gnn_att_edge2, L0_gnn_bias2)
    h = jnp.maximum(_layernorm(x, axis=-1), 0.0)
    x = x + _L1_gnn_ref(h, edge_weight, src, dst, 3)
    h = jnp.maximum(_layernorm(x, axis=-1), 0.0)
    x = x + _L2_gnn_ref(h, edge_index, edge_attr_64, L2_gnn_Wm1, L2_gnn_bm1, L2_gnn_Wm2, L2_gnn_bm2, L2_gnn_Wu1, L2_gnn_bu1, L2_gnn_Wu2, L2_gnn_bu2, L2_gnn_gamma, L2_gnn_beta)
    h = jnp.maximum(_layernorm(x, axis=-1), 0.0)
    x = x + _L3_gnn_ref(h, edge_index, L3_gnn_fc1_w, L3_gnn_fc1_b, L3_gnn_fc2_w, L3_gnn_fc2_b, L3_gnn_conv_w)
    return x

_drawn_inputs = setup_inputs


def setup_inputs(seed=0):
    import zlib

    import numpy as np

    out = dict(_drawn_inputs(seed))
    spreads = {'L0_gnn_bias1': (0.0, 0.1),
     'L0_gnn_bias2': (0.0, 0.1),
     'L2_gnn_gamma': (1.0, 0.2),
     'L2_gnn_beta': (0.0, 0.1)}
    factors = {'edge_attr_16': 4.785,
     'edge_attr_64': 8.0,
     'L0_gnn_att_src1': 4.333,
     'L0_gnn_att_dst1': 64.0,
     'L0_gnn_W_edge1': 8.0,
     'L0_gnn_att_edge1': 6.742,
     'L0_gnn_att_src2': 8.0,
     'L0_gnn_att_dst2': 64.0,
     'L0_gnn_W_edge2': 5.796,
     'L0_gnn_att_edge2': 7.0,
     'L2_gnn_Wm1': 4.907,
     'L2_gnn_bm1': 64.0,
     'L2_gnn_Wm2': 3.7,
     'L2_gnn_bm2': 64.0,
     'L2_gnn_bu1': 5.629,
     'L3_gnn_fc1_b': 8.0,
     'L3_gnn_fc2_b': 2.685,
     'L3_gnn_conv_w': 3.605}
    for name, (base, spread) in spreads.items():
        noise = np.random.default_rng([zlib.crc32(name.encode()), seed]).standard_normal(out[name].shape)
        drawn = base * np.exp(spread * noise) if base else spread * noise
        out[name] = jnp.asarray(drawn.astype(out[name].dtype))
    for name, factor in factors.items():
        out[name] = (out[name] * factor).astype(out[name].dtype)
    return out
```

```python
from contextlib import ExitStack

import concourse.bass as bass
from concourse import mybir

F32 = mybir.dt.float32
I32 = mybir.dt.int32
BF16 = mybir.dt.bfloat16
U32 = mybir.dt.uint32
ALU = mybir.AluOpType
ACT = mybir.ActivationFunctionType
AX_X = mybir.AxisListType.X

N, E, D, H = 50000, 25000, 128, 4
P = 128
CH = D // H
T = -(-E // P)
EP = T * P
E_LAST = E - (P - 1) * T
KE16, KE64 = 16, 64
WA = D + 2 * H
U = 14
NB = T // U
G, S = 4, 4
ROWS = G * S * P
NODE_ITERS = 25
NODE_STEP = (N - ROWS) // (NODE_ITERS - 1)
EDGE_ITERS = 13
EDGE_STEP = (T - G * S) // (EDGE_ITERS - 1)
assert NODE_STEP * (NODE_ITERS - 1) + ROWS == N and NODE_STEP <= ROWS
assert EDGE_STEP * (EDGE_ITERS - 1) + G * S == T and EDGE_STEP <= G * S
assert NB * U == T and NB % 2 == 0
R = 256
SKIP = 1 << 20
BIG = 1e30
LN_EPS = 1e-5
NEG_SLOPE = 0.2
ALPHA, THETA, GCN_LAYERS = 0.1, 0.5, 3
X0_SCALE = (1.0 - ALPHA) / ALPHA


def log_beta(i):
    import math
    return math.log(THETA / (i + 1) + 1.0)


class Net:
    pass


def row(vec):
    return vec.rearrange("(a n) -> a n", a=1).to_broadcast([P, D])


def slots(t):
    return t[:, :].unsqueeze(1).to_broadcast([P, S, D])



def phase_setup(nc, net, inp):
    sb = lambda name, shape, dt=F32: nc.alloc_sbuf_tensor(name, shape, dt)
    sem = nc.alloc_semaphore
    w = net.w
    with nc.cleanup_on_exit():
        ps = [nc.alloc_psum_tensor(f"setup_ps{i}", [P, 512], F32) for i in range(8)]
        ones = net.ones
        att = sb("att_cols", [P, 6])
        att_blocks = sb("att_blocks", [P, 4, H])
        we = sb("w_edge", [KE16, 2, D])
        we_prod = sb("w_edge_prod", [P, 2, H, KE16])
        w_t = sb("w_transposed", [P, 3, P])
        wm2 = sb("wm2", [P, P])
        wu1b = sb("wu1b", [P, P])
        wae = sb("w_att_edge", [P, 2 * H, KE16])
        bm2 = sb("bm2_col", [P, 1])
        bm2_wide = sb("bm2_wide", [P, P])
        conv = sb("conv", [P, GCN_LAYERS, P])
        ea = sb("edge_attr", [P, T, KE16])
        prod = sb("edge_prod", [P, T, KE16])
        dst_i = sb("dst_int", [P, T], I32)
        nxt_i = sb("next_dst_int", [P, 1], I32)
        nxt = sb("next_dst", [P, 1])
        diag = sb("dst_diag", [P, 2, P])
        lower = sb("lower", [P, P])
        tmp = sb("setup_tmp", [P, T])
        iota_i = sb("iota_i", [P, R], I32)

        loaded = sem("weights_loaded")
        edges_loaded = sem("edges_loaded")
        cleared = sem("pads_cleared")
        zeros = sb("zeros", [P, D])
        split, part_b = sb("bias_split", [P, 3, D]), sb("bias_part", [P, D], BF16)
        zeroed, padded = sem("zeroed"), sem("padded")
        pool_made = sem("identity_made")
        p_step = sem("pool_step")
        v_step = sem("vector_step")
        t_done = sem("tensor_step")
        with nc.Block("setup") as block:
            @block.sync
            def _(sp):
                n = 0

                def load(dst, src):
                    sp.dma_start(dst, src).then_inc(loaded, 16)
                    return 1
                col = lambda v: v.rearrange("(p a) -> p a", a=1)
                flat = lambda v: v.rearrange("h (c a) -> (h c) a", a=1)
                n += load(w["W1"][:, 0:D], inp["L0_gnn_W1"])
                n += load(w["W2"][:, 0:D], inp["L0_gnn_W2"])
                n += load(w["Wm1a"][:, :], inp["L2_gnn_Wm1"][0:D, :])
                n += load(w["Wm1b"][:, :], inp["L2_gnn_Wm1"][D:2 * D, :])
                n += load(w["Wm1c"][:, :], inp["L2_gnn_Wm1"][2 * D:2 * D + KE64, :])
                n += load(wm2[:, :], inp["L2_gnn_Wm2"])
                n += load(w["Wu1a"][:, :], inp["L2_gnn_Wu1"][0:D, :])
                n += load(wu1b[:, :], inp["L2_gnn_Wu1"][D:2 * D, :])
                n += load(w["Wu2"][:, :], inp["L2_gnn_Wu2"])
                n += load(w["fc1"][:, :], inp["L3_gnn_fc1_w"])
                n += load(w["fc2"][:, :], inp["L3_gnn_fc2_w"])
                for i in range(GCN_LAYERS):
                    n += load(conv[:, i, :], inp["L3_gnn_conv_w"][i])
                for i, name in enumerate(("src1", "dst1", "src2", "dst2", "edge1", "edge2")):
                    n += load(att[:, i:i + 1], flat(inp[f"L0_gnn_att_{name}"]))
                for i in range(2):
                    n += load(we[:, i, :], inp[f"L0_gnn_W_edge{i + 1}"])
                n += load(bm2[:, :], col(inp["L2_gnn_bm2"]))
                n += load(w["b1"][:, :], col(inp["L0_gnn_bias1"]))
                n += load(w["bu1"][:, :], col(inp["L2_gnn_bu1"]))
                n += load(w["fc1_b"][:, :], col(inp["L3_gnn_fc1_b"]))
                for name, key in ROW_BIASES:
                    n += load(w[name][:, :], row(inp[key]))
                assert n == N_LOADS
                sp.wait_ge(zeroed, 1)
                sp.dma_start(net.EA64[E:EP, :], zeros[0:EP - E, 0:KE64]).then_inc(padded, 16)
                sp.dma_start(net.C1[EP:EP + 1, :], zeros[0:1, :]).then_inc(padded, 16)
                sp.dma_start(net.C2[EP:EP + 1, :], zeros[0:1, :]).then_inc(padded, 16)
                sp.wait_ge(cleared, 5)

                def edge_load(dst, src, k):
                    head = src[0:(P - 1) * T, :].rearrange("(p t) k -> p t k", t=T)
                    for a, b in ((0, 112), (112, P - 1)):
                        sp.dma_start(dst[a:b, :, :], head[a:b]).then_inc(edges_loaded, 16)
                    sp.dma_start(dst[P - 1:P, 0:E_LAST, :],
                                 src[(P - 1) * T:E, :].rearrange("(p t) k -> p t k", p=1)).then_inc(edges_loaded, 16)
                one = lambda v: v.rearrange("(e k) -> e k", k=1)
                edge_load(dst_i[:, :].unsqueeze(2), one(inp["dst"]), 1)
                edge_load(net.src[:, :].unsqueeze(2), one(inp["src"]), 1)
                edge_load(net.ew[:, :].unsqueeze(2), one(inp["edge_weight"]), 1)
                edge_load(ea[:, :, :], inp["edge_attr_16"], KE16)
                sp.dma_start(net.EA64[0:E, :], inp["edge_attr_64"]).then_inc(padded, 16)
                sp.dma_start(nxt_i[0:P - 1, :], next_heads(inp["dst"]), allow_slow_non_contiguous=True).then_inc(edges_loaded, 16)
                sp.wait_ge(padded, 64)

            @block.gpsimd
            def _(pool):
                nc.gpsimd.memset(net.ident[:, :], 0.0).then_inc(p_step, 1)
                nc.gpsimd.memset(net.upper[:, :], 1.0).then_inc(p_step, 1)
                nc.gpsimd.memset(lower[:, :], 1.0).then_inc(p_step, 1)
                nc.gpsimd.memset(net.shift[:, :], 0.0).then_inc(p_step, 1)
                nc.gpsimd.iota(iota_i[:, :], [[1, R]], base=0, channel_multiplier=0).then_inc(p_step, 1)
                nc.gpsimd.iota(net.own_row[:, :], [[1, T]], base=N, channel_multiplier=T).then_inc(p_step, 1)
                nc.gpsimd.iota(net.node_id[:, :], [[1, N // 125]], base=0, channel_multiplier=N // 125).then_inc(p_step, 1)
                pool.wait_ge(p_step, 7)
                nc.gpsimd.affine_select(out=net.ident[:, :], in_=net.ident[:, :], compare_op=ALU.not_equal, fill=1.0,
                                        base=0, pattern=[[-1, P]], channel_multiplier=1).then_inc(pool_made, 1)
                nc.gpsimd.affine_select(out=net.upper[:, :], in_=net.upper[:, :], compare_op=ALU.is_gt, fill=0.0,
                                        base=0, pattern=[[1, P]], channel_multiplier=-1).then_inc(pool_made, 1)
                nc.gpsimd.affine_select(out=lower[:, :], in_=lower[:, :], compare_op=ALU.is_gt, fill=0.0,
                                        base=0, pattern=[[-1, P]], channel_multiplier=1).then_inc(pool_made, 1)
                nc.gpsimd.affine_select(out=net.shift[:, :], in_=net.shift[:, :], compare_op=ALU.not_equal, fill=1.0,
                                        base=-1, pattern=[[-1, P]], channel_multiplier=1).then_inc(pool_made, 1)
                pool.dma_start(net.OWN[0:N, :].rearrange("(p j) k -> p (j k)", p=125), net.node_id[:, :]).then_inc(net.own_base, 16)
                pool.wait_ge(net.own_base, 16)

            @block.vector
            def _(v):
                steps = [0]

                def link(ins):
                    steps[0] += 1
                    ins.then_inc(v_step, 1)
                    v.wait_ge(v_step, steps[0])

                nc.vector.memset(dst_i[:, :], N).then_inc(cleared, 1)
                nc.vector.memset(net.src[:, :], 0).then_inc(cleared, 1)
                nc.vector.memset(net.ew[:, :], 0.0).then_inc(cleared, 1)
                nc.vector.memset(ea[:, :, :], 0.0).then_inc(cleared, 1)
                nc.vector.memset(nxt_i[:, :], -1).then_inc(cleared, 1)
                nc.vector.memset(net.eps[:, :], LN_EPS)
                nc.vector.memset(zeros[:, :], 0.0).then_inc(zeroed, 1)
                nc.vector.memset(att_blocks[:, :, :], 0.0)
                nc.vector.memset(we_prod[:, :, :, :], 0.0)
                link(nc.vector.memset(ones[:, :], 1.0))
                v.wait_ge(loaded, 16 * N_LOADS)
                for a in range(4):
                    for h in range(H):
                        r = slice(h * CH, (h + 1) * CH)
                        nc.vector.tensor_copy(att_blocks[r, a, h:h + 1], att[r, a:a + 1])
                link(nc.vector.tensor_copy(bm2_wide[:, :], bm2[:, :].to_broadcast([P, P])))
                v.wait_ge(pool_made, 4)
                nc.vector.tensor_copy(net.iota_r[:, :], iota_i[:, :])
                nc.vector.tensor_copy(net.ones_b[:, :], ones[:, :])
                nc.vector.tensor_copy(net.above[:, :], net.upper[:, :])
                v.wait_ge(t_done, 1)
                link(nc.vector.tensor_copy(w_t[:, :, :], ps[0][:, 0:3 * P].rearrange("p (a b) -> p a b", a=3)))
                for i in range(2):
                    for h in range(H):
                        r = slice(h * CH, (h + 1) * CH)
                        last = nc.vector.tensor_scalar(we_prod[r, i, h, :], ps[1][r, i * KE16:(i + 1) * KE16],
                                                       att[r, 4 + i:5 + i], None, ALU.mult)
                link(last)
                v.wait_ge(t_done, 2)
                nc.vector.tensor_copy(w["W1"][:, D:WA], ps[2][:, 0:2 * H])
                nc.vector.tensor_copy(w["W2"][:, D:WA], ps[2][:, 2 * H:4 * H])
                nc.vector.tensor_copy(w["Wm2u"][:, :], ps[3][:, 0:P])
                nc.vector.tensor_copy(w["bm2u"][:, :], ps[4][:, 0:P])
                link(nc.vector.tensor_copy(wae[:, :, :], ps[5][:, 0:2 * H * KE16].rearrange("p (a b) -> p a b", b=KE16)))
                for i in range(GCN_LAYERS):
                    link(nc.vector.tensor_scalar(w[f"conv{i}"][:, :], net.ident[:, :], 1.0 - log_beta(i), None, ALU.mult))
                    link(nc.vector.scalar_tensor_tensor(out=w[f"conv{i}"][:, :], in0=conv[:, i, :], scalar=log_beta(i),
                                                        in1=w[f"conv{i}"][:, :], op0=ALU.mult, op1=ALU.add))
                    if i == 0:
                        link(nc.vector.tensor_scalar(w["conv_lone"][:, :], w["conv0"][:, :], X0_SCALE, None, ALU.mult))
                    link(nc.vector.tensor_scalar(w[f"conv{i}"][:, :], w[f"conv{i}"][:, :], 1.0 - ALPHA, None, ALU.mult))
                link(nc.vector.tensor_scalar(w["fc1_b"][:, :], w["fc1_b"][:, :], 1.0 / X0_SCALE, None, ALU.mult))
                for name in net.parts:
                    high, rest = split[:, 0, :], split[:, 1, :]
                    link(nc.vector.tensor_copy(rest, w[name][:, :]))
                    for k in range(3):
                        link(nc.vector.tensor_copy(part_b[:, :], rest))
                        link(nc.vector.tensor_copy(high, part_b[:, :]))
                        link(nc.vector.tensor_tensor(rest, rest, high, ALU.subtract))
                        if k == 0:
                            link(nc.vector.tensor_scalar(split[:, 2, :], high, net.ident[:, 0:1], None, ALU.mult))
                        else:
                            link(nc.vector.scalar_tensor_tensor(out=split[:, 2, :], in0=high, scalar=net.ident[:, k:k + 1], in1=split[:, 2, :],
                                                                op0=ALU.mult, op1=ALU.add))
                    link(nc.vector.tensor_copy(net.parts[name][:, :, :], split[:, 2:3, :].to_broadcast([P, S, D])))
                v.wait_ge(edges_loaded, 16 * N_EDGE_LOADS)
                dst = net.dst
                nc.vector.tensor_copy(nxt[:, :], nxt_i[:, :])
                link(nc.vector.tensor_copy(dst[:, :], dst_i[:, :]))
                nc.vector.memset(net.cont[:, 0:1], 0.0)
                nc.vector.tensor_tensor(net.cont[:, 1:T], dst[:, 1:T], dst[:, 0:T - 1], ALU.is_equal)
                nc.vector.tensor_tensor(net.ends[:, 0:T - 1], dst[:, 1:T], dst[:, 0:T - 1], ALU.not_equal)
                nc.vector.tensor_tensor(net.ends[:, T - 1:T], dst[:, T - 1:T], nxt[:, :], ALU.not_equal)
                nc.vector.tensor_scalar(net.first[:, :], dst[:, :], dst[:, 0:1], None, ALU.is_equal)
                link(nc.vector.tensor_scalar(net.last[:, :], dst[:, :], dst[:, T - 1:T], None, ALU.is_equal))
                link(nc.vector.tensor_scalar(net.not_end[:, :], net.ends[:, :], -1.0, 1.0, ALU.mult, ALU.add))
                v.wait_ge(pool_made, 4)
                end_of_first(nc, link, net, net, tmp)
                nc.vector.tensor_scalar(diag[:, 0, :], net.ident[:, :], dst[:, 0:1], None, ALU.mult)
                link(nc.vector.tensor_scalar(diag[:, 1, :], net.ident[:, :], dst[:, T - 1:T], None, ALU.mult))
                net.diag_step = steps[0]
                link(nc.vector.tensor_scalar(tmp[:, :], dst[:, :], -float(SKIP), None, ALU.add))
                link(nc.vector.tensor_tensor(tmp[:, :], tmp[:, :], net.ends[:, :], ALU.mult))
                link(nc.vector.tensor_scalar(net.own_idx[:, :], tmp[:, :], float(SKIP), None, ALU.add))
                link(nc.vector.tensor_scalar(net.dst_idx[:, :], dst[:, :], float(N - 1), None, ALU.min))
                v.wait_ge(t_done, 3)
                nc.vector.tensor_scalar(net.later[:, :], ps[6][:, 0:P], dst[:, T - 1:T], None, ALU.is_equal)
                link(nc.vector.tensor_scalar(net.earlier[:, :], ps[7][:, 0:P], dst[:, 0:1], None, ALU.is_equal))
                nc.vector.tensor_tensor(net.later[:, :], net.later[:, :], net.upper[:, :], ALU.mult)
                link(nc.vector.tensor_tensor(net.earlier[:, :], net.earlier[:, :], lower[:, :], ALU.mult))
                link(nc.vector.tensor_scalar(net.earlier_mask[:, :], net.earlier[:, :], -1.0, BIG, ALU.add, ALU.mult))
                for j in range(2 * H):
                    link(nc.vector.tensor_tensor(prod[:, :, :], ea[:, :, :],
                                                 wae[:, j:j + 1, :].to_broadcast([P, T, KE16]), ALU.mult))
                    link(nc.vector.tensor_reduce(net.a_edge[:, j, :], prod[:, :, :], AX_X, ALU.add))
                nc.vector.memset(tmp[:, :], 1.0)
                link(nc.vector.memset(net.seg[:, :, :], 0.0))
                for j in range(2 * H):
                    nc.vector.tensor_tensor_scan(net.seg[:, j, :], net.cont[:, :], net.a_edge[:, j, :], 0.0, ALU.mult, ALU.add)
                link(nc.vector.tensor_tensor_scan(net.seg[:, 2 * H, :], net.cont[:, :], tmp[:, :], 0.0, ALU.mult, ALU.add))
                net.seg_step = steps[0]
                v.wait_ge(t_done, 4)
                link(nc.vector.tensor_copy(net.carry[:, 0:2 * H + 1], ps[0][:, 0:2 * H + 1]))
                for j in range(2 * H + 1):
                    last = nc.vector.scalar_tensor_tensor(out=net.seg[:, j, :], in0=net.first[:, :], scalar=net.carry[:, j:j + 1],
                                                          in1=net.seg[:, j, :], op0=ALU.mult, op1=ALU.add)
                link(last)
                cnt = net.seg[:, 2 * H, :]
                link(nc.vector.tensor_scalar(tmp[:, :], cnt, 1.0, None, ALU.max))
                link(nc.vector.reciprocal(tmp[:, :], tmp[:, :]))
                for j in range(2 * H):
                    last = nc.vector.tensor_tensor(net.seg[:, j, :], net.seg[:, j, :], tmp[:, :], ALU.mult)
                link(last)
                net.cnt_step = steps[0]
                v.wait_ge(t_done, 5)
                link(nc.vector.reciprocal(net.dinv[:, :], net.dinv[:, :]))

            @block.tensor
            def _(pe):
                pe.wait_ge(loaded, 16 * N_LOADS)
                pe.wait_ge(pool_made, 4)
                pe.wait_ge(v_step, 2)
                for i, m in enumerate((w["W1"][:, 0:D], w["W2"][:, 0:D], wm2[:, :])):
                    nc.tensor.transpose(ps[0][:, i * P:(i + 1) * P], m, net.ident[:, :])
                for i in range(2):
                    last = nc.tensor.transpose(ps[1][:, i * KE16:(i + 1) * KE16], we[:, i, :], net.ident[0:KE16, 0:KE16])
                last.then_inc(t_done, 1)
                pe.wait_ge(v_step, 4)
                for i in range(4):
                    nc.tensor.matmul(ps[2][:, i * H:(i + 1) * H], w_t[:, i // 2, :], att_blocks[:, i, :], start=True, stop=True)
                nc.tensor.matmul(ps[3][:, 0:P], w_t[:, 2, :], wu1b[:, :], start=True, stop=True)
                nc.tensor.matmul(ps[4][:, 0:P], bm2_wide[:, :], wu1b[:, :], start=True, stop=True)
                nc.tensor.matmul(ps[5][:, 0:2 * H * KE16], ones[:, :], we_prod[:, :, :, :].rearrange("p a h k -> p (a h k)"),
                                 start=True, stop=True).then_inc(t_done, 1)
                pe.wait_ge(v_step, net.diag_step)
                nc.tensor.matmul(ps[6][:, 0:P], ones[:, :], diag[:, 0, :], start=True, stop=True)
                nc.tensor.matmul(ps[7][:, 0:P], ones[:, :], diag[:, 1, :], start=True, stop=True).then_inc(t_done, 1)
                pe.wait_ge(v_step, net.seg_step)
                nc.tensor.matmul(ps[0][:, 0:2 * H + 1], net.later[:, :], net.seg[:, 0:2 * H + 1, T - 1], start=True,
                                 stop=True).then_inc(t_done, 1)

            @block.scalar
            def _(act):
                act.wait_ge(v_step, net.cnt_step)
                nc.scalar.activation(net.dinv[:, :], net.seg[:, 2 * H, :], ACT.Sqrt, bias=ones[:, 0:1]).then_inc(t_done, 1)


N_EDGE_LOADS = 4 * 3 + 1
ROW_BIASES = [("b2", "L0_gnn_bias2"), ("bu2", "L2_gnn_bu2"), ("gamma", "L2_gnn_gamma"), ("beta", "L2_gnn_beta"),
              ("fc2_b", "L3_gnn_fc2_b"), ("bm1", "L2_gnn_bm1")]
N_LOADS = 11 + GCN_LAYERS + 6 + 2 + 4 + len(ROW_BIASES)


def next_heads(dst):
    return bass.AP(tensor=dst.tensor, offset=dst.offset + T, ap=[[T, P - 1], [1, 1]])


def end_of_first(nc, link, net, order, tmp):
    link(nc.vector.tensor_reduce(tmp[:, 0:1], order.first[:, :], AX_X, ALU.add))
    link(nc.vector.tensor_tensor(tmp[:, 0:1], tmp[:, 0:1], net.own_row[:, 0:1], ALU.add))
    link(nc.vector.tensor_scalar(order.first_end[:, :], tmp[:, 0:1], -float(N + 1), None, ALU.add))


def allocate(nc, net):
    sb = lambda name, shape, dt=F32: nc.alloc_sbuf_tensor(name, shape, dt)
    dram = lambda name, shape, dt=F32: nc.dram_tensor(name, shape, dt, kind="Internal").ap()
    net.w = {name: sb(f"w_{name}", [P, P]) for name in
             ("Wm1a", "Wm1b", "Wu1a", "Wm2u", "bm2u", "Wu2", "fc1", "fc2", "conv0", "conv1", "conv2", "conv_lone")}
    net.w["W1"], net.w["W2"] = sb("w_W1", [P, WA]), sb("w_W2", [P, WA])
    net.w["Wm1c"] = sb("w_Wm1c", [KE64, P])
    for name in ("b1", "bu1", "fc1_b"):
        net.w[name] = sb(f"w_{name}", [P, 1])
    for name, _ in ROW_BIASES:
        net.w[name] = sb(f"w_{name}", [P, D])
    net.parts = {name: sb(f"parts_{name}", [P, S, D], BF16) for name in ("b2", "bu2", "fc2_b", "bm1")}
    net.ident = sb("ident", [P, P])
    net.eps = sb("eps", [P, 1])
    net.later, net.earlier, net.earlier_mask = (sb(n, [P, P]) for n in ("later", "earlier", "earlier_mask"))
    net.src, net.own_row = sb("src_cols", [P, T], I32), sb("own_row", [P, T], I32)
    net.node_id = sb("node_id", [125, N // 125], I32)
    net.own_idx, net.dst_idx, net.q, net.r = (sb(n, [P, T], I32) for n in
                                             ("own_idx", "dst_idx", "q", "r"))
    net.dst, net.cont, net.ends, net.not_end, net.first, net.last, net.ew, net.dinv = (
        sb(n, [P, T]) for n in ("dst", "cont", "ends", "not_end", "first", "last", "ew", "dinv"))
    net.a_edge = sb("a_edge", [P, 2 * H, T])
    net.seg = sb("seg", [P, 2 * H + 1, T])
    net.carry = sb("carry", [P, WA])
    net.own_base = nc.alloc_semaphore("own_base")
    net.XD = dram("XD", (EP, D))
    net.J1, net.J2, net.PACK = dram("J1", (EP, 2), I32), dram("J2", (EP, 2), I32), dram("PACK", (EP, 5))
    net.OWNS = dram("OWNS", (N + 1, 1), I32)
    net.iota_r = sb("iota_r", [P, R])
    net.ones, net.ones_b, net.above = sb("ones", [P, P]), sb("ones_b", [P, P], BF16), sb("above", [P, P], BF16)
    net.upper, net.shift = sb("upper", [P, P]), sb("shift", [P, P])
    net.s, net.home2, net.home3 = (sb(n, [P, T], I32) for n in ("s", "home2", "home3"))
    net.S = Net()
    net.S.cont, net.S.first, net.S.ew = (sb(n, [P, T]) for n in ("s_cont", "s_first", "s_ew"))
    net.S.r, net.S.q, net.S.s, net.S.own_idx = (sb(n, [P, T], I32) for n in ("s_r", "s_q", "s_s", "s_own_idx"))
    net.S.later = sb("s_later", [P, P])
    net.OWN = dram("OWN", (N + 1, 1), I32)
    NT = N + EP
    net.first_end, net.S.first_end = sb("first_end", [P, 1], I32), sb("s_first_end", [P, 1], I32)
    net.ad, net.pself = sb("node_scores", [P, 2 * H, T]), sb("p_self", [P, H, T])
    net.T1, net.T2 = dram("T1", (N, WA)), dram("T2", (N + EP, WA))
    net.AD1, net.RG = dram("AD1", (EP, WA)), dram("RG", (EP, D + H))
    net.XHX, net.HD, net.XS = dram("XHX", (N + 2 * EP, D)), dram("HD", (EP, D)), dram("XS", (EP, D))
    net.C1, net.C2, net.C3 = dram("C1", (EP + 1, D)), dram("C2", (EP + 1, D)), dram("C3", (EP, D))
    net.PS, net.X2D, net.H2D, net.Z, net.RM = (dram(n, (EP, D)) for n in ("PS", "X2D", "H2D", "Z", "RM"))
    net.X3D, net.X0D = dram("X3D", (EP, D)), dram("X0D", (EP, D))
    net.GT = [dram(f"GT{i}", (2 * EP, D)) for i in range(3)]
    net.RC = [dram(f"RC{i}", (EP, D)) for i in range(3)]
    net.EA64 = dram("EA64", (EP, KE64))



def gather_columns(nc, pool, table, index, b, rounds=0):
    ring, stage, staged, arrived, freed, freed_by = (b[x] for x in ("ring", "stage", "staged", "arrived", "freed", "freed_by"))
    before = rounds * (NB // 2)

    def half_batch(batch, half, uses):
        if uses is not None:
            pool.wait_ge(arrived[half], uses * (16 * U))
            pool.wait_ge(freed[half], uses * freed_by)
        nc.gpsimd.tensor_copy(stage[:, half, :], index[:, bass.ds(batch * U, U)]).then_inc(staged, 1)
        pool.wait_ge(staged, 1)
        pool.sem_clear(staged)
        for u in range(U):
            nc.gpsimd.indirect_dma_start(
                out=ring[:, half, u, :], out_offset=None, in_=table,
                in_offset=bass.IndirectOffsetOnAxis(ap=stage[:, half, u:u + 1], axis=0)).then_inc(arrived[half], 16)

    half_batch(0, 0, before or None)
    half_batch(1, 1, before or None)
    with pool.Fori(1, NB // 2) as k:
        half_batch(k * 2, 0, k + before)
        half_batch(k * 2 + 1, 1, k + before)


def gather_buffers(nc, name, width, dt=F32, freed_by=1):
    return dict(ring=nc.alloc_sbuf_tensor(f"{name}_ring", [P, 2, U, width], dt),
                stage=nc.alloc_sbuf_tensor(f"{name}_stage", [P, 2, U], U32),
                staged=nc.alloc_semaphore(f"{name}_staged"),
                arrived=[nc.alloc_semaphore(f"{name}_arrived{i}") for i in range(2)],
                freed=[nc.alloc_semaphore(f"{name}_freed{i}") for i in range(2)], freed_by=freed_by)


def owner_scan(nc, link, net, values, out):
    J = values.shape[1]
    link(nc.vector.tensor_tensor(values, values, net.ends[:, :].unsqueeze(1).to_broadcast([P, J, T]), ALU.mult))
    for j in range(J):
        last = nc.vector.tensor_tensor_scan(out[:, j, ::-1], net.not_end[:, ::-1], values[:, j, ::-1], 0.0, ALU.mult, ALU.add)
    link(last)


def owner_carry(nc, link, net, carried, out):
    J = out.shape[1]
    link(nc.vector.tensor_copy(net.carry[:, 0:J], carried))
    for j in range(J):
        last = nc.vector.scalar_tensor_tensor(out=out[:, j, :], in0=net.last[:, :], scalar=net.carry[:, j:j + 1],
                                              in1=out[:, j, :], op0=ALU.mult, op1=ALU.add)
    link(last)


def fetch_columns(nc, pool, table, index, b, take, rounds=0):
    ring, stage, staged, arrived = (b[x] for x in ("ring", "stage", "staged", "arrived"))
    before = rounds * (NB // 2)

    def half_batch(batch, half, uses):
        if uses is not None:
            pool.wait_ge(arrived[half], uses * (16 * U))
            take(batch - 2, half)
        nc.gpsimd.tensor_copy(stage[:, half, :], index[:, bass.ds(batch * U, U)]).then_inc(staged, 1)
        pool.wait_ge(staged, 1)
        pool.sem_clear(staged)
        for u in range(U):
            nc.gpsimd.indirect_dma_start(
                out=ring[:, half, u, :], out_offset=None, in_=table,
                in_offset=bass.IndirectOffsetOnAxis(ap=stage[:, half, u:u + 1], axis=0)).then_inc(arrived[half], 16)

    half_batch(0, 0, None)
    half_batch(1, 1, None)
    with pool.Fori(1, NB // 2) as k:
        half_batch(k * 2, 0, k + before)
        half_batch(k * 2 + 1, 1, k + before)
    for half in range(2):
        pool.wait_ge(arrived[half], (before + NB // 2) * (16 * U))
        take(NB - 2 + half, half)


def phase_own_rows(nc, net):
    with nc.cleanup_on_exit():
        tmp, r = (nc.alloc_sbuf_tensor(n_, [P, 1, T], F32) for n_ in ("r_tmp", "r_found"))
        ps = nc.alloc_psum_tensor("rows_ps", [P, 512], F32)
        v_step, r_carried = nc.alloc_semaphore("rows_vector_step"), nc.alloc_semaphore("r_carried")
        with nc.Block("own_rows") as block:
            @block.vector
            def _(v):
                steps = [0]

                def link(ins):
                    steps[0] += 1
                    ins.then_inc(v_step, 1)
                    v.wait_ge(v_step, steps[0])
                link(nc.vector.tensor_scalar(tmp[:, 0, :], net.own_row[:, :], -float(N), None, ALU.add))
                owner_scan(nc, link, net, tmp[:, 0:1, :], r)
                net.r_step = steps[0]
                v.wait_ge(r_carried, 1)
                owner_carry(nc, link, net, ps[:, 0:1], r)
                link(nc.vector.tensor_copy(net.r[:, :], r[:, 0, :]))

            @block.tensor
            def _(pe):
                pe.wait_ge(v_step, net.r_step)
                nc.tensor.matmul(ps[:, 0:1], net.earlier[:, :], r[:, 0:1, 0], start=True, stop=True).then_inc(r_carried, 1)


def claim_rows(nc, pool, net, claimed, copied, places, values):
    def claim(batch, half, k):
        if k is not None:
            pool.wait_ge(claimed[half], k * (16 * U))
        nc.gpsimd.tensor_copy(places[:, half, :], net.own_idx[:, bass.ds(batch * U, U)])
        nc.gpsimd.tensor_copy(values[:, half, :], net.own_row[:, bass.ds(batch * U, U)]).then_inc(copied, 1)
        pool.wait_ge(copied, 1)
        pool.sem_clear(copied)
        for u in range(U):
            nc.gpsimd.indirect_dma_start(
                out=net.OWN, out_offset=bass.IndirectOffsetOnAxis(ap=places[:, half, u:u + 1], axis=0),
                in_=values[:, half, u:u + 1], in_offset=None, bounds_check=N, oob_is_err=False
            ).then_inc(claimed[half], 16)
    claim(0, 0, None)
    claim(1, 1, None)
    with pool.Fori(1, NB // 2) as k:
        claim(k * 2, 0, k)
        claim(k * 2 + 1, 1, k)
    for half in range(2):
        pool.wait_ge(claimed[half], NB // 2 * 16 * U)



def scatter_columns(nc, pool, table, b, places, values, bound):
    def half_batch(batch, half, uses):
        if uses is not None:
            pool.wait_ge(b["done"][half], uses * (16 * U))
        nc.gpsimd.tensor_copy(b["places"][:, half, :], places[:, bass.ds(batch * U, U)])
        nc.gpsimd.tensor_copy(b["values"][:, half, :, :], values[:, bass.ds(batch * U, U), :]).then_inc(b["copied"], 1)
        pool.wait_ge(b["copied"], 1)
        pool.sem_clear(b["copied"])
        for u in range(U):
            nc.gpsimd.indirect_dma_start(
                out=table, out_offset=bass.IndirectOffsetOnAxis(ap=b["places"][:, half, u:u + 1], axis=0),
                in_=b["values"][:, half, u, :], in_offset=None, bounds_check=bound, oob_is_err=False
            ).then_inc(b["done"][half], 16)
    half_batch(0, 0, None)
    half_batch(1, 1, None)
    with pool.Fori(1, NB // 2) as k:
        half_batch(k * 2, 0, k)
        half_batch(k * 2 + 1, 1, k)
    for half in range(2):
        pool.wait_ge(b["done"][half], NB // 2 * 16 * U)


def scatter_buffers(nc, name, width):
    return dict(places=nc.alloc_sbuf_tensor(f"{name}_places", [P, 2, U], U32),
                values=nc.alloc_sbuf_tensor(f"{name}_values", [P, 2, U, width], I32),
                copied=nc.alloc_semaphore(f"{name}_copied"),
                done=[nc.alloc_semaphore(f"{name}_done{i}") for i in range(2)])


def phase_digit(nc, net, name, digit_of, places, on_pool, on_sync=None):
    with nc.cleanup_on_exit():
        digits = nc.alloc_sbuf_tensor(f"{name}_digits", [P, T], F32)
        onehot = nc.alloc_sbuf_tensor(f"{name}_onehot", [P, U, R], BF16)
        seen = nc.alloc_sbuf_tensor(f"{name}_seen", [P, U + 1, R], BF16)
        totals = nc.alloc_sbuf_tensor(f"{name}_totals", [P, 2, R], F32)
        base = nc.alloc_sbuf_tensor(f"{name}_base_row", [P, 2, R], F32)
        picked = nc.alloc_sbuf_tensor(f"{name}_picked", [P, 2, R], F32)
        place = nc.alloc_sbuf_tensor(f"{name}_place", [P, U], F32)
        sums = [nc.alloc_psum_tensor(f"{name}_sums{i}", [P, 2, R], F32) for i in range(U // 2)]
        total_ps = nc.alloc_psum_tensor(f"{name}_total", [P, 512], F32)
        step = nc.alloc_semaphore(f"{name}_step")
        counted = nc.alloc_semaphore(f"{name}_counted")
        totalled = nc.alloc_semaphore(f"{name}_totalled")
        marked = nc.alloc_semaphore(f"{name}_marked")
        totals_marked = nc.alloc_semaphore(f"{name}_totals_marked")
        summed = [nc.alloc_semaphore(f"{name}_summed{i}") for i in range(U // 2)]
        taken = [nc.alloc_semaphore(f"{name}_taken{i}") for i in range(U // 2)]
        chain = nc.alloc_semaphore(f"{name}_chain")
        placed = nc.alloc_semaphore(f"{name}_placed")
        with nc.Block(name) as block:
            @block.vector
            def _(v):
                steps = [0]

                def link(ins):
                    steps[0] += 1
                    ins.then_inc(step, 1)
                    v.wait_ge(step, steps[0])

                def mark_columns(batch, last_add):
                    for u in range(U):
                        last = nc.vector.tensor_scalar(onehot[:, u, :], net.iota_r[:, :], digits[:, bass.ds(batch * U + u, 1)], None, ALU.is_equal)
                    last.then_inc(chain, 1)
                    v.wait_ge(chain, 1)
                    v.sem_clear(chain)
                    for u in range(U - 1):
                        nc.vector.tensor_tensor(seen[:, u + 1, :], seen[:, u, :], onehot[:, u, :], ALU.add).then_inc(chain, 1)
                        v.wait_ge(chain, 1)
                        v.sem_clear(chain)
                    nc.vector.tensor_tensor(seen[:, U, :], seen[:, U - 1, :], onehot[:, U - 1, :], ALU.add).then_inc(last_add, 1)
                    v.wait_ge(last_add, batch + 1)
                digit_of(nc, v, link, digits)
                link(nc.vector.memset(seen[:, :, :], 0.0))
                with v.Fori(0, NB) as batch:
                    mark_columns(batch, totals_marked)
                    nc.vector.tensor_copy(seen[:, 0, :], seen[:, U, :]).then_inc(chain, 1)
                    v.wait_ge(chain, 1)
                    v.sem_clear(chain)
                link(nc.vector.tensor_copy(totals[:, 0, :], seen[:, 0, :]))
                net.count_step = steps[0]
                v.wait_ge(totalled, 1)
                link(nc.vector.tensor_copy(totals[:, 1, :], total_ps[:, 0:R]))
                link(nc.vector.memset(base[:, 1, :], 1.0))
                link(nc.vector.tensor_tensor_scan(base[:, 0, :], base[:, 1, :], totals[:, 1, :], 0.0, ALU.mult, ALU.add))
                link(nc.vector.tensor_tensor(base[:, 0, :], base[:, 0, :], totals[:, 1, :], ALU.subtract))
                link(nc.vector.memset(seen[:, 0, :], 0.0))
                with v.Fori(0, NB) as batch:
                    mark_columns(batch, marked)
                    for i in range(U // 2):
                        v.wait_ge(summed[i], batch + 1)
                        nc.vector.tensor_tensor(picked[:, :, :], sums[i][:, :, :], base[:, 0:1, :].to_broadcast([P, 2, R]), ALU.add).then_inc(taken[i], 1)
                        v.wait_ge(taken[i], batch + 1)
                        nc.vector.tensor_tensor(picked[:, :, :], picked[:, :, :], onehot[:, 2 * i:2 * i + 2, :], ALU.mult).then_inc(chain, 1)
                        v.wait_ge(chain, 1)
                        v.sem_clear(chain)
                        nc.vector.tensor_reduce(place[:, 2 * i:2 * i + 2], picked[:, :, :], AX_X, ALU.add).then_inc(chain, 1)
                        v.wait_ge(chain, 1)
                        v.sem_clear(chain)
                    nc.vector.tensor_copy(places[:, bass.ds(batch * U, U)], place[:, :])
                    nc.vector.tensor_copy(seen[:, 0, :], seen[:, U, :]).then_inc(placed, 1)
                    v.wait_ge(placed, batch + 1)

            @block.tensor
            def _(pe):
                pe.wait_ge(step, net.count_step)
                nc.tensor.matmul(total_ps[:, 0:R], net.ones[:, :], totals[:, 0, :], start=True, stop=True).then_inc(totalled, 1)
                with pe.Fori(0, NB) as batch:
                    pe.wait_ge(marked, batch + 1)
                    for i in range(U // 2):
                        nc.tensor.matmul(sums[i][:, :, :].rearrange("p a b -> p (a b)"), net.above[:, :],
                                         onehot[:, 2 * i:2 * i + 2, :].rearrange("p a b -> p (a b)"), start=True, stop=False)
                        nc.tensor.matmul(sums[i][:, :, :].rearrange("p a b -> p (a b)"), net.ones_b[:, :],
                                         seen[:, 2 * i:2 * i + 2, :].rearrange("p a b -> p (a b)"), start=False, stop=True
                                         ).then_inc(summed[i], 1)

            @block.gpsimd
            def _(pool):
                on_pool(pool)

            if on_sync is not None:
                @block.sync
                def _(sp):
                    on_sync(sp)



def at_value(it, g):
    return it * G + (g + 1)


def flat(t):
    return t[:, :, :].rearrange("p j d -> p (j d)")


def blocks(ps):
    return ps[:, :].rearrange("p (j d) -> p j d", j=S)


class Pass:

    def __init__(self, nc, name, iters, step, unit, buffers, io, steps, norms=0):
        self.nc, self.name, self.iters, self.step, self.unit = nc, name, iters, step, unit
        sem = lambda n_: nc.alloc_semaphore(f"{name}_{n_}")
        self.buf = {b: [nc.alloc_sbuf_tensor(f"{name}_{b}{g}", [P, S, width], F32) for g in range(G)] for b, width in buffers}
        self.io = {n_: [sem(f"{n_}{g}") for g in range(G)] for n_ in io}
        self.sem = {n_: sem(n_) for n_ in steps}
        self.psA = [nc.alloc_psum_tensor(f"{name}_psA{g}", [P, 512], F32) for g in range(G)]
        self.psB = [nc.alloc_psum_tensor(f"{name}_psB{g}", [P, 512], F32) for g in range(G)]
        if norms:
            self.stats = [nc.alloc_sbuf_tensor(f"{name}_stats{g}", [P, norms, S, 6], F32) for g in range(G)]
            self.mv = [nc.alloc_sbuf_tensor(f"{name}_mv{g}", [P, norms, S, 2], F32) for g in range(G)]
            self.std = [nc.alloc_sbuf_tensor(f"{name}_std{g}", [P, norms, S], F32) for g in range(G)]
            self.stat = [sem(f"stat{g}") for g in range(G)]
            self.aggregated, self.rooted, self.inverted = ([sem(f"{w_}{i}") for i in range(norms)] for w_ in ("aggregated", "rooted", "inverted"))


def rows_at(c, table, it, g, base=0):
    if c.unit == "nodes":
        return table[bass.ds(it * c.step + (base + g * S * P), S * P), :].rearrange("(p j) d -> p j d", j=S)
    return table[base:base + EP, :].rearrange("(p t) d -> p t d", t=T)[:, bass.ds(column_of(c, it, g), S), :]


def column_of(c, it, g):
    return it * EDGE_STEP + g * S


def prime(c, sp, names):
    for n_ in names:
        for s_ in c.io[n_]:
            sp.sem_inc(s_, 16)


def load_rows(c, sp, name, dst, table, it, base=0):
    for g in range(G):
        sp.dma_start(dst[g][:, :, :], rows_at(c, table, it, g, base)).then_inc(c.io[name][g], 16)


def reload_rows(c, sp, name, dst, table, it, freed, base=0, primed=0):
    for g in range(G):
        rows = rows_at(c, table, it + 1, g, base)
        sp.wait_ge(c.sem[freed], at_value(it, g) + primed)
        sp.dma_start(dst[g][:, :, :], rows).then_inc(c.io[name][g], 16)


def store_rows(c, sp, name, table, src, it, ready, base=0, primed=0):
    for g in range(G):
        rows = rows_at(c, table, it, g, base)
        sp.wait_ge(c.sem[ready], at_value(it, g) + primed)
        if g == 0:
            for g2 in range(G):
                sp.wait_ge(c.io[name][g2], it * 16 + 16)
        sp.dma_start(rows, src[g][:, :, :]).then_inc(c.io[name][g], 16)


def settle(c, sp, names):
    for n_ in names:
        for s_ in c.io[n_]:
            sp.wait_ge(s_, 16 * c.iters + 16)


def loaded(c, engine, name, it, g):
    engine.wait_ge(c.io[name][g], it * 16 + 16)


def stored(c, engine, name, it, g):
    loaded(c, engine, name, it, g)


def each_group(c, engine, it, waits, f, done):
    for g in range(G):
        for w_ in waits:
            if w_ in c.io:
                loaded(c, engine, w_, it, g)
            else:
                engine.wait_ge(c.sem[w_], at_value(it, g))
        f(g).then_inc(c.sem[done], 1)


def take_statistics(c, v, it, i, rows, waits):
    nc = c.nc
    for g in range(G):
        for w_ in waits:
            if w_ in c.io:
                loaded(c, v, w_, it, g)
            else:
                v.wait_ge(c.sem[w_], at_value(it, g))
        for j in range(S):
            last = nc.vector.bn_stats(c.stats[g][:, i, j, :], rows[g][:, j, :])
        last.then_inc(c.stat[g], 1)
    for g in range(G):
        v.wait_ge(c.stat[g], 1)
        v.sem_clear(c.stat[g])
        for j in range(S):
            last = nc.vector.bn_aggr(c.mv[g][:, i, j, :], c.stats[g][:, i, j, :])
        last.then_inc(c.aggregated[i], 1)
    for g in range(G):
        v.wait_ge(c.rooted[i], at_value(it, g))
        nc.vector.reciprocal(c.std[g][:, i, :], c.std[g][:, i, :]).then_inc(c.inverted[i], 1)


def take_root(c, act, net, it, i):
    for g in range(G):
        act.wait_ge(c.aggregated[i], at_value(it, g))
        c.nc.scalar.activation(c.std[g][:, i, :], c.mv[g][:, i, :, 1], ACT.Sqrt, bias=net.eps[:, 0:1]).then_inc(c.rooted[i], 1)


def normalize(c, v, it, i, out, rows, done):
    for g in range(G):
        v.wait_ge(c.inverted[i], at_value(it, g))
        for j in range(S):
            last = c.nc.vector.tensor_scalar(out[g][:, j, :], rows[g][:, j, :], c.mv[g][:, i, j, 0:1],
                                                c.std[g][:, i, j:j + 1], ALU.subtract, ALU.mult)
        last.then_inc(c.sem[done], 1)


def turn_group(c, net, src, ps, width=D):
    for j in range(S):
        last = c.nc.tensor.transpose(ps[0:width, j * P:(j + 1) * P], src[:, j, 0:width], net.ident[:, :])
    return last


def row_product(c, srcT, weight, ps, net=None, bias=None):
    if bias is not None:
        c.nc.tensor.matmul(ps[:, :], net.ones_b[:, :], net.parts[bias][:, :, :].rearrange("p j d -> p (j d)"), start=True, stop=False)
    for j in range(S):
        last = c.nc.tensor.matmul(ps[:, j * P:(j + 1) * P], srcT[:, j, :], weight, start=bias is None, stop=bias is None or j == S - 1)
    return last


def column_product(c, srcT, weight, ps):
    return c.nc.tensor.matmul(ps[:, :], weight, flat(srcT), start=True, stop=True)


def score_product(c, srcT, weight, ps):
    for j in range(S):
        last = c.nc.tensor.matmul(ps[:, j * 2 * H:(j + 1) * 2 * H], srcT[:, j, :], weight, start=True, stop=True)
    return last


def gat_rows_act(c, net, act, it, rows, done, waits, store):
    nc = c.nc
    for g in range(G):
        stored(c, act, store, it, g)
        for w_ in waits:
            act.wait_ge(c.sem[w_], at_value(it, g))
        nc.scalar.activation(rows[g][:, :, 0:D], blocks(c.psB[g]), ACT.Copy)
        nc.scalar.activation(rows[g][:, :, D:WA], c.psA[g][:, 0:S * 2 * H].rearrange("p (j d) -> p j d", j=S), ACT.Copy
                             ).then_inc(c.sem[done], 1)


def scatter_stage(nc, name):
    return dict(places=nc.alloc_sbuf_tensor(f"{name}_places", [P, G, S], U32), copied=nc.alloc_semaphore(f"{name}_copied"),
                done=[nc.alloc_semaphore(f"{name}_done{g}") for g in range(G)], free=nc.alloc_semaphore(f"{name}_free"))


def scatter_rows(nc, pool, c, b, it, idx, out, rows, ready):
    for g in range(G):
        pool.wait_ge(c.sem[ready], at_value(it, g) + G)
        nc.gpsimd.tensor_copy(b["places"][:, g, :], idx[:, bass.ds(column_of(c, it, g), S)]).then_inc(b["copied"], 1)
        pool.wait_ge(b["copied"], 1)
        pool.sem_clear(b["copied"])
        for j in range(S):
            nc.gpsimd.indirect_dma_start(
                out=out, out_offset=bass.IndirectOffsetOnAxis(ap=b["places"][:, g, j:j + 1], axis=0),
                in_=rows[g][:, j, :], in_offset=None, bounds_check=N - 1, oob_is_err=False).then_inc(b["done"][g], 16)
    for g in range(G):
        pool.wait_ge(b["done"][g], it * (16 * S) + 16 * S)
        pool.sem_inc(b["free"], 1)



TAIL_STEPS = ["n2_made", "x2b_made", "h2_made", "h2_turned", "h2T_made", "p_done", "p_made", "u_done", "uT_made",
              "upd_done", "y_made", "yg_made", "x3_made", "n4_made", "h3_turned", "h3T_made", "x0_done", "x0T_made",
              "c1_done", "x1T_made", "g1_made", "c2_done", "x2T_made", "g2_made", "c3_done", "x3T_made", "o_done", "o_made",
              "x0_turned", "r0_made", "x1_turned", "r1_made", "x2_turned", "r2_made"]
TAIL_BUFFERS = [(n_, D) for n_ in ("x2", "n", "hT", "h2", "x0T", "xT", "o")]


def tail_vector(c, net, v, it, edges, o_free):
    nc, f = c.nc, c.buf
    take_statistics(c, v, it, 2, f["x2"], ["x2_made"])
    normalize(c, v, it, 2, f["n"], f["x2"], "n2_made")
    for g in range(G):
        v.wait_ge(c.io["XHX"][g], it * 16 + 32)
        v.wait_ge(c.sem["n2_made"], at_value(it, g))
        nc.vector.tensor_tensor(f["x2"][g][:, :, :], f["x2"][g][:, :, :], slots(net.w["beta"]), ALU.add).then_inc(c.sem["x2b_made"], 1)
    each_group(c, v, it, ["upd_done"], lambda g: nc.vector.tensor_tensor(flat(f["h2"][g]), c.psB[g][:, :], flat(f["h2"][g]), ALU.add), "y_made")
    layer_norm_affine(c, net, v, it)
    take_statistics(c, v, it, 4, f["x2"], ["x3_made"])
    normalize(c, v, it, 4, f["n"], f["x2"], "n4_made")
    for i, ps in ((1, c.psA), (2, c.psB)):
        if edges:
            each_group(c, v, it, [f"x{i}T_made"], lambda g: nc.vector.tensor_tensor(flat(f["hT"][g]), flat(f["xT"][g]), flat(f["x0T"][g]), ALU.add), f"g{i}_made")
        else:
            each_group(c, v, it, [f"c{i}_done"], lambda g: nc.vector.scalar_tensor_tensor(
                out=flat(f["hT"][g]), in0=ps[g][:, :], scalar=0.0, in1=flat(f["x0T"][g]), op0=ALU.max, op1=ALU.add), f"g{i}_made")
    for g in range(G):
        o_free(g)
        v.wait_ge(c.sem["o_done"], at_value(it, g))
        nc.vector.tensor_tensor(flat(f["o"][g]), c.psB[g][:, :], flat(f["x2"][g]), ALU.add).then_inc(c.sem["o_made"], 1)


def layer_norm_affine(c, net, v, it):
    nc, f = c.nc, c.buf
    take_statistics(c, v, it, 3, f["h2"], ["y_made"])
    for g in range(G):
        v.wait_ge(c.inverted[3], at_value(it, g))
        for j in range(S):
            last = nc.vector.scalar_tensor_tensor(out=f["h2"][g][:, j, :], in0=f["h2"][g][:, j, :], scalar=c.mv[g][:, 3, j, 0:1],
                                                  in1=net.w["gamma"][:, :], op0=ALU.subtract, op1=ALU.mult)
        last.then_inc(c.sem["yg_made"], 1)
    for g in range(G):
        v.wait_ge(c.sem["yg_made"], at_value(it, g))
        v.wait_ge(c.sem["x2b_made"], at_value(it, g))
        for j in range(S):
            last = nc.vector.scalar_tensor_tensor(out=f["x2"][g][:, j, :], in0=f["h2"][g][:, j, :], scalar=c.std[g][:, 3, j:j + 1],
                                                  in1=f["x2"][g][:, j, :], op0=ALU.mult, op1=ALU.add)
        last.then_inc(c.sem["x3_made"], 1)


def tail_scalar(c, net, act, it, edges):
    nc, f, w = c.nc, c.buf, net.w
    relu = lambda dst, src, **kw: nc.scalar.activation(flat(dst), src, ACT.Relu, **kw)
    copy = lambda dst, src, **kw: nc.scalar.activation(flat(dst), src, ACT.Copy, **kw)
    take_root(c, act, net, it, 2)
    each_group(c, act, it, ["n2_made"], lambda g: relu(f["h2"][g], flat(f["n"][g])), "h2_made")
    each_group(c, act, it, ["h2_turned"], lambda g: copy(f["hT"][g], c.psA[g][:, :]), "h2T_made")
    if edges:
        each_group(c, act, it, ["PS", "p_done"], lambda g: copy(f["p"][g], c.psB[g][:, :]), "p_made")
    each_group(c, act, it, ["u_done"], lambda g: relu(f["hT"][g], c.psA[g][:, :], bias=w["bu1"][:, 0:1]), "uT_made")
    take_root(c, act, net, it, 3)
    take_root(c, act, net, it, 4)
    each_group(c, act, it, ["h3_turned"], lambda g: relu(f["hT"][g], c.psA[g][:, :]), "h3T_made")
    each_group(c, act, it, ["x0_done"], lambda g: relu(f["x0T"][g], c.psB[g][:, :], bias=w["fc1_b"][:, 0:1], scale=1.0 / X0_SCALE), "x0T_made")
    if edges:
        each_group(c, act, it, ["c1_done"], lambda g: relu(f["xT"][g], c.psA[g][:, :]), "x1T_made")
        each_group(c, act, it, ["GT0", "x0_turned"], lambda g: copy(f["r0"][g], c.psB[g][:, :], scale=X0_SCALE), "r0_made")
        each_group(c, act, it, ["GT1", "x1_turned"], lambda g: copy(f["r1"][g], c.psA[g][:, :]), "r1_made")
        each_group(c, act, it, ["c2_done"], lambda g: relu(f["xT"][g], c.psB[g][:, :]), "x2T_made")
        each_group(c, act, it, ["GT2", "x2_turned"], lambda g: copy(f["r2"][g], c.psB[g][:, :]), "r2_made")
    each_group(c, act, it, ["c3_done"], lambda g: relu(f["hT"][g], c.psA[g][:, :]), "x3T_made")


def tail_tensor(c, net, pe, it, edges):
    f, w = c.buf, net.w
    each_group(c, pe, it, ["h2_made"], lambda g: turn_group(c, net, f["h2"][g], c.psA[g]), "h2_turned")
    if edges:
        each_group(c, pe, it, ["h2T_made"], lambda g: row_product(c, f["hT"][g], w["Wm1a"][:, :], c.psB[g]), "p_done")
    each_group(c, pe, it, ["h2T_made"], lambda g: column_product(c, f["hT"][g], w["Wu1a"][:, :], c.psA[g]), "u_done")
    each_group(c, pe, it, ["p_made", "uT_made"] if edges else ["uT_made"], lambda g: row_product(c, f["hT"][g], w["Wu2"][:, :], c.psB[g], net, "bu2"), "upd_done")
    each_group(c, pe, it, ["n4_made"], lambda g: turn_group(c, net, f["n"][g], c.psA[g]), "h3_turned")
    each_group(c, pe, it, ["h3T_made"], lambda g: column_product(c, f["hT"][g], w["fc1"][:, :], c.psB[g]), "x0_done")
    each_group(c, pe, it, ["x0T_made"], lambda g: column_product(c, f["x0T"][g], w["conv_lone"][:, :], c.psA[g]), "c1_done")
    if edges:
        each_group(c, pe, it, [], lambda g: turn_group(c, net, f["x0T"][g], c.psB[g]), "x0_turned")
        each_group(c, pe, it, ["x1T_made"], lambda g: turn_group(c, net, f["xT"][g], c.psA[g]), "x1_turned")
    each_group(c, pe, it, ["g1_made", "r0_made"] if edges else ["g1_made"], lambda g: column_product(c, f["hT"][g], w["conv1"][:, :], c.psB[g]), "c2_done")
    each_group(c, pe, it, ["g2_made", "r1_made"] if edges else ["g2_made"], lambda g: column_product(c, f["hT"][g], w["conv2"][:, :], c.psA[g]), "c3_done")
    if edges:
        each_group(c, pe, it, ["x2T_made"], lambda g: turn_group(c, net, f["xT"][g], c.psB[g]), "x2_turned")
    each_group(c, pe, it, ["x3T_made", "r2_made"] if edges else ["x3T_made"], lambda g: row_product(c, f["hT"][g], w["fc2"][:, :], c.psB[g], net, "fc2_b"), "o_done")



def phase_nodes(nc, net, inp, out, name, first, iters, on_pool=None):
    w = net.w
    base = first * NODE_STEP
    with nc.cleanup_on_exit():
        c = Pass(nc, name, iters, NODE_STEP, "nodes",
                 TAIL_BUFFERS + [("x", D), ("h1", D), ("t1", WA), ("t2", WA)], ["x", "T1", "T2", "XHX", "out"],
                 TAIL_STEPS + ["n0_made", "h0_turned", "h0T_made", "xh1_done", "t1_made", "xh1_turned", "h1T_made", "xh2_done",
                               "t2_made", "x1_made", "n1_made", "h1_made", "x2_made"], norms=5)
        f = c.buf
        with nc.Block(name) as block:
            @block.sync
            def _(sp):
                prime(c, sp, ["T1", "T2", "XHX", "out"])
                load_rows(c, sp, "x", f["x"], inp["x"], 0, base)

                def iteration(it, more):
                    store_rows(c, sp, "T1", net.T1, f["t1"], it, "t1_made", base=base)
                    store_rows(c, sp, "T2", net.T2, f["t2"], it, "t2_made", base=base)
                    if more:
                        reload_rows(c, sp, "x", f["x"], inp["x"], it, "x1_made", base=base)
                    store_rows(c, sp, "XHX", net.XHX, f["x2"], it, "x2_made", base=base)
                    store_rows(c, sp, "out", out, f["o"], it, "o_made", base=base, primed=G)
                with sp.Fori(0, c.iters - 1) as it:
                    iteration(it, True)
                iteration(c.iters - 1, False)
                settle(c, sp, ["T1", "T2", "XHX", "out"])

            @block.vector
            def _(v):
                with v.Fori(0, c.iters) as it:
                    take_statistics(c, v, it, 0, f["x"], ["x"])
                    normalize(c, v, it, 0, f["n"], f["x"], "n0_made")
                    each_group(c, v, it, ["t2_made"], lambda g: nc.vector.tensor_tensor(
                        f["x2"][g][:, :, :], f["t2"][g][:, :, 0:D], f["x"][g][:, :, :], ALU.add), "x1_made")
                    take_statistics(c, v, it, 1, f["x2"], ["x1_made"])
                    normalize(c, v, it, 1, f["n"], f["x2"], "n1_made")
                    each_group(c, v, it, ["h1_made"], lambda g: nc.vector.tensor_tensor(flat(f["x2"][g]), flat(f["x2"][g]), flat(f["h1"][g]), ALU.add), "x2_made")
                    tail_vector(c, net, v, it, False, lambda g: stored(c, v, "out", it, g))

            @block.scalar
            def _(act):
                relu = lambda dst, src, **kw: nc.scalar.activation(flat(dst), src, ACT.Relu, **kw)
                with act.Fori(0, c.iters) as it:
                    take_root(c, act, net, it, 0)
                    each_group(c, act, it, ["h0_turned"], lambda g: relu(f["hT"][g], c.psA[g][:, :]), "h0T_made")
                    gat_rows_act(c, net, act, it, f["t1"], "t1_made", ["xh1_done"], "T1")
                    each_group(c, act, it, ["xh1_turned"], lambda g: relu(f["hT"][g], c.psA[g][:, :], bias=w["b1"][:, 0:1]), "h1T_made")
                    gat_rows_act(c, net, act, it, f["t2"], "t2_made", ["xh2_done"], "T2")
                    take_root(c, act, net, it, 1)
                    each_group(c, act, it, ["n1_made"], lambda g: relu(f["h1"][g], flat(f["n"][g])), "h1_made")
                    tail_scalar(c, net, act, it, False)

            @block.tensor
            def _(pe):
                pe.sem_inc(c.sem["o_made"], G)
                with pe.Fori(0, c.iters) as it:
                    each_group(c, pe, it, ["n0_made"], lambda g: turn_group(c, net, f["n"][g], c.psA[g]), "h0_turned")
                    for g in range(G):
                        pe.wait_ge(c.sem["o_made"], at_value(it, g))
                        pe.wait_ge(c.sem["h0T_made"], at_value(it, g))
                        row_product(c, f["hT"][g], w["W1"][:, 0:D], c.psB[g])
                        score_product(c, f["hT"][g], w["W1"][:, D:WA], c.psA[g]).then_inc(c.sem["xh1_done"], 1)
                    each_group(c, pe, it, ["t1_made"], lambda g: turn_group(c, net, f["t1"][g], c.psA[g]), "xh1_turned")
                    for g in range(G):
                        pe.wait_ge(c.sem["h1T_made"], at_value(it, g))
                        row_product(c, f["hT"][g], w["W2"][:, 0:D], c.psB[g], net, "b2")
                        score_product(c, f["hT"][g], w["W2"][:, D:WA], c.psA[g]).then_inc(c.sem["xh2_done"], 1)
                    tail_tensor(c, net, pe, it, False)

            if on_pool is not None:
                @block.gpsimd
                def _(pool):
                    on_pool(pool)


def phase_index(nc, net, inp, out):
    s_ = net.S
    half_rows = T // 2
    with nc.cleanup_on_exit():
        sb = lambda name, shape, dt=F32: nc.alloc_sbuf_tensor(name, shape, dt)
        item = sb("sort_items", [P, T, 2], I32)
        key = sb("sort_key", [P, T])
        low = sb("sort_low", [P, T], I32)
        places = sb("sort_places", [P, T], I32)
        packed, tmp = sb("packed", [P, T, 5]), sb("so_tmp", [P, 3, T])
        ordered = sb("ordered", [P, 5, T])
        got = sb("own_src_got", [P, 3, T], I32)
        own_idx, own_val, dst_s = sb("own_src_idx", [P, T], I32), sb("own_src_val", [P, T, 1], I32), sb("dst_s", [P, T], I32)

        def low_digit(nc, v, link, digits):
            link(nc.vector.tensor_scalar(key[:, :], net.dst[:, :], float(N), float(N), ALU.is_equal, ALU.mult))
            link(nc.vector.tensor_tensor(key[:, :], key[:, :], net.src[:, :], ALU.add))
            link(nc.vector.tensor_copy(item[:, :, 0], key[:, :]))
            link(nc.vector.tensor_scalar(item[:, :, 1], net.own_row[:, :], -float(N), None, ALU.add))
            link(nc.vector.tensor_scalar(low[:, :], item[:, :, 0], R - 1, None, ALU.bitwise_and))
            link(nc.vector.tensor_copy(digits[:, :], low[:, :]))


        with nc.cleanup_on_exit():
            values = nc.alloc_sbuf_tensor("own_values", [P, 2, U], I32)
            claim_places = nc.alloc_sbuf_tensor("own_places", [P, 2, U], U32)
            copied = nc.alloc_semaphore("own_copied")
            claimed = [nc.alloc_semaphore(f"own_claimed{i}") for i in range(2)]
            qb = gather_buffers(nc, "q", 1, I32)

            def own_and_q(pool):
                claim_rows(nc, pool, net, claimed, copied, claim_places, values)
                fetch_columns(nc, pool, net.OWN, net.src, qb, lambda batch, half: nc.gpsimd.tensor_copy(
                    net.q[:, bass.ds(batch * U, U)], qb["ring"][:, half, :, 0]))
            phase_digit(nc, net, "low_digit", low_digit, places, own_and_q)

        with nc.cleanup_on_exit():
            b1 = scatter_buffers(nc, "low_items", 2)
            phase_nodes(nc, net, inp, out, "nodes_a", 0, NODE_SPLIT[0],
                        lambda pool: scatter_columns(nc, pool, net.J1, b1, places, item, EP - 1))

        with nc.cleanup_on_exit():
            back = nc.alloc_sbuf_tensor("sort_back", [half_rows, 2, P, 2], I32)
            back_f = nc.alloc_sbuf_tensor("sort_back_f", [half_rows, 2, 2, P], F32)
            ps = nc.alloc_psum_tensor("sort_turn", [P, 512], F32)
            loaded, split, turned, step = (nc.alloc_semaphore(f"sort_{x}") for x in ("loaded", "split", "turned", "step"))
            with nc.Block("turn") as block:
                @block.sync
                def _(sp):
                    sp.dma_start(back[:, :, :, :], net.J1.rearrange("(h t p) k -> t h p k", h=2, p=P)).then_inc(loaded, 16)

                @block.vector
                def _(v):
                    v.wait_ge(loaded, 16)
                    nc.vector.tensor_copy(back_f[:, :, :, :], back[:, :, :, :].rearrange("t h p k -> t h k p")).then_inc(split, 1)
                    v.wait_ge(turned, 1)
                    for h in range(2):
                        for k in range(2):
                            at = (h * 2 + k) * half_rows
                            last = nc.vector.tensor_copy(item[:, h * half_rows:(h + 1) * half_rows, k], ps[:, at:at + half_rows])
                    last.then_inc(step, 1)
                    v.wait_ge(step, 1)
                    steps = [1]

                    def link(ins):
                        steps[0] += 1
                        ins.then_inc(step, 1)
                        v.wait_ge(step, steps[0])
                    link(nc.vector.tensor_scalar(tmp[:, 0, :], net.dst[:, :], float(N), float(N), ALU.is_equal, ALU.mult))
                    link(nc.vector.tensor_tensor(packed[:, :, 0], tmp[:, 0, :], net.src[:, :], ALU.add))
                    nc.vector.tensor_copy(packed[:, :, 1], net.ew[:, :])
                    nc.vector.tensor_copy(packed[:, :, 2], net.r[:, :])
                    link(nc.vector.tensor_copy(packed[:, :, 3], net.q[:, :]))
                    link(nc.vector.tensor_copy(packed[:, :, 4], net.dst_idx[:, :]))

                @block.tensor
                def _(pe):
                    pe.wait_ge(split, 1)
                    for h in range(2):
                        for k in range(2):
                            at = (h * 2 + k) * half_rows
                            last = nc.tensor.transpose(ps[:, at:at + half_rows], back_f[:, h, k, :], net.ident[0:half_rows, 0:half_rows])
                    last.then_inc(turned, 1)


        def high_digit(nc, v, link, digits):
            link(nc.vector.tensor_scalar(low[:, :], item[:, :, 0], 8, None, ALU.logical_shift_right))
            link(nc.vector.tensor_copy(digits[:, :], low[:, :]))

        with nc.cleanup_on_exit():
            xb = gather_buffers(nc, "xd", D, freed_by=16)
            xd = net.XD.rearrange("(p t) d -> p t d", t=T)

            def store_xd(sp):
                with sp.Fori(0, NB // 2) as k:
                    for half in range(2):
                        sp.wait_ge(xb["arrived"][half], k * (16 * U) + 16 * U)
                        sp.dma_start(xd[:, bass.ds((k * 2 + half) * U, U), :], xb["ring"][:, half, :, :]).then_inc(xb["freed"][half], 16)
                for half in range(2):
                    sp.wait_ge(xb["freed"][half], NB // 2 * 16)
            phase_digit(nc, net, "high_digit", high_digit, places,
                        lambda pool: gather_columns(nc, pool, inp["x"], net.dst_idx, xb), store_xd)

        with nc.cleanup_on_exit():
            b2 = scatter_buffers(nc, "high_items", 2)
            pb = gather_buffers(nc, "packed", 5)
            perm2 = sb("perm2", [P, T, 2], I32)
            perm = sb("perm", [P, T], I32)
            stored, loaded_ = nc.alloc_semaphore("packed_stored"), nc.alloc_semaphore("perm_loaded")

            def order_edges(pool):
                pool.dma_start(net.PACK.rearrange("(p t) k -> p t k", t=T), packed[:, :, :]).then_inc(stored, 16)
                scatter_columns(nc, pool, net.J2, b2, places, item, EP - 1)
                pool.dma_start(perm2[:, :, :], net.J2.rearrange("(p t) k -> p t k", t=T)).then_inc(loaded_, 16)
                pool.wait_ge(stored, 16)
                pool.wait_ge(loaded_, 16)
                nc.gpsimd.tensor_copy(perm[:, :], perm2[:, :, 1]).then_inc(pb["staged"], 1)
                pool.wait_ge(pb["staged"], 1)
                pool.sem_clear(pb["staged"])
                fetch_columns(nc, pool, net.PACK, perm, pb, lambda batch, half: nc.gpsimd.tensor_copy(
                    ordered[:, :, bass.ds(batch * U, U)], pb["ring"][:, half, :, :].rearrange("p t k -> p k t")))
            phase_nodes(nc, net, inp, out, "nodes_b", NODE_SPLIT[0], NODE_SPLIT[1], order_edges)

        with nc.cleanup_on_exit():
            nxt = nc.alloc_sbuf_tensor("next_src", [P, 1], F32)
            diag = nc.alloc_sbuf_tensor("so_diag", [P, P], F32)
            ps = [nc.alloc_psum_tensor(f"so_ps{i}", [P, 512], F32) for i in range(2)]
            v_step, turned = nc.alloc_semaphore("so_v_step"), nc.alloc_semaphore("so_turned")
            with nc.Block("source_segments") as block:
                @block.vector
                def _(v):
                    steps = [0]

                    def link(ins):
                        steps[0] += 1
                        ins.then_inc(v_step, 1)
                        v.wait_ge(v_step, steps[0])
                    key = ordered[:, 0, :]
                    nc.vector.tensor_copy(s_.ew[:, :], ordered[:, 1, :])
                    nc.vector.tensor_copy(s_.r[:, :], ordered[:, 2, :])
                    nc.vector.tensor_copy(s_.q[:, :], ordered[:, 3, :])
                    nc.vector.tensor_copy(dst_s[:, :], ordered[:, 4, :])
                    nc.vector.memset(s_.cont[:, 0:1], 0.0)
                    nc.vector.tensor_tensor(s_.cont[:, 1:T], key[:, 1:T], key[:, 0:T - 1], ALU.is_equal)
                    nc.vector.tensor_tensor(tmp[:, 0, 0:T - 1], key[:, 1:T], key[:, 0:T - 1], ALU.not_equal)
                    nc.vector.tensor_scalar(s_.first[:, :], key, key[:, 0:1], None, ALU.is_equal)
                    link(nc.vector.tensor_scalar(diag[:, :], net.ident[:, :], key[:, 0:1], None, ALU.mult))
                    net.so_step = steps[0]
                    v.wait_ge(turned, 1)
                    nc.vector.tensor_copy(nxt[:, :], ps[0][:, 0:1])
                    link(nc.vector.tensor_scalar(s_.later[:, :], ps[1][:, 0:P], key[:, T - 1:T], None, ALU.is_equal))
                    nc.vector.tensor_tensor(tmp[:, 0, T - 1:T], key[:, T - 1:T], nxt[:, :], ALU.not_equal)
                    link(nc.vector.tensor_tensor(s_.later[:, :], s_.later[:, :], net.upper[:, :], ALU.mult))
                    end_of_first(nc, link, net, s_, tmp[:, 2, :])
                    link(nc.vector.tensor_scalar(tmp[:, 1, :], key, -float(SKIP), None, ALU.add))
                    link(nc.vector.tensor_tensor(tmp[:, 1, :], tmp[:, 1, :], tmp[:, 0, :], ALU.mult))
                    nc.vector.tensor_scalar(own_idx[:, :], tmp[:, 1, :], float(SKIP), None, ALU.add)
                    nc.vector.tensor_scalar(s_.own_idx[:, :], tmp[:, 1, :], float(SKIP), None, ALU.add)
                    link(nc.vector.tensor_scalar(own_val[:, :, 0], net.own_row[:, :], -float(N), None, ALU.add))

                @block.tensor
                def _(pe):
                    pe.wait_ge(v_step, net.so_step)
                    nc.tensor.matmul(ps[0][:, 0:1], net.shift[:, :], ordered[:, 0, 0:1], start=True, stop=True)
                    nc.tensor.matmul(ps[1][:, 0:P], net.ones[:, :], diag[:, :], start=True, stop=True).then_inc(turned, 1)


        with nc.cleanup_on_exit():
            sb_ = scatter_buffers(nc, "own_src", 1)
            ob = gather_buffers(nc, "own_src", 1, I32)
            none = nc.alloc_sbuf_tensor("no_row", [125, N // 125], I32)
            based = nc.alloc_semaphore("own_src_based")

            def source_rows_of(pool):
                nc.gpsimd.memset(none[:, :], EP).then_inc(ob["staged"], 1)
                pool.wait_ge(ob["staged"], 1)
                pool.sem_clear(ob["staged"])
                pool.dma_start(net.OWNS[0:N, :].rearrange("(p j) k -> p (j k)", p=125), none[:, :]).then_inc(based, 16)
                pool.wait_ge(based, 16)
                scatter_columns(nc, pool, net.OWNS, sb_, own_idx, own_val, N)
                for i, index in enumerate((dst_s, net.src, net.dst_idx)):
                    fetch_columns(nc, pool, net.OWNS, index, ob, lambda batch, half, i=i: nc.gpsimd.tensor_copy(
                        got[:, i, bass.ds(batch * U, U)], ob["ring"][:, half, :, 0]), i)
            phase_nodes(nc, net, inp, out, "nodes_c", sum(NODE_SPLIT[0:2]), NODE_SPLIT[2], source_rows_of)

        with nc.cleanup_on_exit():
            v_step = nc.alloc_semaphore("homes_step")
            with nc.Block("homes") as block:
                @block.vector
                def _(v):
                    steps = [0]

                    def link(ins):
                        steps[0] += 1
                        ins.then_inc(v_step, 1)
                        v.wait_ge(v_step, steps[0])
                    nc.vector.tensor_copy(s_.s[:, :], got[:, 0, :])
                    link(nc.vector.tensor_scalar(got[:, 1, :], got[:, 1, :], float(EP - 1), None, ALU.min))
                    nc.vector.tensor_copy(net.s[:, :], got[:, 1, :])
                    link(nc.vector.tensor_scalar(tmp[:, 0, :], got[:, 2, :], float(EP), None, ALU.is_lt))
                    link(nc.vector.tensor_tensor(tmp[:, 1, :], got[:, 2, :], net.r[:, :], ALU.subtract))
                    link(nc.vector.tensor_scalar(tmp[:, 1, :], tmp[:, 1, :], float(EP), None, ALU.add))
                    link(nc.vector.tensor_tensor(tmp[:, 1, :], tmp[:, 1, :], tmp[:, 0, :], ALU.mult))
                    link(nc.vector.tensor_tensor(tmp[:, 1, :], tmp[:, 1, :], net.r[:, :], ALU.add))
                    link(nc.vector.tensor_scalar(net.home2[:, :], tmp[:, 1, :], float(N), None, ALU.add))
                    link(nc.vector.tensor_scalar(tmp[:, 0, :], net.q[:, :], float(N), None, ALU.is_ge))
                    link(nc.vector.tensor_tensor(tmp[:, 1, :], net.q[:, :], got[:, 1, :], ALU.subtract))
                    link(nc.vector.tensor_scalar(tmp[:, 1, :], tmp[:, 1, :], -float(N + EP), None, ALU.add))
                    link(nc.vector.tensor_tensor(tmp[:, 1, :], tmp[:, 1, :], tmp[:, 0, :], ALU.mult))
                    link(nc.vector.tensor_tensor(tmp[:, 1, :], tmp[:, 1, :], got[:, 1, :], ALU.add))
                    link(nc.vector.tensor_scalar(net.home3[:, :], tmp[:, 1, :], float(EP), None, ALU.add))


    phase_nodes(nc, net, inp, out, "nodes_d", sum(NODE_SPLIT[0:3]), NODE_ITERS - sum(NODE_SPLIT[0:3]))


NODE_SPLIT = (2, 4, 8)



def phase_fetch(nc, net, name, table, index, out):
    with nc.cleanup_on_exit():
        b = gather_buffers(nc, name, D, freed_by=16)
        view = out.rearrange("(p t) d -> p t d", t=T)
        with nc.Block(name) as block:
            @block.gpsimd
            def _(pool):
                gather_columns(nc, pool, table, index, b)

            @block.sync
            def _(sp):
                with sp.Fori(0, NB // 2) as k:
                    for half in range(2):
                        sp.wait_ge(b["arrived"][half], k * (16 * U) + 16 * U)
                        sp.dma_start(view[:, bass.ds((k * 2 + half) * U, U), :], b["ring"][:, half, :, :]).then_inc(b["freed"][half], 16)
                for half in range(2):
                    sp.wait_ge(b["freed"][half], NB // 2 * 16)


def fix_first_ends(nc, name, out, width):
    return dict(row=nc.alloc_sbuf_tensor(f"{name}_fix_row", [P, width], F32), at=nc.alloc_sbuf_tensor(f"{name}_fix_at", [P, 1], U32),
                carried=nc.alloc_semaphore(f"{name}_carried"), fetched=nc.alloc_semaphore(f"{name}_fix_fetched"),
                added=nc.alloc_semaphore(f"{name}_fix_added"), placed=nc.alloc_semaphore(f"{name}_fix_placed"),
                copied=nc.alloc_semaphore(f"{name}_fix_copied"))


def fix_pool(nc, pool, fix, out, order):
    nc.gpsimd.tensor_copy(fix["at"][:, :], order.first_end[:, :]).then_inc(fix["copied"], 1)
    pool.wait_ge(fix["copied"], 1)
    nc.gpsimd.indirect_dma_start(out=fix["row"][:, :], out_offset=None, in_=out,
                                 in_offset=bass.IndirectOffsetOnAxis(ap=fix["at"][:, 0:1], axis=0)).then_inc(fix["fetched"], 16)
    pool.wait_ge(fix["added"], 1)
    nc.gpsimd.indirect_dma_start(out=out, out_offset=bass.IndirectOffsetOnAxis(ap=fix["at"][:, 0:1], axis=0),
                                 in_=fix["row"][:, :], in_offset=None).then_inc(fix["placed"], 16)
    pool.wait_ge(fix["placed"], 16)


def fix_vector(nc, v, fix, ps, width):
    v.wait_ge(fix["fetched"], 16)
    v.wait_ge(fix["carried"], 1)
    nc.vector.tensor_tensor(fix["row"][:, :], fix["row"][:, :], ps[:, 0:width], ALU.add).then_inc(fix["added"], 1)


def phase_sum(nc, net, name, table, index, order, out, weight=None, relu_with=None):
    with nc.cleanup_on_exit():
        b = gather_buffers(nc, name, D)
        acc = nc.alloc_sbuf_tensor(f"{name}_acc", [P, 2, U, D], F32)
        other = nc.alloc_sbuf_tensor(f"{name}_other", [P, 2, U, D], F32) if relu_with is not None else None
        ps = nc.alloc_psum_tensor(f"{name}_ps", [P, 512], F32)
        chain, cleared = (nc.alloc_semaphore(f"{name}_{x}") for x in ("chain", "cleared"))
        summed, stored, loaded, used = ([nc.alloc_semaphore(f"{name}_{x}{i}") for i in range(2)] for x in ("summed", "stored", "loaded", "used"))
        fix = fix_first_ends(nc, name, out, D)
        view = out[0:EP, :].rearrange("(p t) d -> p t d", t=T)
        with nc.Block(name) as block:
            @block.gpsimd
            def _(pool):
                gather_columns(nc, pool, table, index, b)
                for half in range(2):
                    pool.wait_ge(stored[half], NB // 2 * 16 + 16)
                fix_pool(nc, pool, fix, out, order)

            @block.sync
            def _(sp):
                for half in range(2):
                    sp.sem_inc(stored[half], 16)
                with sp.Fori(0, NB // 2) as k:
                    for half in range(2):
                        sp.wait_ge(summed[half], k + 1)
                        sp.dma_start(view[:, bass.ds((k * 2 + half) * U, U), :], acc[:, half, :, :]).then_inc(stored[half], 16)
                for half in range(2):
                    sp.wait_ge(stored[half], NB // 2 * 16 + 16)

            if relu_with is not None:
                source = relu_with.rearrange("(p t) d -> p t d", t=T)

                @block.scalar
                def _(act):
                    for half in range(2):
                        act.dma_start(other[:, half, :, :], source[:, half * U:(half + 1) * U, :]).then_inc(loaded[half], 16)
                    with act.Fori(1, NB // 2) as k:
                        for half in range(2):
                            act.wait_ge(used[half], k)
                            act.dma_start(other[:, half, :, :], source[:, bass.ds((k * 2 + half) * U, U), :]).then_inc(loaded[half], 16)

            @block.vector
            def _(v):
                def chained(ins):
                    ins.then_inc(chain, 1)
                    v.wait_ge(chain, 1)
                    v.sem_clear(chain)
                chained(nc.vector.memset(acc[:, 1, U - 1, :], 0.0))
                with v.Fori(0, NB // 2) as k:
                    for half in range(2):
                        got = b["ring"][:, half, :, :]
                        v.wait_ge(b["arrived"][half], k * (16 * U) + 16 * U)
                        if relu_with is not None:
                            v.wait_ge(loaded[half], k * 16 + 16)
                            nc.vector.tensor_tensor(got, got, other[:, half, :, :], ALU.add).then_inc(used[half], 1)
                            v.wait_ge(used[half], k + 1)
                            chained(nc.vector.tensor_scalar(got, got, 0.0, None, ALU.max))
                        if weight is not None:
                            chained(nc.vector.tensor_tensor(got, got, weight[:, bass.ds((k * 2 + half) * U, U)].unsqueeze(2).to_broadcast([P, U, D]), ALU.mult))
                        v.wait_ge(stored[half], k * 16 + 16)
                        for u in range(U):
                            before = acc[:, half, u - 1, :] if u else acc[:, 1 - half, U - 1, :]
                            ins = nc.vector.scalar_tensor_tensor(out=acc[:, half, u, :], in0=before, scalar=order.cont[:, bass.ds((k * 2 + half) * U + u, 1)],
                                                                 in1=b["ring"][:, half, u, :], op0=ALU.mult, op1=ALU.add)
                            if u < U - 1:
                                chained(ins)
                        ins.then_inc(b["freed"][half], 1)
                        v.wait_ge(b["freed"][half], k + 1)
                        v.sem_inc(summed[half], 1)
                fix_vector(nc, v, fix, ps, D)

            @block.tensor
            def _(pe):
                pe.wait_ge(summed[1], NB // 2)
                nc.tensor.matmul(ps[:, 0:D], order.later[:, :], acc[:, 1, U - 1, :], start=True, stop=True).then_inc(fix["carried"], 1)



def phase_gat(nc, net, layer):
    name = f"gat{layer + 1}"
    table, index = (net.T1, net.src) if layer == 0 else (net.T2, net.q)
    W_ = D + H
    with nc.cleanup_on_exit():
        Y = nc.alloc_sbuf_tensor(f"{name}_rows", [P, T, W_], F32)
        b = gather_buffers(nc, name, WA)
        alpha, of_owner, m = (nc.alloc_sbuf_tensor(f"{name}_{x}", [P, H, T], F32) for x in ("alpha", "of_owner", "max"))
        own, mask = nc.alloc_sbuf_tensor(f"{name}_own", [P, H, T], F32), nc.alloc_sbuf_tensor(f"{name}_mask", [P, T], F32)
        diag = nc.alloc_sbuf_tensor(f"{name}_diag", [P, H, P], F32)
        cm = nc.alloc_sbuf_tensor(f"{name}_carried_max", [P, H], F32)
        ps = [nc.alloc_psum_tensor(f"{name}_ps{i}", [P, 512], F32) for i in range(4)]
        step, t_step, a_step, out_done, scored = (nc.alloc_semaphore(f"{name}_{x}") for x in ("v_step", "t_step", "a_step", "stored", "scored"))
        fetched = [nc.alloc_semaphore(f"{name}_ad_stored{i}") for i in range(2)]
        fix = fix_first_ends(nc, name, net.RG, W_)
        rounds = 1 if layer == 0 else 0
        before = rounds * (NB // 2)
        ad_view = net.AD1.rearrange("(p t) d -> p t d", t=T)
        value = {}
        with nc.Block(name) as block:
            @block.gpsimd
            def _(pool):
                if layer == 0:
                    gather_columns(nc, pool, net.T1, net.dst_idx, b)
                gather_columns(nc, pool, table, index, b, rounds)
                pool.wait_ge(out_done, 16)
                fix_pool(nc, pool, fix, net.RG, net)

            @block.sync
            def _(sp):
                if layer == 0:
                    with sp.Fori(0, NB // 2) as k:
                        for half in range(2):
                            sp.wait_ge(b["arrived"][half], k * (16 * U) + 16 * U)
                            sp.dma_start(ad_view[:, bass.ds((k * 2 + half) * U, U), :], b["ring"][:, half, :, :]).then_inc(fetched[half], 16)
                    for half in range(2):
                        sp.wait_ge(fetched[half], NB // 2 * 16)
                sp.wait_ge(scored, 1)
                sp.dma_start(net.RG.rearrange("(p t) d -> p t d", t=T), Y[:, :, :]).then_inc(out_done, 16)
                sp.wait_ge(out_done, 16)

            @block.vector
            def _(v):
                steps = [0]

                def link(ins):
                    steps[0] += 1
                    ins.then_inc(step, 1)
                    v.wait_ge(step, steps[0])
                if layer == 0:
                    with v.Fori(0, NB // 2) as k:
                        for half in range(2):
                            v.wait_ge(b["arrived"][half], k * (16 * U) + 16 * U)
                            v.wait_ge(fetched[half], k * 16 + 16)
                            nc.vector.tensor_copy(net.ad[:, :, bass.ds((k * 2 + half) * U, U)],
                                                  b["ring"][:, half, :, D:WA].rearrange("p t k -> p k t")).then_inc(b["freed"][half], 1)
                    for half in range(2):
                        v.wait_ge(b["freed"][half], NB // 2)
                link(nc.vector.tensor_copy(own[:, :, :], net.ad[:, H:2 * H, :]))
                owner_scan(nc, link, net, own[:, :, :], of_owner)
                value["scores"] = steps[0]
                v.wait_ge(t_step, 1)
                owner_carry(nc, link, net, ps[0][:, 0:H], of_owner)
                a_edge, seg = net.a_edge[:, layer * H:(layer + 1) * H, :], net.seg[:, layer * H:(layer + 1) * H, :]
                link(nc.vector.tensor_tensor(of_owner[:, :, :], of_owner[:, :, :], a_edge, ALU.add))
                link(nc.vector.tensor_tensor(own[:, :, :], net.ad[:, 0:H, :], net.ad[:, H:2 * H, :], ALU.add))
                link(nc.vector.tensor_tensor(own[:, :, :], own[:, :, :], seg, ALU.add))
                link(nc.vector.scalar_tensor_tensor(out=own[:, :, :], in0=own[:, :, :], scalar=NEG_SLOPE, in1=own[:, :, :], op0=ALU.mult, op1=ALU.max))
                with v.Fori(0, NB // 2) as k:
                    for half in range(2):
                        v.wait_ge(b["arrived"][half], (k + before) * (16 * U) + 16 * U)
                        nc.vector.tensor_copy(Y[:, bass.ds((k * 2 + half) * U, U), :], b["ring"][:, half, :, 0:W_]).then_inc(b["freed"][half], 1)
                for half in range(2):
                    v.wait_ge(b["freed"][half], before + NB // 2)
                scores_in = Y[:, :, D:W_].rearrange("p t h -> p h t")
                link(nc.vector.tensor_tensor(alpha[:, :, :], scores_in, of_owner[:, :, :], ALU.add))
                link(nc.vector.scalar_tensor_tensor(out=alpha[:, :, :], in0=alpha[:, :, :], scalar=NEG_SLOPE, in1=alpha[:, :, :], op0=ALU.mult, op1=ALU.max))
                link(nc.vector.tensor_scalar(mask[:, :], net.cont[:, :], -1.0, BIG, ALU.add, ALU.mult))
                for h in range(H):
                    last = nc.vector.tensor_tensor_scan(m[:, h, :], mask[:, :], alpha[:, h, :], 0.0, ALU.add, ALU.max)
                link(last)
                for h in range(H):
                    last = nc.vector.tensor_scalar(diag[:, h, :], net.ident[:, :], m[:, h, T - 1:T], None, ALU.mult)
                link(last)
                value["maxima"] = steps[0]
                v.wait_ge(t_step, 2)
                for h in range(H):
                    last = nc.vector.tensor_tensor(diag[:, h, :], ps[1][:, h * P:(h + 1) * P], net.earlier[:, :], ALU.mult)
                link(last)
                link(nc.vector.tensor_tensor(diag[:, :, :], diag[:, :, :], net.earlier_mask[:, :].unsqueeze(1).to_broadcast([P, H, P]), ALU.add))
                link(nc.vector.tensor_reduce(cm[:, :], diag[:, :, :], AX_X, ALU.max))
                link(nc.vector.tensor_scalar(mask[:, :], net.first[:, :], -1.0, BIG, ALU.add, ALU.mult))
                for h in range(H):
                    last = nc.vector.scalar_tensor_tensor(out=m[:, h, :], in0=mask[:, :], scalar=cm[:, h:h + 1], in1=m[:, h, :], op0=ALU.add, op1=ALU.max)
                link(last)
                link(nc.vector.tensor_tensor(m[:, :, :], m[:, :, :], own[:, :, :], ALU.max))
                link(nc.vector.tensor_tensor(own[:, :, :], own[:, :, :], m[:, :, :], ALU.subtract))
                value["own"] = steps[0]
                owner_scan(nc, link, net, m[:, :, :], of_owner)
                value["max"] = steps[0]
                v.wait_ge(t_step, 3)
                owner_carry(nc, link, net, ps[2][:, 0:H], of_owner)
                link(nc.vector.tensor_tensor(alpha[:, :, :], alpha[:, :, :], of_owner[:, :, :], ALU.subtract))
                value["alpha"] = steps[0]
                v.wait_ge(a_step, 2)
                for i in range(NB):
                    cols = slice(i * U, (i + 1) * U)
                    nc.vector.tensor_tensor(Y[:, cols, 0:D].rearrange("p t (h c) -> p t h c", h=H), Y[:, cols, 0:D].rearrange("p t (h c) -> p t h c", h=H),
                                            alpha[:, :, cols].rearrange("p h t -> p t h").unsqueeze(3).to_broadcast([P, U, H, CH]), ALU.mult)
                link(nc.vector.tensor_copy(scores_in, alpha[:, :, :]))
                for d in range(W_):
                    last = nc.vector.tensor_tensor_scan(Y[:, :, d], net.cont[:, :], Y[:, :, d], 0.0, ALU.mult, ALU.add)
                last.then_inc(scored, 1)
                fix_vector(nc, v, fix, ps[3], W_)

            @block.scalar
            def _(act):
                act.wait_ge(step, value["own"])
                nc.scalar.activation(net.pself[:, :, :], own[:, :, :], ACT.Exp).then_inc(a_step, 1)
                act.wait_ge(step, value["alpha"])
                nc.scalar.activation(alpha[:, :, :], alpha[:, :, :], ACT.Exp).then_inc(a_step, 1)

            @block.tensor
            def _(pe):
                pe.wait_ge(step, value["scores"])
                nc.tensor.matmul(ps[0][:, 0:H], net.earlier[:, :], of_owner[:, :, 0], start=True, stop=True).then_inc(t_step, 1)
                pe.wait_ge(step, value["maxima"])
                nc.tensor.matmul(ps[1][:, :], net.ones[:, :], diag[:, :, :].rearrange("p h q -> p (h q)"), start=True, stop=True).then_inc(t_step, 1)
                pe.wait_ge(step, value["max"])
                nc.tensor.matmul(ps[2][:, 0:H], net.earlier[:, :], of_owner[:, :, 0], start=True, stop=True).then_inc(t_step, 1)
                pe.wait_ge(scored, 1)
                nc.tensor.matmul(ps[3][:, 0:W_], net.later[:, :], Y[:, T - 1, :], start=True, stop=True).then_inc(fix["carried"], 1)


GAT_STEPS = ["den_made", "inv_made", "self_made", "num_made", "gat_made"]


def gat_divide(c, net, v, it):
    nc, f = c.nc, c.buf
    own = lambda g: net.pself[:, :, bass.ds(column_of(c, it, g), S)].rearrange("p h s -> p s h")
    heads = lambda buf: buf[:, :, 0:D].rearrange("p s (h c) -> p s h c", h=H)
    each_group(c, v, it, ["r"], lambda g: nc.vector.scalar_tensor_tensor(out=f["inv"][g][:, :, :], in0=f["r"][g][:, :, D:D + H], scalar=1e-16,
                                                                  in1=own(g), op0=ALU.add, op1=ALU.add), "den_made")
    each_group(c, v, it, ["den_made"], lambda g: nc.vector.reciprocal(f["inv"][g][:, :, :], f["inv"][g][:, :, :]), "inv_made")
    each_group(c, v, it, ["xh"], lambda g: nc.vector.tensor_tensor(heads(f["xh"][g]), heads(f["xh"][g]), own(g).unsqueeze(3).to_broadcast([P, S, H, CH]), ALU.mult), "self_made")
    each_group(c, v, it, ["self_made"], lambda g: nc.vector.tensor_tensor(f["r"][g][:, :, 0:D], f["r"][g][:, :, 0:D], f["xh"][g][:, :, 0:D], ALU.add), "num_made")
    each_group(c, v, it, ["num_made", "inv_made"], lambda g: nc.vector.tensor_tensor(
        heads(f["r"][g]), heads(f["r"][g]), f["inv"][g][:, :, :].unsqueeze(3).to_broadcast([P, S, H, CH]), ALU.mult), "gat_made")


def phase_gat1_rows(nc, net):
    w = net.w
    with nc.cleanup_on_exit():
        c = Pass(nc, "gat1_rows", EDGE_ITERS, EDGE_STEP, "edges", [("r", D + H), ("xh", WA), ("inv", H), ("hT", D), ("t2", WA)],
                 ["r", "xh", "T2"], GAT_STEPS + ["turned", "h1T_made", "xh2_done", "t2_made", "ad_made"])
        f = c.buf
        with nc.Block("gat1_rows") as block:
            @block.sync
            def _(sp):
                prime(c, sp, ["T2"])
                load_rows(c, sp, "r", f["r"], net.RG, 0)
                load_rows(c, sp, "xh", f["xh"], net.AD1, 0)

                def iteration(it, more):
                    if more:
                        reload_rows(c, sp, "xh", f["xh"], net.AD1, it, "num_made")
                        reload_rows(c, sp, "r", f["r"], net.RG, it, "turned")
                    store_rows(c, sp, "T2", net.T2, f["t2"], it, "t2_made", base=N)
                with sp.Fori(0, c.iters - 1) as it:
                    iteration(it, True)
                iteration(c.iters - 1, False)
                settle(c, sp, ["T2"])

            @block.vector
            def _(v):
                with v.Fori(0, c.iters) as it:
                    gat_divide(c, net, v, it)

            @block.scalar
            def _(act):
                with act.Fori(0, c.iters) as it:
                    each_group(c, act, it, ["turned"], lambda g: nc.scalar.activation(flat(f["hT"][g]), c.psA[g][:, :], ACT.Relu, bias=w["b1"][:, 0:1]), "h1T_made")
                    gat_rows_act(c, net, act, it, f["t2"], "t2_made", ["xh2_done"], "T2")
                    each_group(c, act, it, [], lambda g: nc.scalar.activation(
                        net.ad[:, :, bass.ds(column_of(c, it, g), S)], c.psA[g][:, 0:S * 2 * H].rearrange("p (j k) -> p k j", j=S), ACT.Copy), "ad_made")

            @block.tensor
            def _(pe):
                pe.sem_inc(c.sem["ad_made"], G)
                with pe.Fori(0, c.iters) as it:
                    each_group(c, pe, it, ["ad_made", "gat_made"], lambda g: turn_group(c, net, f["r"][g], c.psA[g]), "turned")
                    for g in range(G):
                        pe.wait_ge(c.sem["h1T_made"], at_value(it, g))
                        row_product(c, f["hT"][g], w["W2"][:, 0:D], c.psB[g], net, "b2")
                        score_product(c, f["hT"][g], w["W2"][:, D:WA], c.psA[g]).then_inc(c.sem["xh2_done"], 1)


def phase_gat2_rows(nc, net):
    w = net.w
    with nc.cleanup_on_exit():
        c = Pass(nc, "gat2_rows", EDGE_ITERS, EDGE_STEP, "edges", [("r", D + H), ("xh", WA), ("inv", H), ("xd", D), ("x2", D), ("n", D), ("h1", D), ("o", D)],
                 ["r", "xh", "xd", "HD", "XHX"], GAT_STEPS + ["x1_made", "n1_made", "h1_made", "x2_made"], norms=2)
        f = c.buf
        with nc.Block("gat2_rows") as block:
            @block.sync
            def _(sp):
                prime(c, sp, ["HD", "XHX"])
                load_rows(c, sp, "r", f["r"], net.RG, 0)
                load_rows(c, sp, "xh", f["xh"], net.T2, 0, base=N)
                load_rows(c, sp, "xd", f["xd"], net.XD, 0)

                def iteration(it, more):
                    if more:
                        reload_rows(c, sp, "xh", f["xh"], net.T2, it, "num_made", base=N)
                        reload_rows(c, sp, "r", f["r"], net.RG, it, "x1_made")
                        reload_rows(c, sp, "xd", f["xd"], net.XD, it, "x1_made")
                    store_rows(c, sp, "HD", net.HD, f["h1"], it, "h1_made")
                    store_rows(c, sp, "XHX", net.XHX, f["o"], it, "x2_made", base=N)
                with sp.Fori(0, c.iters - 1) as it:
                    iteration(it, True)
                iteration(c.iters - 1, False)
                settle(c, sp, ["HD", "XHX"])

            @block.vector
            def _(v):
                with v.Fori(0, c.iters) as it:
                    gat_divide(c, net, v, it)
                    each_group(c, v, it, ["xd", "gat_made"], lambda g: nc.vector.tensor_tensor(
                        f["x2"][g][:, :, :], f["r"][g][:, :, 0:D], f["xd"][g][:, :, :], ALU.add), "x1_made")
                    take_statistics(c, v, it, 1, f["x2"], ["x1_made"])
                    normalize(c, v, it, 1, f["n"], f["x2"], "n1_made")
                    for g in range(G):
                        stored(c, v, "XHX", it, g)
                        v.wait_ge(c.sem["h1_made"], at_value(it, g))
                        nc.vector.tensor_tensor(flat(f["o"][g]), flat(f["x2"][g]), flat(f["h1"][g]), ALU.add).then_inc(c.sem["x2_made"], 1)

            @block.scalar
            def _(act):
                with act.Fori(0, c.iters) as it:
                    take_root(c, act, net, it, 1)
                    each_group(c, act, it, ["HD", "n1_made"], lambda g: nc.scalar.activation(flat(f["h1"][g]), flat(f["n"][g]), ACT.Relu), "h1_made")


def phase_source_rows(nc, net, out):
    with nc.cleanup_on_exit():
        ios = ["XHX", "PS", "GT0", "GT1", "GT2"]
        c = Pass(nc, "source_rows", EDGE_ITERS, EDGE_STEP, "edges",
                 TAIL_BUFFERS + [(n_, D) for n_ in ("xs", "c1", "c2", "c3", "p", "r0", "r1", "r2")], ["xs", "c1", "c2", "c3"] + ios,
                 TAIL_STEPS + ["a_made", "b_made", "x2_made"], norms=5)
        f = c.buf
        places = scatter_stage(nc, "source_out")
        stores = [("PS", net.PS, "p", "p_made", 0), ("XHX", net.XHX, "x2", "x2_made", N + EP), ("GT0", net.GT[0], "r0", "r0_made", EP),
                  ("GT1", net.GT[1], "r1", "r1_made", EP), ("GT2", net.GT[2], "r2", "r2_made", EP)]
        loads = [("xs", net.XS), ("c1", net.C1), ("c2", net.C2), ("c3", net.C3)]
        with nc.Block("source_rows") as block:
            @block.sync
            def _(sp):
                prime(c, sp, ios)
                for n_, table in loads:
                    load_rows(c, sp, n_, f[n_], table, 0)

                def iteration(it, more):
                    if more:
                        for n_, table in loads:
                            reload_rows(c, sp, n_, f[n_], table, it, "x2_made")
                    for n_, table, buf_, ready, base in stores:
                        store_rows(c, sp, n_, table, f[buf_], it, ready, base=base)
                with sp.Fori(0, c.iters - 1) as it:
                    iteration(it, True)
                iteration(c.iters - 1, False)
                settle(c, sp, ios)

            @block.vector
            def _(v):
                with v.Fori(0, c.iters) as it:
                    each_group(c, v, it, ["a_made", "b_made"], lambda g: nc.vector.tensor_tensor(flat(f["x2"][g]), flat(f["c1"][g]), flat(f["c3"][g]), ALU.add), "x2_made")
                    tail_vector(c, net, v, it, True, lambda g: v.wait_ge(places["free"], at_value(it, g)))

            @block.scalar
            def _(act):
                with act.Fori(0, c.iters) as it:
                    tail_scalar(c, net, act, it, True)

            @block.tensor
            def _(pe):
                pe.sem_inc(c.sem["o_made"], G)
                with pe.Fori(0, c.iters) as it:
                    for g in range(G):
                        pe.wait_ge(c.sem["o_made"], at_value(it, g))
                    tail_tensor(c, net, pe, it, True)

            @block.gpsimd
            def _(pool):
                pool.sem_inc(places["free"], G)
                with pool.Fori(0, c.iters) as it:
                    each_group(c, pool, it, ["c1", "c2"], lambda g: nc.gpsimd.tensor_tensor(flat(f["c1"][g]), flat(f["c1"][g]), flat(f["c2"][g]), ALU.add), "a_made")
                    each_group(c, pool, it, ["c3", "xs"], lambda g: nc.gpsimd.tensor_tensor(flat(f["c3"][g]), flat(f["c3"][g]), flat(f["xs"][g]), ALU.add), "b_made")
                    scatter_rows(nc, pool, c, places, it, net.S.own_idx, out, f["o"], "o_made")


def phase_message_rows(nc, net):
    w = net.w
    with nc.cleanup_on_exit():
        c = Pass(nc, "message_rows", EDGE_ITERS, EDGE_STEP, "edges", [("x", D), ("ea", KE64), ("n", D), ("h2", D), ("hT", D), ("eT", D), ("z", D)],
                 ["x", "ea", "H2D", "Z"], ["n2_made", "h2_made", "turned", "hT_made", "eT_made", "z_done", "z_made"], norms=1)
        f = c.buf
        with nc.Block("message_rows") as block:
            @block.sync
            def _(sp):
                prime(c, sp, ["H2D", "Z"])
                load_rows(c, sp, "x", f["x"], net.X2D, 0)
                load_rows(c, sp, "ea", f["ea"], net.EA64, 0)

                def iteration(it, more):
                    if more:
                        reload_rows(c, sp, "x", f["x"], net.X2D, it, "n2_made")
                        reload_rows(c, sp, "ea", f["ea"], net.EA64, it, "turned")
                    store_rows(c, sp, "H2D", net.H2D, f["h2"], it, "h2_made")
                    store_rows(c, sp, "Z", net.Z, f["z"], it, "z_made", primed=G)
                with sp.Fori(0, c.iters - 1) as it:
                    iteration(it, True)
                iteration(c.iters - 1, False)
                settle(c, sp, ["H2D", "Z"])

            @block.vector
            def _(v):
                with v.Fori(0, c.iters) as it:
                    take_statistics(c, v, it, 0, f["x"], ["x"])
                    normalize(c, v, it, 0, f["n"], f["x"], "n2_made")

            @block.scalar
            def _(act):
                with act.Fori(0, c.iters) as it:
                    take_root(c, act, net, it, 0)
                    each_group(c, act, it, ["H2D", "n2_made"], lambda g: nc.scalar.activation(flat(f["h2"][g]), flat(f["n"][g]), ACT.Relu), "h2_made")
                    each_group(c, act, it, ["turned"], lambda g: nc.scalar.activation(flat(f["hT"][g]), c.psA[g][:, :], ACT.Copy), "hT_made")
                    each_group(c, act, it, [], lambda g: nc.scalar.activation(f["eT"][g][0:KE64, :, :].rearrange("p j d -> p (j d)"),
                                                                                  c.psB[g][0:KE64, :], ACT.Copy), "eT_made")
                    each_group(c, act, it, ["Z", "z_done"], lambda g: nc.scalar.activation(flat(f["z"][g]), c.psB[g][:, :], ACT.Copy), "z_made")

            @block.tensor
            def _(pe):
                pe.sem_inc(c.sem["z_made"], G)

                def z_rows(g):
                    nc.tensor.matmul(c.psB[g][:, :], net.ones_b[:, :], net.parts["bm1"][:, :, :].rearrange("p j d -> p (j d)"), start=True, stop=False)
                    for j in range(S):
                        ps = c.psB[g][:, j * P:(j + 1) * P]
                        nc.tensor.matmul(ps, f["hT"][g][:, j, :], w["Wm1b"][:, :], start=False, stop=False)
                        last = nc.tensor.matmul(ps, f["eT"][g][0:KE64, j, :], w["Wm1c"][:, :], start=False, stop=j == S - 1)
                    return last
                with pe.Fori(0, c.iters) as it:
                    for g in range(G):
                        pe.wait_ge(c.sem["z_made"], at_value(it, g))
                        loaded(c, pe, "ea", it, g)
                        pe.wait_ge(c.sem["h2_made"], at_value(it, g))
                        turn_group(c, net, f["h2"][g], c.psA[g])
                        turn_group(c, net, f["ea"][g], c.psB[g], KE64).then_inc(c.sem["turned"], 1)
                    each_group(c, pe, it, ["hT_made", "eT_made"], z_rows, "z_done")


def phase_update_rows(nc, net):
    w = net.w
    with nc.cleanup_on_exit():
        ios = ["X3D", "X0D", "GT0"]
        c = Pass(nc, "update_rows", EDGE_ITERS, EDGE_STEP, "edges",
                 [(n_, D) for n_ in ("h2", "x2", "r", "count", "hT", "rT", "n", "x0T", "x0", "g0")], ["h2", "x2", "r"] + ios,
                 ["count_made", "h2_turned", "h2T_made", "r_turned", "rT_made", "u_done", "uT_made", "upd_done", "x2b_made",
                  "y_made", "yg_made", "x3_made", "n4_made", "h3_turned", "h3T_made", "x0_done", "x0T_made", "x0_turned", "x0_made", "g0_made"], norms=5)
        f = c.buf
        loads = [("h2", net.H2D, "x3_made"), ("r", net.RM, "r_turned")]
        with nc.Block("update_rows") as block:
            @block.sync
            def _(sp):
                prime(c, sp, ios)
                for n_, table, _ in loads:
                    load_rows(c, sp, n_, f[n_], table, 0)
                load_rows(c, sp, "x2", f["x2"], net.X2D, 0)

                def iteration(it, more):
                    if more:
                        for n_, table, freed in reversed(loads):
                            reload_rows(c, sp, n_, f[n_], table, it, freed)
                    store_rows(c, sp, "X3D", net.X3D, f["x2"], it, "x3_made")
                    if more:
                        for g in range(G):
                            sp.wait_ge(c.io["X3D"][g], it * 16 + 32)
                        reload_rows(c, sp, "x2", f["x2"], net.X2D, it, "n4_made")
                    store_rows(c, sp, "X0D", net.X0D, f["x0"], it, "x0_made", primed=G)
                    store_rows(c, sp, "GT0", net.GT[0], f["g0"], it, "g0_made")
                with sp.Fori(0, c.iters - 1) as it:
                    iteration(it, True)
                iteration(c.iters - 1, False)
                settle(c, sp, ios)

            @block.vector
            def _(v):
                with v.Fori(0, c.iters) as it:
                    for g in range(G):
                        for j in range(S):
                            last = nc.vector.tensor_scalar(f["count"][g][:, j, :], net.ident[:, :], net.seg[:, 2 * H, bass.ds(column_of(c, it, g) + j, 1)], None, ALU.mult)
                        last.then_inc(c.sem["count_made"], 1)
                    each_group(c, v, it, ["x2"], lambda g: nc.vector.tensor_tensor(
                        f["x2"][g][:, :, :], f["x2"][g][:, :, :], slots(w["beta"]), ALU.add), "x2b_made")
                    each_group(c, v, it, ["upd_done"], lambda g: nc.vector.tensor_tensor(flat(f["h2"][g]), c.psB[g][:, :], flat(f["h2"][g]), ALU.add), "y_made")
                    layer_norm_affine(c, net, v, it)
                    take_statistics(c, v, it, 4, f["x2"], ["x3_made"])
                    normalize(c, v, it, 4, f["n"], f["x2"], "n4_made")
                    for g in range(G):
                        stored(c, v, "GT0", it, g)
                        v.wait_ge(c.sem["x0_made"], at_value(it, g) + G)
                        for j in range(S):
                            last = nc.vector.tensor_scalar(f["g0"][g][:, j, :], f["x0"][g][:, j, :], net.dinv[:, bass.ds(column_of(c, it, g) + j, 1)], X0_SCALE, ALU.mult, ALU.mult)
                        last.then_inc(c.sem["g0_made"], 1)

            @block.scalar
            def _(act):
                relu = lambda dst, src, **kw: nc.scalar.activation(flat(dst), src, ACT.Relu, **kw)
                copy = lambda dst, src, **kw: nc.scalar.activation(flat(dst), src, ACT.Copy, **kw)
                with act.Fori(0, c.iters) as it:
                    each_group(c, act, it, ["h2_turned"], lambda g: copy(f["hT"][g], c.psA[g][:, :]), "h2T_made")
                    each_group(c, act, it, ["r_turned"], lambda g: copy(f["rT"][g], c.psB[g][:, :]), "rT_made")
                    each_group(c, act, it, ["u_done"], lambda g: relu(f["hT"][g], c.psA[g][:, :], bias=w["bu1"][:, 0:1]), "uT_made")
                    take_root(c, act, net, it, 3)
                    take_root(c, act, net, it, 4)
                    each_group(c, act, it, ["h3_turned"], lambda g: relu(f["hT"][g], c.psA[g][:, :]), "h3T_made")
                    each_group(c, act, it, ["x0_done"], lambda g: relu(f["x0T"][g], c.psB[g][:, :], bias=w["fc1_b"][:, 0:1], scale=1.0 / X0_SCALE), "x0T_made")
                    each_group(c, act, it, ["X0D", "x0_turned"], lambda g: copy(f["x0"][g], c.psA[g][:, :]), "x0_made")

            @block.tensor
            def _(pe):
                pe.sem_inc(c.sem["x0_made"], G)
                def update(g):
                    nc.tensor.matmul(c.psA[g][:, :], w["Wu1a"][:, :], flat(f["hT"][g]), start=True, stop=False)
                    nc.tensor.matmul(c.psA[g][:, :], w["Wm2u"][:, :], flat(f["rT"][g]), start=False, stop=False)
                    return nc.tensor.matmul(c.psA[g][:, :], w["bm2u"][:, :], flat(f["count"][g]), start=False, stop=True)
                with pe.Fori(0, c.iters) as it:
                    for g in range(G):
                        pe.wait_ge(c.sem["x0_made"], at_value(it, g))
                        loaded(c, pe, "h2", it, g)
                        turn_group(c, net, f["h2"][g], c.psA[g]).then_inc(c.sem["h2_turned"], 1)
                    each_group(c, pe, it, ["r"], lambda g: turn_group(c, net, f["r"][g], c.psB[g]), "r_turned")
                    each_group(c, pe, it, ["h2T_made", "rT_made", "count_made"], update, "u_done")
                    each_group(c, pe, it, ["uT_made"], lambda g: row_product(c, f["hT"][g], w["Wu2"][:, :], c.psB[g], net, "bu2"), "upd_done")
                    each_group(c, pe, it, ["n4_made"], lambda g: turn_group(c, net, f["n"][g], c.psA[g]), "h3_turned")
                    each_group(c, pe, it, ["h3T_made"], lambda g: column_product(c, f["hT"][g], w["fc1"][:, :], c.psB[g]), "x0_done")
                    each_group(c, pe, it, ["x0T_made"], lambda g: turn_group(c, net, f["x0T"][g], c.psA[g]), "x0_turned")


def phase_gcn_rows(nc, net, i, out):
    w = net.w
    last_layer = i == GCN_LAYERS - 1
    with nc.cleanup_on_exit():
        c = Pass(nc, f"gcn_rows{i}", EDGE_ITERS, EDGE_STEP, "edges",
                 [(n_, D) for n_ in ("r", "g", "x0", "h", "hT", "o") + (("x3", "xT") if last_layer else ())],
                 ["r", "g", "x0", "x3", "GT"], ["s_made", "h_made", "turned", "hT_made", "x_done", "xT_made", "o_done", "o_made"])
        f = c.buf
        loads = [("g", net.GT[i], "s_made"), ("r", net.RC[i], "h_made"), ("x0", net.X0D, "h_made")]
        places = scatter_stage(nc, f"gcn_out{i}") if last_layer else None
        with nc.Block(f"gcn_rows{i}") as block:
            @block.sync
            def _(sp):
                prime(c, sp, ["GT"])
                for n_, table, _ in loads:
                    load_rows(c, sp, n_, f[n_], table, 0)
                if last_layer:
                    load_rows(c, sp, "x3", f["x3"], net.X3D, 0)

                def iteration(it, more):
                    if more:
                        for n_, table, freed in loads:
                            reload_rows(c, sp, n_, f[n_], table, it, freed)
                        if last_layer:
                            reload_rows(c, sp, "x3", f["x3"], net.X3D, it, "o_made", primed=G)
                    if not last_layer:
                        store_rows(c, sp, "GT", net.GT[i + 1], f["o"], it, "o_made", primed=G)
                with sp.Fori(0, c.iters - 1) as it:
                    iteration(it, True)
                iteration(c.iters - 1, False)
                if not last_layer:
                    settle(c, sp, ["GT"])

            @block.vector
            def _(v):
                with v.Fori(0, c.iters) as it:
                    for g in range(G):
                        loaded(c, v, "x0", it, g)
                        v.wait_ge(c.sem["s_made"], at_value(it, g))
                        for j in range(S):
                            last = nc.vector.scalar_tensor_tensor(out=f["h"][g][:, j, :], in0=f["r"][g][:, j, :], scalar=net.dinv[:, bass.ds(column_of(c, it, g) + j, 1)],
                                                                  in1=f["x0"][g][:, j, :], op0=ALU.mult, op1=ALU.add)
                        last.then_inc(c.sem["h_made"], 1)
                    if last_layer:
                        for g in range(G):
                            v.wait_ge(places["free"], at_value(it, g))
                            loaded(c, v, "x3", it, g)
                            v.wait_ge(c.sem["o_done"], at_value(it, g))
                            nc.vector.tensor_tensor(flat(f["o"][g]), c.psA[g][:, :], flat(f["x3"][g]), ALU.add).then_inc(c.sem["o_made"], 1)
                    else:
                        for g in range(G):
                            stored(c, v, "GT", it, g)
                            v.wait_ge(c.sem["x_done"], at_value(it, g))
                            for j in range(S):
                                last = nc.vector.tensor_scalar(f["o"][g][:, j, :], c.psB[g][:, j * P:(j + 1) * P], 0.0,
                                                               net.dinv[:, bass.ds(column_of(c, it, g) + j, 1)], ALU.max, ALU.mult)
                            last.then_inc(c.sem["o_made"], 1)

            @block.scalar
            def _(act):
                with act.Fori(0, c.iters) as it:
                    each_group(c, act, it, ["turned"], lambda g: nc.scalar.activation(flat(f["hT"][g]), c.psA[g][:, :], ACT.Copy), "hT_made")
                    if last_layer:
                        each_group(c, act, it, ["x_done"], lambda g: nc.scalar.activation(flat(f["xT"][g]), c.psB[g][:, :], ACT.Relu), "xT_made")

            @block.tensor
            def _(pe):
                pe.sem_inc(c.sem["o_made"], G)
                with pe.Fori(0, c.iters) as it:
                    each_group(c, pe, it, ["o_made", "h_made"], lambda g: turn_group(c, net, f["h"][g], c.psA[g]), "turned")
                    if last_layer:
                        each_group(c, pe, it, ["hT_made"], lambda g: column_product(c, f["hT"][g], w[f"conv{i}"][:, :], c.psB[g]), "x_done")
                        each_group(c, pe, it, ["xT_made"], lambda g: row_product(c, f["xT"][g], w["fc2"][:, :], c.psA[g], net, "fc2_b"), "o_done")
                    else:
                        each_group(c, pe, it, ["hT_made"], lambda g: row_product(c, f["hT"][g], w[f"conv{i}"][:, :], c.psB[g]), "x_done")

            @block.gpsimd
            def _(pool):
                if last_layer:
                    pool.sem_inc(places["free"], G)
                with pool.Fori(0, c.iters) as it:
                    each_group(c, pool, it, ["r", "g"], lambda g: nc.gpsimd.tensor_tensor(flat(f["r"][g]), flat(f["r"][g]), flat(f["g"][g]), ALU.add), "s_made")
                    if last_layer:
                        scatter_rows(nc, pool, c, places, it, net.own_idx, out, f["o"], "o_made")


_INS = ["x", "src", "dst", "edge_attr_16", "edge_attr_64", "edge_weight", "L0_gnn_W1", "L0_gnn_att_src1", "L0_gnn_att_dst1",
        "L0_gnn_W_edge1", "L0_gnn_att_edge1", "L0_gnn_bias1", "L0_gnn_W2", "L0_gnn_att_src2", "L0_gnn_att_dst2",
        "L0_gnn_W_edge2", "L0_gnn_att_edge2", "L0_gnn_bias2", "L2_gnn_Wm1", "L2_gnn_bm1", "L2_gnn_Wm2", "L2_gnn_bm2",
        "L2_gnn_Wu1", "L2_gnn_bu1", "L2_gnn_Wu2", "L2_gnn_bu2", "L2_gnn_gamma", "L2_gnn_beta", "L3_gnn_fc1_w",
        "L3_gnn_fc1_b", "L3_gnn_fc2_w", "L3_gnn_fc2_b", "L3_gnn_conv_w"]


def gnn_kernel(nc, inp, out):
    net = Net()
    allocate(nc, net)
    phase_setup(nc, net, inp)
    phase_own_rows(nc, net)
    phase_index(nc, net, inp, out)
    phase_gat(nc, net, 0)
    phase_gat1_rows(nc, net)
    phase_gat(nc, net, 1)
    phase_gat2_rows(nc, net)
    s_ = net.S
    phase_sum(nc, net, "light1", net.HD, s_.r, s_, net.C1, weight=s_.ew)
    phase_sum(nc, net, "light2", net.C1, s_.s, s_, net.C2, weight=s_.ew)
    phase_sum(nc, net, "light3", net.C2, s_.s, s_, net.C3, weight=s_.ew)
    phase_fetch(nc, net, "fetch_xs", net.XHX[0:N + EP, :], s_.q, net.XS)
    phase_source_rows(nc, net, out)
    phase_fetch(nc, net, "fetch_x2", net.XHX, net.home2, net.X2D)
    phase_message_rows(nc, net)
    phase_sum(nc, net, "messages", net.PS, net.s, net, net.RM, relu_with=net.Z)
    phase_update_rows(nc, net)
    for i in range(GCN_LAYERS):
        phase_sum(nc, net, f"gcn{i}", net.GT[i], net.home3, net, net.RC[i])
        phase_gcn_rows(nc, net, i, out)


def kernel(**inputs):
    import numpy as _np
    import concourse.bacc as _bacc
    from concourse import mybir as _mybir
    from concourse.bass_utils import run_bass_kernel_spmd as _run

    nc = _bacc.Bacc("TRN2", target_bir_lowering=False, num_devices=1)
    arrays, aps = {}, {}
    for name in _INS:
        a = _np.ascontiguousarray(inputs[name])
        arrays[f"in_{name}"] = a
        aps[name] = nc.dram_tensor(f"in_{name}", a.shape, _mybir.dt.from_np(a.dtype), kind="ExternalInput").ap()
    out = nc.dram_tensor("out", (N, D), F32, kind="ExternalOutput").ap()
    gnn_kernel(nc, aps, out)
    return _run(nc, [arrays], core_ids=[0]).results[0]["out"]
```

```python
from contextlib import ExitStack

import concourse.bass as bass
from concourse import mybir

F32 = mybir.dt.float32
I32 = mybir.dt.int32
BF16 = mybir.dt.bfloat16
U32 = mybir.dt.uint32
ALU = mybir.AluOpType
ACT = mybir.ActivationFunctionType
AX_X = mybir.AxisListType.X

N, E, D, H = 50000, 25000, 128, 4
P = 128
CH = D // H
T = -(-E // P)
EP = T * P
E_LAST = E - (P - 1) * T
KE16, KE64 = 16, 64
WA = D + 2 * H
U = 14
NB = T // U
G, S = 4, 4
ROWS = G * S * P
NODE_ITERS = 25
NODE_STEP = (N - ROWS) // (NODE_ITERS - 1)
EDGE_ITERS = 13
EDGE_STEP = (T - G * S) // (EDGE_ITERS - 1)
assert NODE_STEP * (NODE_ITERS - 1) + ROWS == N and NODE_STEP <= ROWS
assert EDGE_STEP * (EDGE_ITERS - 1) + G * S == T and EDGE_STEP <= G * S
assert NB * U == T and NB % 2 == 0
R = 256
SKIP = 1 << 20
BIG = 1e30
LN_EPS = 1e-5
NEG_SLOPE = 0.2
ALPHA, THETA, GCN_LAYERS = 0.1, 0.5, 3
X0_SCALE = (1.0 - ALPHA) / ALPHA


def log_beta(i):
    import math
    return math.log(THETA / (i + 1) + 1.0)


class Net:
    pass


def row(vec):
    return vec.rearrange("(a n) -> a n", a=1).to_broadcast([P, D])


def slots(t):
    return t[:, :].unsqueeze(1).to_broadcast([P, S, D])



def phase_setup(nc, net, inp):
    sb = lambda name, shape, dt=F32: nc.alloc_sbuf_tensor(name, shape, dt)
    sem = nc.alloc_semaphore
    w = net.w
    with nc.cleanup_on_exit():
        ps = [nc.alloc_psum_tensor(f"setup_ps{i}", [P, 512], F32) for i in range(8)]
        ones = net.ones
        att = sb("att_cols", [P, 6])
        att_blocks = sb("att_blocks", [P, 4, H])
        we = sb("w_edge", [KE16, 2, D])
        we_prod = sb("w_edge_prod", [P, 2, H, KE16])
        w_t = sb("w_transposed", [P, 3, P])
        wm2 = sb("wm2", [P, P])
        wu1b = sb("wu1b", [P, P])
        wae = sb("w_att_edge", [P, 2 * H, KE16])
        bm2 = sb("bm2_col", [P, 1])
        bm2_wide = sb("bm2_wide", [P, P])
        conv = sb("conv", [P, GCN_LAYERS, P])
        ea = sb("edge_attr", [P, T, KE16])
        prod = sb("edge_prod", [P, T, KE16])
        dst_i = sb("dst_int", [P, T], I32)
        nxt_i = sb("next_dst_int", [P, 1], I32)
        nxt = sb("next_dst", [P, 1])
        diag = sb("dst_diag", [P, 2, P])
        lower = sb("lower", [P, P])
        tmp = sb("setup_tmp", [P, T])
        iota_i = sb("iota_i", [P, R], I32)

        loaded = sem("weights_loaded")
        edges_loaded = sem("edges_loaded")
        cleared = sem("pads_cleared")
        zeros = sb("zeros", [P, D])
        split, part_b = sb("bias_split", [P, 3, D]), sb("bias_part", [P, D], BF16)
        zeroed, padded = sem("zeroed"), sem("padded")
        pool_made = sem("identity_made")
        p_step = sem("pool_step")
        v_step = sem("vector_step")
        t_done = sem("tensor_step")
        with nc.Block("setup") as block:
            @block.sync
            def _(sp):
                n = 0

                def load(dst, src):
                    sp.dma_start(dst, src).then_inc(loaded, 16)
                    return 1
                col = lambda v: v.rearrange("(p a) -> p a", a=1)
                flat = lambda v: v.rearrange("h (c a) -> (h c) a", a=1)
                n += load(w["W1"][:, 0:D], inp["L0_gnn_W1"])
                n += load(w["W2"][:, 0:D], inp["L0_gnn_W2"])
                n += load(w["Wm1a"][:, :], inp["L2_gnn_Wm1"][0:D, :])
                n += load(w["Wm1b"][:, :], inp["L2_gnn_Wm1"][D:2 * D, :])
                n += load(w["Wm1c"][:, :], inp["L2_gnn_Wm1"][2 * D:2 * D + KE64, :])
                n += load(wm2[:, :], inp["L2_gnn_Wm2"])
                n += load(w["Wu1a"][:, :], inp["L2_gnn_Wu1"][0:D, :])
                n += load(wu1b[:, :], inp["L2_gnn_Wu1"][D:2 * D, :])
                n += load(w["Wu2"][:, :], inp["L2_gnn_Wu2"])
                n += load(w["fc1"][:, :], inp["L3_gnn_fc1_w"])
                n += load(w["fc2"][:, :], inp["L3_gnn_fc2_w"])
                for i in range(GCN_LAYERS):
                    n += load(conv[:, i, :], inp["L3_gnn_conv_w"][i])
                for i, name in enumerate(("src1", "dst1", "src2", "dst2", "edge1", "edge2")):
                    n += load(att[:, i:i + 1], flat(inp[f"L0_gnn_att_{name}"]))
                for i in range(2):
                    n += load(we[:, i, :], inp[f"L0_gnn_W_edge{i + 1}"])
                n += load(bm2[:, :], col(inp["L2_gnn_bm2"]))
                n += load(w["b1"][:, :], col(inp["L0_gnn_bias1"]))
                n += load(w["bu1"][:, :], col(inp["L2_gnn_bu1"]))
                n += load(w["fc1_b"][:, :], col(inp["L3_gnn_fc1_b"]))
                for name, key in ROW_BIASES:
                    n += load(w[name][:, :], row(inp[key]))
                assert n == N_LOADS
                sp.wait_ge(zeroed, 1)
                sp.dma_start(net.EA64[E:EP, :], zeros[0:EP - E, 0:KE64]).then_inc(padded, 16)
                sp.dma_start(net.C1[EP:EP + 1, :], zeros[0:1, :]).then_inc(padded, 16)
                sp.dma_start(net.C2[EP:EP + 1, :], zeros[0:1, :]).then_inc(padded, 16)
                sp.wait_ge(cleared, 5)

                def edge_load(dst, src, k):
                    head = src[0:(P - 1) * T, :].rearrange("(p t) k -> p t k", t=T)
                    for a, b in ((0, 112), (112, P - 1)):
                        sp.dma_start(dst[a:b, :, :], head[a:b]).then_inc(edges_loaded, 16)
                    sp.dma_start(dst[P - 1:P, 0:E_LAST, :],
                                 src[(P - 1) * T:E, :].rearrange("(p t) k -> p t k", p=1)).then_inc(edges_loaded, 16)
                one = lambda v: v.rearrange("(e k) -> e k", k=1)
                edge_load(dst_i[:, :].unsqueeze(2), one(inp["dst"]), 1)
                edge_load(net.src[:, :].unsqueeze(2), one(inp["src"]), 1)
                edge_load(net.ew[:, :].unsqueeze(2), one(inp["edge_weight"]), 1)
                edge_load(ea[:, :, :], inp["edge_attr_16"], KE16)
                sp.dma_start(net.EA64[0:E, :], inp["edge_attr_64"]).then_inc(padded, 16)
                sp.dma_start(nxt_i[0:P - 1, :], next_heads(inp["dst"]), allow_slow_non_contiguous=True).then_inc(edges_loaded, 16)
                sp.wait_ge(padded, 64)

            @block.gpsimd
            def _(pool):
                nc.gpsimd.memset(net.ident[:, :], 0.0).then_inc(p_step, 1)
                nc.gpsimd.memset(net.upper[:, :], 1.0).then_inc(p_step, 1)
                nc.gpsimd.memset(lower[:, :], 1.0).then_inc(p_step, 1)
                nc.gpsimd.memset(net.shift[:, :], 0.0).then_inc(p_step, 1)
                nc.gpsimd.iota(iota_i[:, :], [[1, R]], base=0, channel_multiplier=0).then_inc(p_step, 1)
                nc.gpsimd.iota(net.own_row[:, :], [[1, T]], base=N, channel_multiplier=T).then_inc(p_step, 1)
                nc.gpsimd.iota(net.node_id[:, :], [[1, N // 125]], base=0, channel_multiplier=N // 125).then_inc(p_step, 1)
                pool.wait_ge(p_step, 7)
                nc.gpsimd.affine_select(out=net.ident[:, :], in_=net.ident[:, :], compare_op=ALU.not_equal, fill=1.0,
                                        base=0, pattern=[[-1, P]], channel_multiplier=1).then_inc(pool_made, 1)
                nc.gpsimd.affine_select(out=net.upper[:, :], in_=net.upper[:, :], compare_op=ALU.is_gt, fill=0.0,
                                        base=0, pattern=[[1, P]], channel_multiplier=-1).then_inc(pool_made, 1)
                nc.gpsimd.affine_select(out=lower[:, :], in_=lower[:, :], compare_op=ALU.is_gt, fill=0.0,
                                        base=0, pattern=[[-1, P]], channel_multiplier=1).then_inc(pool_made, 1)
                nc.gpsimd.affine_select(out=net.shift[:, :], in_=net.shift[:, :], compare_op=ALU.not_equal, fill=1.0,
                                        base=-1, pattern=[[-1, P]], channel_multiplier=1).then_inc(pool_made, 1)
                pool.dma_start(net.OWN[0:N, :].rearrange("(p j) k -> p (j k)", p=125), net.node_id[:, :]).then_inc(net.own_base, 16)
                pool.wait_ge(net.own_base, 16)

            @block.vector
            def _(v):
                steps = [0]

                def link(ins):
                    steps[0] += 1
                    ins.then_inc(v_step, 1)
                    v.wait_ge(v_step, steps[0])

                nc.vector.memset(dst_i[:, :], N).then_inc(cleared, 1)
                nc.vector.memset(net.src[:, :], 0).then_inc(cleared, 1)
                nc.vector.memset(net.ew[:, :], 0.0).then_inc(cleared, 1)
                nc.vector.memset(ea[:, :, :], 0.0).then_inc(cleared, 1)
                nc.vector.memset(nxt_i[:, :], -1).then_inc(cleared, 1)
                nc.vector.memset(net.eps[:, :], LN_EPS)
                nc.vector.memset(zeros[:, :], 0.0).then_inc(zeroed, 1)
                nc.vector.memset(att_blocks[:, :, :], 0.0)
                nc.vector.memset(we_prod[:, :, :, :], 0.0)
                link(nc.vector.memset(ones[:, :], 1.0))
                v.wait_ge(loaded, 16 * N_LOADS)
                for a in range(4):
                    for h in range(H):
                        r = slice(h * CH, (h + 1) * CH)
                        nc.vector.tensor_copy(att_blocks[r, a, h:h + 1], att[r, a:a + 1])
                link(nc.vector.tensor_copy(bm2_wide[:, :], bm2[:, :].to_broadcast([P, P])))
                v.wait_ge(pool_made, 4)
                nc.vector.tensor_copy(net.iota_r[:, :], iota_i[:, :])
                nc.vector.tensor_copy(net.ones_b[:, :], ones[:, :])
                nc.vector.tensor_copy(net.above[:, :], net.upper[:, :])
                v.wait_ge(t_done, 1)
                link(nc.vector.tensor_copy(w_t[:, :, :], ps[0][:, 0:3 * P].rearrange("p (a b) -> p a b", a=3)))
                for i in range(2):
                    for h in range(H):
                        r = slice(h * CH, (h + 1) * CH)
                        last = nc.vector.tensor_scalar(we_prod[r, i, h, :], ps[1][r, i * KE16:(i + 1) * KE16],
                                                       att[r, 4 + i:5 + i], None, ALU.mult)
                link(last)
                v.wait_ge(t_done, 2)
                nc.vector.tensor_copy(w["W1"][:, D:WA], ps[2][:, 0:2 * H])
                nc.vector.tensor_copy(w["W2"][:, D:WA], ps[2][:, 2 * H:4 * H])
                nc.vector.tensor_copy(w["Wm2u"][:, :], ps[3][:, 0:P])
                nc.vector.tensor_copy(w["bm2u"][:, :], ps[4][:, 0:P])
                link(nc.vector.tensor_copy(wae[:, :, :], ps[5][:, 0:2 * H * KE16].rearrange("p (a b) -> p a b", b=KE16)))
                for i in range(GCN_LAYERS):
                    link(nc.vector.tensor_scalar(w[f"conv{i}"][:, :], net.ident[:, :], 1.0 - log_beta(i), None, ALU.mult))
                    link(nc.vector.scalar_tensor_tensor(out=w[f"conv{i}"][:, :], in0=conv[:, i, :], scalar=log_beta(i),
                                                        in1=w[f"conv{i}"][:, :], op0=ALU.mult, op1=ALU.add))
                    if i == 0:
                        link(nc.vector.tensor_scalar(w["conv_lone"][:, :], w["conv0"][:, :], X0_SCALE, None, ALU.mult))
                    link(nc.vector.tensor_scalar(w[f"conv{i}"][:, :], w[f"conv{i}"][:, :], 1.0 - ALPHA, None, ALU.mult))
                link(nc.vector.tensor_scalar(w["fc1_b"][:, :], w["fc1_b"][:, :], 1.0 / X0_SCALE, None, ALU.mult))
                for name in net.parts:
                    high, rest = split[:, 0, :], split[:, 1, :]
                    link(nc.vector.tensor_copy(rest, w[name][:, :]))
                    for k in range(3):
                        link(nc.vector.tensor_copy(part_b[:, :], rest))
                        link(nc.vector.tensor_copy(high, part_b[:, :]))
                        link(nc.vector.tensor_tensor(rest, rest, high, ALU.subtract))
                        if k == 0:
                            link(nc.vector.tensor_scalar(split[:, 2, :], high, net.ident[:, 0:1], None, ALU.mult))
                        else:
                            link(nc.vector.scalar_tensor_tensor(out=split[:, 2, :], in0=high, scalar=net.ident[:, k:k + 1], in1=split[:, 2, :],
                                                                op0=ALU.mult, op1=ALU.add))
                    link(nc.vector.tensor_copy(net.parts[name][:, :, :], split[:, 2:3, :].to_broadcast([P, S, D])))
                v.wait_ge(edges_loaded, 16 * N_EDGE_LOADS)
                dst = net.dst
                nc.vector.tensor_copy(nxt[:, :], nxt_i[:, :])
                link(nc.vector.tensor_copy(dst[:, :], dst_i[:, :]))
                nc.vector.memset(net.cont[:, 0:1], 0.0)
                nc.vector.tensor_tensor(net.cont[:, 1:T], dst[:, 1:T], dst[:, 0:T - 1], ALU.is_equal)
                nc.vector.tensor_tensor(net.ends[:, 0:T - 1], dst[:, 1:T], dst[:, 0:T - 1], ALU.not_equal)
                nc.vector.tensor_tensor(net.ends[:, T - 1:T], dst[:, T - 1:T], nxt[:, :], ALU.not_equal)
                nc.vector.tensor_scalar(net.first[:, :], dst[:, :], dst[:, 0:1], None, ALU.is_equal)
                link(nc.vector.tensor_scalar(net.last[:, :], dst[:, :], dst[:, T - 1:T], None, ALU.is_equal))
                link(nc.vector.tensor_scalar(net.not_end[:, :], net.ends[:, :], -1.0, 1.0, ALU.mult, ALU.add))
                v.wait_ge(pool_made, 4)
                end_of_first(nc, link, net, net, tmp)
                nc.vector.tensor_scalar(diag[:, 0, :], net.ident[:, :], dst[:, 0:1], None, ALU.mult)
                link(nc.vector.tensor_scalar(diag[:, 1, :], net.ident[:, :], dst[:, T - 1:T], None, ALU.mult))
                net.diag_step = steps[0]
                link(nc.vector.tensor_scalar(tmp[:, :], dst[:, :], -float(SKIP), None, ALU.add))
                link(nc.vector.tensor_tensor(tmp[:, :], tmp[:, :], net.ends[:, :], ALU.mult))
                link(nc.vector.tensor_scalar(net.own_idx[:, :], tmp[:, :], float(SKIP), None, ALU.add))
                link(nc.vector.tensor_scalar(net.dst_idx[:, :], dst[:, :], float(N - 1), None, ALU.min))
                v.wait_ge(t_done, 3)
                nc.vector.tensor_scalar(net.later[:, :], ps[6][:, 0:P], dst[:, T - 1:T], None, ALU.is_equal)
                link(nc.vector.tensor_scalar(net.earlier[:, :], ps[7][:, 0:P], dst[:, 0:1], None, ALU.is_equal))
                nc.vector.tensor_tensor(net.later[:, :], net.later[:, :], net.upper[:, :], ALU.mult)
                link(nc.vector.tensor_tensor(net.earlier[:, :], net.earlier[:, :], lower[:, :], ALU.mult))
                link(nc.vector.tensor_scalar(net.earlier_mask[:, :], net.earlier[:, :], -1.0, BIG, ALU.add, ALU.mult))
                for j in range(2 * H):
                    link(nc.vector.tensor_tensor(prod[:, :, :], ea[:, :, :],
                                                 wae[:, j:j + 1, :].to_broadcast([P, T, KE16]), ALU.mult))
                    link(nc.vector.tensor_reduce(net.a_edge[:, j, :], prod[:, :, :], AX_X, ALU.add))
                nc.vector.memset(tmp[:, :], 1.0)
                link(nc.vector.memset(net.seg[:, :, :], 0.0))
                for j in range(2 * H):
                    nc.vector.tensor_tensor_scan(net.seg[:, j, :], net.cont[:, :], net.a_edge[:, j, :], 0.0, ALU.mult, ALU.add)
                link(nc.vector.tensor_tensor_scan(net.seg[:, 2 * H, :], net.cont[:, :], tmp[:, :], 0.0, ALU.mult, ALU.add))
                net.seg_step = steps[0]
                v.wait_ge(t_done, 4)
                link(nc.vector.tensor_copy(net.carry[:, 0:2 * H + 1], ps[0][:, 0:2 * H + 1]))
                for j in range(2 * H + 1):
                    last = nc.vector.scalar_tensor_tensor(out=net.seg[:, j, :], in0=net.first[:, :], scalar=net.carry[:, j:j + 1],
                                                          in1=net.seg[:, j, :], op0=ALU.mult, op1=ALU.add)
                link(last)
                cnt = net.seg[:, 2 * H, :]
                link(nc.vector.tensor_scalar(tmp[:, :], cnt, 1.0, None, ALU.max))
                link(nc.vector.reciprocal(tmp[:, :], tmp[:, :]))
                for j in range(2 * H):
                    last = nc.vector.tensor_tensor(net.seg[:, j, :], net.seg[:, j, :], tmp[:, :], ALU.mult)
                link(last)
                net.cnt_step = steps[0]
                v.wait_ge(t_done, 5)
                link(nc.vector.reciprocal(net.dinv[:, :], net.dinv[:, :]))

            @block.tensor
            def _(pe):
                pe.wait_ge(loaded, 16 * N_LOADS)
                pe.wait_ge(pool_made, 4)
                pe.wait_ge(v_step, 2)
                for i, m in enumerate((w["W1"][:, 0:D], w["W2"][:, 0:D], wm2[:, :])):
                    nc.tensor.transpose(ps[0][:, i * P:(i + 1) * P], m, net.ident[:, :])
                for i in range(2):
                    last = nc.tensor.transpose(ps[1][:, i * KE16:(i + 1) * KE16], we[:, i, :], net.ident[0:KE16, 0:KE16])
                last.then_inc(t_done, 1)
                pe.wait_ge(v_step, 4)
                for i in range(4):
                    nc.tensor.matmul(ps[2][:, i * H:(i + 1) * H], w_t[:, i // 2, :], att_blocks[:, i, :], start=True, stop=True)
                nc.tensor.matmul(ps[3][:, 0:P], w_t[:, 2, :], wu1b[:, :], start=True, stop=True)
                nc.tensor.matmul(ps[4][:, 0:P], bm2_wide[:, :], wu1b[:, :], start=True, stop=True)
                nc.tensor.matmul(ps[5][:, 0:2 * H * KE16], ones[:, :], we_prod[:, :, :, :].rearrange("p a h k -> p (a h k)"),
                                 start=True, stop=True).then_inc(t_done, 1)
                pe.wait_ge(v_step, net.diag_step)
                nc.tensor.matmul(ps[6][:, 0:P], ones[:, :], diag[:, 0, :], start=True, stop=True)
                nc.tensor.matmul(ps[7][:, 0:P], ones[:, :], diag[:, 1, :], start=True, stop=True).then_inc(t_done, 1)
                pe.wait_ge(v_step, net.seg_step)
                nc.tensor.matmul(ps[0][:, 0:2 * H + 1], net.later[:, :], net.seg[:, 0:2 * H + 1, T - 1], start=True,
                                 stop=True).then_inc(t_done, 1)

            @block.scalar
            def _(act):
                act.wait_ge(v_step, net.cnt_step)
                nc.scalar.activation(net.dinv[:, :], net.seg[:, 2 * H, :], ACT.Sqrt, bias=ones[:, 0:1]).then_inc(t_done, 1)


N_EDGE_LOADS = 4 * 3 + 1
ROW_BIASES = [("b2", "L0_gnn_bias2"), ("bu2", "L2_gnn_bu2"), ("gamma", "L2_gnn_gamma"), ("beta", "L2_gnn_beta"),
              ("fc2_b", "L3_gnn_fc2_b"), ("bm1", "L2_gnn_bm1")]
N_LOADS = 11 + GCN_LAYERS + 6 + 2 + 4 + len(ROW_BIASES)


def next_heads(dst):
    return bass.AP(tensor=dst.tensor, offset=dst.offset + T, ap=[[T, P - 1], [1, 1]])


def end_of_first(nc, link, net, order, tmp):
    link(nc.vector.tensor_reduce(tmp[:, 0:1], order.first[:, :], AX_X, ALU.add))
    link(nc.vector.tensor_tensor(tmp[:, 0:1], tmp[:, 0:1], net.own_row[:, 0:1], ALU.add))
    link(nc.vector.tensor_scalar(order.first_end[:, :], tmp[:, 0:1], -float(N + 1), None, ALU.add))


def allocate(nc, net):
    sb = lambda name, shape, dt=F32: nc.alloc_sbuf_tensor(name, shape, dt)
    dram = lambda name, shape, dt=F32: nc.dram_tensor(name, shape, dt, kind="Internal").ap()
    net.w = {name: sb(f"w_{name}", [P, P]) for name in
             ("Wm1a", "Wm1b", "Wu1a", "Wm2u", "bm2u", "Wu2", "fc1", "fc2", "conv0", "conv1", "conv2", "conv_lone")}
    net.w["W1"], net.w["W2"] = sb("w_W1", [P, WA]), sb("w_W2", [P, WA])
    net.w["Wm1c"] = sb("w_Wm1c", [KE64, P])
    for name in ("b1", "bu1", "fc1_b"):
        net.w[name] = sb(f"w_{name}", [P, 1])
    for name, _ in ROW_BIASES:
        net.w[name] = sb(f"w_{name}", [P, D])
    net.parts = {name: sb(f"parts_{name}", [P, S, D], BF16) for name in ("b2", "bu2", "fc2_b", "bm1")}
    net.ident = sb("ident", [P, P])
    net.eps = sb("eps", [P, 1])
    net.later, net.earlier, net.earlier_mask = (sb(n, [P, P]) for n in ("later", "earlier", "earlier_mask"))
    net.src, net.own_row = sb("src_cols", [P, T], I32), sb("own_row", [P, T], I32)
    net.node_id = sb("node_id", [125, N // 125], I32)
    net.own_idx, net.dst_idx, net.q, net.r = (sb(n, [P, T], I32) for n in
                                             ("own_idx", "dst_idx", "q", "r"))
    net.dst, net.cont, net.ends, net.not_end, net.first, net.last, net.ew, net.dinv = (
        sb(n, [P, T]) for n in ("dst", "cont", "ends", "not_end", "first", "last", "ew", "dinv"))
    net.a_edge = sb("a_edge", [P, 2 * H, T])
    net.seg = sb("seg", [P, 2 * H + 1, T])
    net.carry = sb("carry", [P, WA])
    net.own_base = nc.alloc_semaphore("own_base")
    net.XD = dram("XD", (EP, D))
    net.J1, net.J2, net.PACK = dram("J1", (EP, 2), I32), dram("J2", (EP, 2), I32), dram("PACK", (EP, 5))
    net.OWNS = dram("OWNS", (N + 1, 1), I32)
    net.iota_r = sb("iota_r", [P, R])
    net.ones, net.ones_b, net.above = sb("ones", [P, P]), sb("ones_b", [P, P], BF16), sb("above", [P, P], BF16)
    net.upper, net.shift = sb("upper", [P, P]), sb("shift", [P, P])
    net.s, net.home2, net.home3 = (sb(n, [P, T], I32) for n in ("s", "home2", "home3"))
    net.S = Net()
    net.S.cont, net.S.first, net.S.ew = (sb(n, [P, T]) for n in ("s_cont", "s_first", "s_ew"))
    net.S.r, net.S.q, net.S.s, net.S.own_idx = (sb(n, [P, T], I32) for n in ("s_r", "s_q", "s_s", "s_own_idx"))
    net.S.later = sb("s_later", [P, P])
    net.OWN = dram("OWN", (N + 1, 1), I32)
    NT = N + EP
    net.first_end, net.S.first_end = sb("first_end", [P, 1], I32), sb("s_first_end", [P, 1], I32)
    net.ad, net.pself = sb("node_scores", [P, 2 * H, T]), sb("p_self", [P, H, T])
    net.T1, net.T2 = dram("T1", (N, WA)), dram("T2", (N + EP, WA))
    net.AD1, net.RG = dram("AD1", (EP, WA)), dram("RG", (EP, D + H))
    net.XHX, net.HD = dram("XHX", (N + 2 * EP, D)), dram("HD", (EP, D))
    net.C1, net.C2, net.C3 = dram("C1", (EP + 1, D)), dram("C2", (EP + 1, D)), dram("C3", (EP, D))
    net.PS, net.X2D, net.H2D, net.Z, net.RM = (dram(n, (EP, D)) for n in ("PS", "X2D", "H2D", "Z", "RM"))
    net.X3D, net.X0D = dram("X3D", (EP, D)), dram("X0D", (EP, D))
    net.GT = [dram(f"GT{i}", (2 * EP, D)) for i in range(3)]
    net.RC = [dram(f"RC{i}", (EP, D)) for i in range(3)]
    net.EA64 = dram("EA64", (EP, KE64))



def gather_columns(nc, pool, table, index, b, rounds=0):
    ring, stage, staged, arrived, freed, freed_by = (b[x] for x in ("ring", "stage", "staged", "arrived", "freed", "freed_by"))
    before = rounds * (NB // 2)

    def half_batch(batch, half, uses):
        if uses is not None:
            pool.wait_ge(arrived[half], uses * (16 * U))
            pool.wait_ge(freed[half], uses * freed_by)
        nc.gpsimd.tensor_copy(stage[:, half, :], index[:, bass.ds(batch * U, U)]).then_inc(staged, 1)
        pool.wait_ge(staged, 1)
        pool.sem_clear(staged)
        for u in range(U):
            nc.gpsimd.indirect_dma_start(
                out=ring[:, half, u, :], out_offset=None, in_=table,
                in_offset=bass.IndirectOffsetOnAxis(ap=stage[:, half, u:u + 1], axis=0)).then_inc(arrived[half], 16)

    half_batch(0, 0, before or None)
    half_batch(1, 1, before or None)
    with pool.Fori(1, NB // 2) as k:
        half_batch(k * 2, 0, k + before)
        half_batch(k * 2 + 1, 1, k + before)


def gather_buffers(nc, name, width, dt=F32, freed_by=1):
    return dict(ring=nc.alloc_sbuf_tensor(f"{name}_ring", [P, 2, U, width], dt),
                stage=nc.alloc_sbuf_tensor(f"{name}_stage", [P, 2, U], U32),
                staged=nc.alloc_semaphore(f"{name}_staged"),
                arrived=[nc.alloc_semaphore(f"{name}_arrived{i}") for i in range(2)],
                freed=[nc.alloc_semaphore(f"{name}_freed{i}") for i in range(2)], freed_by=freed_by)


def owner_scan(nc, link, net, values, out):
    J = values.shape[1]
    link(nc.vector.tensor_tensor(values, values, net.ends[:, :].unsqueeze(1).to_broadcast([P, J, T]), ALU.mult))
    for j in range(J):
        last = nc.vector.tensor_tensor_scan(out[:, j, ::-1], net.not_end[:, ::-1], values[:, j, ::-1], 0.0, ALU.mult, ALU.add)
    link(last)


def owner_carry(nc, link, net, carried, out):
    J = out.shape[1]
    link(nc.vector.tensor_copy(net.carry[:, 0:J], carried))
    for j in range(J):
        last = nc.vector.scalar_tensor_tensor(out=out[:, j, :], in0=net.last[:, :], scalar=net.carry[:, j:j + 1],
                                              in1=out[:, j, :], op0=ALU.mult, op1=ALU.add)
    link(last)


def fetch_columns(nc, pool, table, index, b, take, rounds=0):
    ring, stage, staged, arrived = (b[x] for x in ("ring", "stage", "staged", "arrived"))
    before = rounds * (NB // 2)

    def half_batch(batch, half, uses):
        if uses is not None:
            pool.wait_ge(arrived[half], uses * (16 * U))
            take(batch - 2, half)
        nc.gpsimd.tensor_copy(stage[:, half, :], index[:, bass.ds(batch * U, U)]).then_inc(staged, 1)
        pool.wait_ge(staged, 1)
        pool.sem_clear(staged)
        for u in range(U):
            nc.gpsimd.indirect_dma_start(
                out=ring[:, half, u, :], out_offset=None, in_=table,
                in_offset=bass.IndirectOffsetOnAxis(ap=stage[:, half, u:u + 1], axis=0)).then_inc(arrived[half], 16)

    half_batch(0, 0, None)
    half_batch(1, 1, None)
    with pool.Fori(1, NB // 2) as k:
        half_batch(k * 2, 0, k + before)
        half_batch(k * 2 + 1, 1, k + before)
    for half in range(2):
        pool.wait_ge(arrived[half], (before + NB // 2) * (16 * U))
        take(NB - 2 + half, half)


def phase_own_rows(nc, net):
    with nc.cleanup_on_exit():
        tmp, r = (nc.alloc_sbuf_tensor(n_, [P, 1, T], F32) for n_ in ("r_tmp", "r_found"))
        ps = nc.alloc_psum_tensor("rows_ps", [P, 512], F32)
        v_step, r_carried = nc.alloc_semaphore("rows_vector_step"), nc.alloc_semaphore("r_carried")
        with nc.Block("own_rows") as block:
            @block.vector
            def _(v):
                steps = [0]

                def link(ins):
                    steps[0] += 1
                    ins.then_inc(v_step, 1)
                    v.wait_ge(v_step, steps[0])
                link(nc.vector.tensor_scalar(tmp[:, 0, :], net.own_row[:, :], -float(N), None, ALU.add))
                owner_scan(nc, link, net, tmp[:, 0:1, :], r)
                net.r_step = steps[0]
                v.wait_ge(r_carried, 1)
                owner_carry(nc, link, net, ps[:, 0:1], r)
                link(nc.vector.tensor_copy(net.r[:, :], r[:, 0, :]))

            @block.tensor
            def _(pe):
                pe.wait_ge(v_step, net.r_step)
                nc.tensor.matmul(ps[:, 0:1], net.earlier[:, :], r[:, 0:1, 0], start=True, stop=True).then_inc(r_carried, 1)


def claim_rows(nc, pool, net, claimed, copied, places, values):
    def claim(batch, half, k):
        if k is not None:
            pool.wait_ge(claimed[half], k * (16 * U))
        nc.gpsimd.tensor_copy(places[:, half, :], net.own_idx[:, bass.ds(batch * U, U)])
        nc.gpsimd.tensor_copy(values[:, half, :], net.own_row[:, bass.ds(batch * U, U)]).then_inc(copied, 1)
        pool.wait_ge(copied, 1)
        pool.sem_clear(copied)
        for u in range(U):
            nc.gpsimd.indirect_dma_start(
                out=net.OWN, out_offset=bass.IndirectOffsetOnAxis(ap=places[:, half, u:u + 1], axis=0),
                in_=values[:, half, u:u + 1], in_offset=None, bounds_check=N, oob_is_err=False
            ).then_inc(claimed[half], 16)
    claim(0, 0, None)
    claim(1, 1, None)
    with pool.Fori(1, NB // 2) as k:
        claim(k * 2, 0, k)
        claim(k * 2 + 1, 1, k)
    for half in range(2):
        pool.wait_ge(claimed[half], NB // 2 * 16 * U)



def scatter_columns(nc, pool, table, b, places, values, bound):
    def half_batch(batch, half, uses):
        if uses is not None:
            pool.wait_ge(b["done"][half], uses * (16 * U))
        nc.gpsimd.tensor_copy(b["places"][:, half, :], places[:, bass.ds(batch * U, U)])
        nc.gpsimd.tensor_copy(b["values"][:, half, :, :], values[:, bass.ds(batch * U, U), :]).then_inc(b["copied"], 1)
        pool.wait_ge(b["copied"], 1)
        pool.sem_clear(b["copied"])
        for u in range(U):
            nc.gpsimd.indirect_dma_start(
                out=table, out_offset=bass.IndirectOffsetOnAxis(ap=b["places"][:, half, u:u + 1], axis=0),
                in_=b["values"][:, half, u, :], in_offset=None, bounds_check=bound, oob_is_err=False
            ).then_inc(b["done"][half], 16)
    half_batch(0, 0, None)
    half_batch(1, 1, None)
    with pool.Fori(1, NB // 2) as k:
        half_batch(k * 2, 0, k)
        half_batch(k * 2 + 1, 1, k)
    for half in range(2):
        pool.wait_ge(b["done"][half], NB // 2 * 16 * U)


def scatter_buffers(nc, name, width):
    return dict(places=nc.alloc_sbuf_tensor(f"{name}_places", [P, 2, U], U32),
                values=nc.alloc_sbuf_tensor(f"{name}_values", [P, 2, U, width], I32),
                copied=nc.alloc_semaphore(f"{name}_copied"),
                done=[nc.alloc_semaphore(f"{name}_done{i}") for i in range(2)])


def phase_digit(nc, net, name, digit_of, places, on_pool, on_sync=None):
    with nc.cleanup_on_exit():
        digits = nc.alloc_sbuf_tensor(f"{name}_digits", [P, T], F32)
        onehot = nc.alloc_sbuf_tensor(f"{name}_onehot", [P, U, R], BF16)
        seen = nc.alloc_sbuf_tensor(f"{name}_seen", [P, U + 1, R], BF16)
        totals = nc.alloc_sbuf_tensor(f"{name}_totals", [P, 2, R], F32)
        base = nc.alloc_sbuf_tensor(f"{name}_base_row", [P, 2, R], F32)
        picked = nc.alloc_sbuf_tensor(f"{name}_picked", [P, 2, R], F32)
        place = nc.alloc_sbuf_tensor(f"{name}_place", [P, U], F32)
        sums = [nc.alloc_psum_tensor(f"{name}_sums{i}", [P, 2, R], F32) for i in range(U // 2)]
        total_ps = nc.alloc_psum_tensor(f"{name}_total", [P, 512], F32)
        step = nc.alloc_semaphore(f"{name}_step")
        marks = nc.alloc_sbuf_tensor(f"{name}_marks", [P, 2, U, R], BF16)
        counted = [nc.alloc_semaphore(f"{name}_counted{i}") for i in range(2)]
        totalled = nc.alloc_semaphore(f"{name}_totalled")
        marked = nc.alloc_semaphore(f"{name}_marked")
        totals_marked = [nc.alloc_semaphore(f"{name}_totals_marked{i}") for i in range(2)]
        summed = [nc.alloc_semaphore(f"{name}_summed{i}") for i in range(U // 2)]
        taken = [nc.alloc_semaphore(f"{name}_taken{i}") for i in range(U // 2)]
        chain = nc.alloc_semaphore(f"{name}_chain")
        placed = nc.alloc_semaphore(f"{name}_placed")
        with nc.Block(name) as block:
            @block.vector
            def _(v):
                steps = [0]

                def link(ins):
                    steps[0] += 1
                    ins.then_inc(step, 1)
                    v.wait_ge(step, steps[0])

                def mark_columns(batch, last_add):
                    for u in range(U):
                        last = nc.vector.tensor_scalar(onehot[:, u, :], net.iota_r[:, :], digits[:, bass.ds(batch * U + u, 1)], None, ALU.is_equal)
                    last.then_inc(chain, 1)
                    v.wait_ge(chain, 1)
                    v.sem_clear(chain)
                    for u in range(U - 1):
                        nc.vector.tensor_tensor(seen[:, u + 1, :], seen[:, u, :], onehot[:, u, :], ALU.add).then_inc(chain, 1)
                        v.wait_ge(chain, 1)
                        v.sem_clear(chain)
                    nc.vector.tensor_tensor(seen[:, U, :], seen[:, U - 1, :], onehot[:, U - 1, :], ALU.add).then_inc(last_add, 1)
                    v.wait_ge(last_add, batch + 1)
                digit_of(nc, v, link, digits)
                link(nc.vector.memset(seen[:, :, :], 0.0))
                with v.Fori(0, NB // 2) as k:
                    for half in range(2):
                        v.wait_ge(counted[half], k + 1)
                        for u in range(U):
                            last = nc.vector.tensor_scalar(marks[:, half, u, :], net.iota_r[:, :],
                                                           digits[:, bass.ds((k * 2 + half) * U + u, 1)], None, ALU.is_equal)
                        last.then_inc(totals_marked[half], 1)
                v.wait_ge(totalled, 1)
                link(nc.vector.tensor_copy(totals[:, 0, :], total_ps[:, 0:R]))
                link(nc.vector.tensor_tensor(totals[:, 1, :], totals[:, 0, :], total_ps[:, R:2 * R], ALU.add))
                link(nc.vector.memset(base[:, 1, :], 1.0))
                link(nc.vector.tensor_tensor_scan(base[:, 0, :], base[:, 1, :], totals[:, 1, :], 0.0, ALU.mult, ALU.add))
                link(nc.vector.tensor_tensor(base[:, 0, :], base[:, 0, :], totals[:, 1, :], ALU.subtract))
                link(nc.vector.memset(seen[:, 0, :], 0.0))
                with v.Fori(0, NB) as batch:
                    mark_columns(batch, marked)
                    for i in range(U // 2):
                        v.wait_ge(summed[i], batch + 1)
                        nc.vector.tensor_tensor(picked[:, :, :], sums[i][:, :, :], base[:, 0:1, :].to_broadcast([P, 2, R]), ALU.add).then_inc(taken[i], 1)
                        v.wait_ge(taken[i], batch + 1)
                        nc.vector.tensor_tensor(picked[:, :, :], picked[:, :, :], onehot[:, 2 * i:2 * i + 2, :], ALU.mult).then_inc(chain, 1)
                        v.wait_ge(chain, 1)
                        v.sem_clear(chain)
                        nc.vector.tensor_reduce(place[:, 2 * i:2 * i + 2], picked[:, :, :], AX_X, ALU.add).then_inc(chain, 1)
                        v.wait_ge(chain, 1)
                        v.sem_clear(chain)
                    nc.vector.tensor_copy(places[:, bass.ds(batch * U, U)], place[:, :])
                    nc.vector.tensor_copy(seen[:, 0, :], seen[:, U, :]).then_inc(placed, 1)
                    v.wait_ge(placed, batch + 1)

            @block.tensor
            def _(pe):
                def count(half, first=False, final=False):
                    for i in range(U // 2):
                        last = nc.tensor.matmul(total_ps[:, :], net.ones_b[:, :], marks[:, half, 2 * i:2 * i + 2, :].rearrange("p a b -> p (a b)"),
                                                start=first and i == 0, stop=final and i == U // 2 - 1)
                    last.then_inc(counted[half], 1)
                for half in range(2):
                    pe.sem_inc(counted[half], 1)
                for half in range(2):
                    pe.wait_ge(totals_marked[half], 1)
                    count(half, first=half == 0)
                with pe.Fori(1, NB // 2 - 1) as k:
                    for half in range(2):
                        pe.wait_ge(totals_marked[half], k + 1)
                        count(half)
                for half in range(2):
                    pe.wait_ge(totals_marked[half], NB // 2)
                    count(half, final=half == 1)
                pe.wait_ge(counted[1], NB // 2 + 1)
                pe.sem_inc(totalled, 1)
                with pe.Fori(0, NB) as batch:
                    pe.wait_ge(marked, batch + 1)
                    for i in range(U // 2):
                        nc.tensor.matmul(sums[i][:, :, :].rearrange("p a b -> p (a b)"), net.above[:, :],
                                         onehot[:, 2 * i:2 * i + 2, :].rearrange("p a b -> p (a b)"), start=True, stop=False)
                        nc.tensor.matmul(sums[i][:, :, :].rearrange("p a b -> p (a b)"), net.ones_b[:, :],
                                         seen[:, 2 * i:2 * i + 2, :].rearrange("p a b -> p (a b)"), start=False, stop=True
                                         ).then_inc(summed[i], 1)

            @block.gpsimd
            def _(pool):
                on_pool(pool)

            if on_sync is not None:
                @block.sync
                def _(sp):
                    on_sync(sp)



def at_value(c, it, g):
    return it * c.per + (g % c.per + 1)


def groups_of(c, part):
    if isinstance(part, tuple):
        return part[0], range(part[1] * c.per, (part[1] + 1) * c.per)
    return part, range(G)


def flat(t):
    return t[:, :, :].rearrange("p j d -> p (j d)")


def blocks(ps):
    return ps[:, :].rearrange("p (j d) -> p j d", j=S)


class Pass:

    def __init__(self, nc, name, iters, step, unit, buffers, io, steps, norms=0, streams=1, gathered=()):
        self.nc, self.name, self.iters, self.step, self.unit = nc, name, iters, step, unit
        sem = lambda n_: nc.alloc_semaphore(f"{name}_{n_}")
        self.buf = {b: [nc.alloc_sbuf_tensor(f"{name}_{b}{g}", [P, S, width], F32) for g in range(G)] for b, width in buffers}
        self.io = {n_: [sem(f"{n_}{g}") for g in range(G)] for n_ in io}
        self.per = G // streams
        self.streams = streams
        self.gathered = gathered
        self.sem = {n_: [sem(f"{n_}{s_}") for s_ in range(streams)] for n_ in steps}
        self.psA = [nc.alloc_psum_tensor(f"{name}_psA{g}", [P, 512], F32) for g in range(G)]
        self.psB = [nc.alloc_psum_tensor(f"{name}_psB{g}", [P, 512], F32) for g in range(G)]
        if norms:
            self.stats = [nc.alloc_sbuf_tensor(f"{name}_stats{g}", [P, norms, S, 6], F32) for g in range(G)]
            self.mv = [nc.alloc_sbuf_tensor(f"{name}_mv{g}", [P, norms, S, 2], F32) for g in range(G)]
            self.std = [nc.alloc_sbuf_tensor(f"{name}_std{g}", [P, norms, S], F32) for g in range(G)]
            self.stat = [sem(f"stat{g}") for g in range(G)]
            self.aggregated, self.rooted, self.inverted = ([[sem(f"{w_}{i}_{s_}") for s_ in range(streams)] for i in range(norms)] for w_ in ("aggregated", "rooted", "inverted"))


def rows_at(c, table, it, g, base=0):
    if c.unit == "nodes":
        return table[bass.ds(it * c.step + (base + g * S * P), S * P), :].rearrange("(p j) d -> p j d", j=S)
    return table[base:base + EP, :].rearrange("(p t) d -> p t d", t=T)[:, bass.ds(column_of(c, it, g), S), :]


def column_of(c, it, g):
    return it * EDGE_STEP + g * S


def prime(c, sp, names):
    for n_ in names:
        for s_ in c.io[n_]:
            sp.sem_inc(s_, 16)


def load_rows(c, sp, name, dst, table, part, base=0):
    if part is None:
        return
    it, groups = groups_of(c, part)
    for g in groups:
        sp.dma_start(dst[g][:, :, :], rows_at(c, table, it, g, base)).then_inc(c.io[name][g], 16)


def reload_rows(c, sp, name, dst, table, part, freed, base=0, primed=0):
    if part is None:
        return
    it, groups = groups_of(c, part)
    for g in groups:
        rows = rows_at(c, table, it + 1, g, base)
        sp.wait_ge(c.sem[freed][g // c.per], at_value(c, it, g) + primed)
        sp.dma_start(dst[g][:, :, :], rows).then_inc(c.io[name][g], 16)


def store_rows(c, sp, name, table, src, part, ready, base=0, primed=0, noted=None):
    if part is None:
        return
    it, groups = groups_of(c, part)
    for g in groups:
        rows = rows_at(c, table, it, g, base)
        sp.wait_ge(c.sem[ready][g // c.per], at_value(c, it, g) + primed)
        if g == 0:
            for g2 in range(G):
                sp.wait_ge(c.io[name][g2], it * 16 + 16)
        if noted is not None:
            sp.sem_inc(noted, 1)
        sp.dma_start(rows, src[g][:, :, :]).then_inc(c.io[name][g], 16)


def settle(c, sp, names):
    for n_ in names:
        for s_ in c.io[n_]:
            sp.wait_ge(s_, 16 * c.iters + 16)


def loaded(c, engine, name, it, g):
    each = 16 * S if name in c.gathered else 16
    engine.wait_ge(c.io[name][g], it * each + each)


def stored(c, engine, name, it, g):
    loaded(c, engine, name, it, g)


def each_group(c, engine, part, waits, f, done):
    if part is None:
        return
    it, groups = groups_of(c, part)
    for g in groups:
        for w_ in waits:
            if w_ in c.io:
                loaded(c, engine, w_, it, g)
            else:
                engine.wait_ge(c.sem[w_][g // c.per], at_value(c, it, g))
        f(g).then_inc(c.sem[done][g // c.per], 1)


def take_statistics(c, v, part, i, rows, waits):
    if part is None:
        return
    it, groups = groups_of(c, part)
    nc = c.nc
    for g in groups:
        for w_ in waits:
            if w_ in c.io:
                loaded(c, v, w_, it, g)
            else:
                v.wait_ge(c.sem[w_][g // c.per], at_value(c, it, g))
        for j in range(S):
            last = nc.vector.bn_stats(c.stats[g][:, i, j, :], rows[g][:, j, :])
        last.then_inc(c.stat[g], 1)
    for g in groups:
        v.wait_ge(c.stat[g], 1)
        v.sem_clear(c.stat[g])
        for j in range(S):
            last = nc.vector.bn_aggr(c.mv[g][:, i, j, :], c.stats[g][:, i, j, :])
        last.then_inc(c.aggregated[i][g // c.per], 1)
    for g in groups:
        v.wait_ge(c.rooted[i][g // c.per], at_value(c, it, g))
        nc.vector.reciprocal(c.std[g][:, i, :], c.std[g][:, i, :]).then_inc(c.inverted[i][g // c.per], 1)


def take_root(c, act, net, part, i):
    if part is None:
        return
    it, groups = groups_of(c, part)
    for g in groups:
        act.wait_ge(c.aggregated[i][g // c.per], at_value(c, it, g))
        c.nc.scalar.activation(c.std[g][:, i, :], c.mv[g][:, i, :, 1], ACT.Sqrt, bias=net.eps[:, 0:1]).then_inc(c.rooted[i][g // c.per], 1)


def normalize(c, v, part, i, out, rows, done):
    if part is None:
        return
    it, groups = groups_of(c, part)
    for g in groups:
        v.wait_ge(c.inverted[i][g // c.per], at_value(c, it, g))
        for j in range(S):
            last = c.nc.vector.tensor_scalar(out[g][:, j, :], rows[g][:, j, :], c.mv[g][:, i, j, 0:1],
                                                c.std[g][:, i, j:j + 1], ALU.subtract, ALU.mult)
        last.then_inc(c.sem[done][g // c.per], 1)


def turn_group(c, net, src, ps, width=D):
    for j in range(S):
        last = c.nc.tensor.transpose(ps[0:width, j * P:(j + 1) * P], src[:, j, 0:width], net.ident[:, :])
    return last


def row_product(c, srcT, weight, ps, net=None, bias=None):
    if bias is not None:
        c.nc.tensor.matmul(ps[:, :], net.ones_b[:, :], net.parts[bias][:, :, :].rearrange("p j d -> p (j d)"), start=True, stop=False)
    for j in range(S):
        last = c.nc.tensor.matmul(ps[:, j * P:(j + 1) * P], srcT[:, j, :], weight, start=bias is None, stop=bias is None or j == S - 1)
    return last


def column_product(c, srcT, weight, ps):
    return c.nc.tensor.matmul(ps[:, :], weight, flat(srcT), start=True, stop=True)


def score_product(c, srcT, weight, ps):
    for j in range(S):
        last = c.nc.tensor.matmul(ps[:, j * 2 * H:(j + 1) * 2 * H], srcT[:, j, :], weight, start=True, stop=True)
    return last


def gat_rows_act(c, net, act, part, rows, done, waits, store):
    if part is None:
        return
    it, groups = groups_of(c, part)
    nc = c.nc
    for g in groups:
        stored(c, act, store, it, g)
        for w_ in waits:
            act.wait_ge(c.sem[w_][g // c.per], at_value(c, it, g))
        nc.scalar.activation(rows[g][:, :, 0:D], blocks(c.psB[g]), ACT.Copy)
        nc.scalar.activation(rows[g][:, :, D:WA], c.psA[g][:, 0:S * 2 * H].rearrange("p (j d) -> p j d", j=S), ACT.Copy
                             ).then_inc(c.sem[done][g // c.per], 1)


def scatter_stage(nc, c, name):
    return dict(places=nc.alloc_sbuf_tensor(f"{name}_places", [P, G, S], U32), copied=nc.alloc_semaphore(f"{name}_copied"),
                done=[nc.alloc_semaphore(f"{name}_done{g}") for g in range(G)], free=[nc.alloc_semaphore(f"{name}_free{s_}") for s_ in range(c.streams)])


def gather_stage(nc, name):
    return dict(places=nc.alloc_sbuf_tensor(f"{name}_places", [P, G, S], U32), copied=nc.alloc_semaphore(f"{name}_copied"))


def gather_rows(nc, pool, c, b, name, idx, table, rows, part=None, freed=None):
    it, groups = groups_of(c, part) if part is not None else (-1, range(G))
    for g in groups:
        if part is not None:
            pool.wait_ge(c.sem[freed][g // c.per], at_value(c, it, g))
        nc.gpsimd.tensor_copy(b["places"][:, g, :], idx[:, bass.ds(column_of(c, it + 1, g), S)]).then_inc(b["copied"], 1)
        pool.wait_ge(b["copied"], 1)
        pool.sem_clear(b["copied"])
        for j in range(S):
            nc.gpsimd.indirect_dma_start(
                out=rows[g][:, j, :], out_offset=None, in_=table,
                in_offset=bass.IndirectOffsetOnAxis(ap=b["places"][:, g, j:j + 1], axis=0)).then_inc(c.io[name][g], 16)


def scatter_rows(nc, pool, c, b, part, idx, out, rows, ready):
    if part is None:
        return
    it, groups = groups_of(c, part)
    for g in groups:
        pool.wait_ge(c.sem[ready][g // c.per], at_value(c, it, g) + c.per)
        nc.gpsimd.tensor_copy(b["places"][:, g, :], idx[:, bass.ds(column_of(c, it, g), S)]).then_inc(b["copied"], 1)
        pool.wait_ge(b["copied"], 1)
        pool.sem_clear(b["copied"])
        for j in range(S):
            nc.gpsimd.indirect_dma_start(
                out=out, out_offset=bass.IndirectOffsetOnAxis(ap=b["places"][:, g, j:j + 1], axis=0),
                in_=rows[g][:, j, :], in_offset=None, bounds_check=N - 1, oob_is_err=False).then_inc(b["done"][g], 16)
    for g in groups:
        pool.wait_ge(b["done"][g], it * (16 * S) + 16 * S)
        pool.sem_inc(b["free"][g // c.per], 1)



def layer_norm_affine(c, net, v, part):
    if part is None:
        return
    it, groups = groups_of(c, part)
    nc, f = c.nc, c.buf
    take_statistics(c, v, part, 3, f["h2"], ["y_made"])
    for g in groups:
        v.wait_ge(c.inverted[3][g // c.per], at_value(c, it, g))
        for j in range(S):
            last = nc.vector.scalar_tensor_tensor(out=f["h2"][g][:, j, :], in0=f["h2"][g][:, j, :], scalar=c.mv[g][:, 3, j, 0:1],
                                                  in1=net.w["gamma"][:, :], op0=ALU.subtract, op1=ALU.mult)
        last.then_inc(c.sem["yg_made"][g // c.per], 1)
    for g in groups:
        v.wait_ge(c.sem["yg_made"][g // c.per], at_value(c, it, g))
        v.wait_ge(c.sem["x2b_made"][g // c.per], at_value(c, it, g))
        for j in range(S):
            last = nc.vector.scalar_tensor_tensor(out=f["x2"][g][:, j, :], in0=f["h2"][g][:, j, :], scalar=c.std[g][:, 3, j:j + 1],
                                                  in1=f["x2"][g][:, j, :], op0=ALU.mult, op1=ALU.add)
        last.then_inc(c.sem["x3_made"][g // c.per], 1)


def staggered(c, engine, body):
    body(None, None, (0, 0))
    body((0, 0), None, (0, 1))
    with engine.Fori(0, c.iters - 1) as it:
        body((it, 1), (it, 0), (it + 1, 0))
        body((it + 1, 0), (it, 1), (it + 1, 1))
    body((c.iters - 1, 1), (c.iters - 1, 0), None)
    body(None, (c.iters - 1, 1), None)


def relu_step(c, act, part, waits, dst, src, done, **kw):
    each_group(c, act, part, waits, lambda g: c.nc.scalar.activation(flat(dst[g]), src(g), ACT.Relu, **kw), done)


def copy_step(c, act, part, waits, dst, src, done, **kw):
    each_group(c, act, part, waits, lambda g: c.nc.scalar.activation(flat(dst[g]), src(g), ACT.Copy, **kw), done)


def beta_step(c, net, v, part):
    if part is None:
        return
    it, groups = groups_of(c, part)
    for g in groups:
        v.wait_ge(c.io["XHX"][g], it * 16 + 32)
        v.wait_ge(c.sem["n2_made"][g // c.per], at_value(c, it, g))
        x2 = c.buf["x2"][g]
        c.nc.vector.tensor_tensor(x2[:, :, :], x2[:, :, :], slots(net.w["beta"]), ALU.add).then_inc(c.sem["x2b_made"][g // c.per], 1)


def update_step(c, v, part):
    each_group(c, v, part, ["upd_done"], lambda g: c.nc.vector.tensor_tensor(
        flat(c.buf["h2"][g]), c.psB[g][:, :], flat(c.buf["h2"][g]), ALU.add), "y_made")



def phase_nodes(nc, net, inp, out, name, first, iters, on_pool=None):
    w = net.w
    base = first * NODE_STEP
    with nc.cleanup_on_exit():
        c = Pass(nc, name, iters, NODE_STEP, "nodes",
                 [(n_, D) for n_ in ("x2", "n", "hT", "h2", "x0T", "o", "x", "h1")] + [("t1", WA), ("t2", WA)], ["x", "T1", "T2", "XHX", "out"],
                 ["n0_made", "h0_turned", "h0T_made", "xh1_done", "t1_made", "xh1_turned", "h1T_made", "xh2_done", "t2_made",
                  "x1_made", "n1_made", "h1_made", "x2_made", "n2_made", "x2b_made", "h2_made", "h2_turned", "h2T_made",
                  "u_done", "uT_made", "upd_done", "y_made", "yg_made", "x3_made", "n4_made", "h3_turned", "h3T_made",
                  "x0_done", "x0T_made", "c1_done", "g1_made", "c2_done", "g2_made", "c3_done", "x3T_made", "o_done", "o_made"],
                 norms=5, streams=2)
        f = c.buf
        with nc.Block(name) as block:
            @block.sync
            def _(sp):
                prime(c, sp, ["T1", "T2", "XHX", "out"])
                load_rows(c, sp, "x", f["x"], inp["x"], 0, base)

                def half(front, back, reload=()):
                    for part in reload:
                        reload_rows(c, sp, "x", f["x"], inp["x"], part, "x1_made", base=base)
                    store_rows(c, sp, "T1", net.T1, f["t1"], front, "t1_made", base=base)
                    store_rows(c, sp, "T2", net.T2, f["t2"], front, "t2_made", base=base)
                    store_rows(c, sp, "XHX", net.XHX, f["x2"], front, "x2_made", base=base)
                    store_rows(c, sp, "out", out, f["o"], back, "o_made", base=base, primed=c.per)
                half((0, 0), None)
                with sp.Fori(0, c.iters - 1) as it:
                    half((it, 1), (it, 0), [(it, 0)])
                    half((it + 1, 0), (it, 1), [(it, 1)])
                half((c.iters - 1, 1), (c.iters - 1, 0))
                half(None, (c.iters - 1, 1))
                settle(c, sp, ["T1", "T2", "XHX", "out"])

            @block.vector
            def _(v):
                def gcn_input(part, i, ps):
                    each_group(c, v, part, [f"c{i}_done"], lambda g: nc.vector.scalar_tensor_tensor(
                        out=flat(f["hT"][g]), in0=ps[g][:, :], scalar=0.0, in1=flat(f["x0T"][g]), op0=ALU.max, op1=ALU.add), f"g{i}_made")

                def half(front, back, coming=None):
                    beta_step(c, net, v, back)
                    update_step(c, v, back)
                    layer_norm_affine(c, net, v, back)
                    each_group(c, v, front, ["t2_made"], lambda g: nc.vector.tensor_tensor(
                        f["x2"][g][:, :, :], f["t2"][g][:, :, 0:D], f["x"][g][:, :, :], ALU.add), "x1_made")
                    take_statistics(c, v, back, 4, f["x2"], ["x3_made"])
                    normalize(c, v, back, 4, f["n"], f["x2"], "n4_made")
                    take_statistics(c, v, front, 1, f["x2"], ["x1_made"])
                    normalize(c, v, front, 1, f["n"], f["x2"], "n1_made")
                    each_group(c, v, front, ["h1_made"], lambda g: nc.vector.tensor_tensor(
                        flat(f["x2"][g]), flat(f["x2"][g]), flat(f["h1"][g]), ALU.add), "x2_made")
                    gcn_input(back, 1, c.psA)
                    take_statistics(c, v, front, 2, f["x2"], ["x2_made"])
                    normalize(c, v, front, 2, f["n"], f["x2"], "n2_made")
                    gcn_input(back, 2, c.psB)
                    take_statistics(c, v, coming, 0, f["x"], ["x"])
                    normalize(c, v, coming, 0, f["n"], f["x"], "n0_made")
                    each_group(c, v, back, ["out", "o_done"], lambda g: nc.vector.tensor_tensor(
                        flat(f["o"][g]), c.psB[g][:, :], flat(f["x2"][g]), ALU.add), "o_made")
                staggered(c, v, half)

            @block.scalar
            def _(act):
                psA, psB = (lambda g: c.psA[g][:, :]), (lambda g: c.psB[g][:, :])

                normed = lambda g: flat(f["n"][g])

                def half(front, back, coming=None):
                    relu_step(c, act, front, ["h0_turned"], f["hT"], psA, "h0T_made")
                    take_root(c, act, net, back, 3)
                    gat_rows_act(c, net, act, front, f["t1"], "t1_made", ["xh1_done"], "T1")
                    relu_step(c, act, front, ["xh1_turned"], f["hT"], psA, "h1T_made", bias=w["b1"][:, 0:1])
                    gat_rows_act(c, net, act, front, f["t2"], "t2_made", ["xh2_done"], "T2")
                    take_root(c, act, net, back, 4)
                    take_root(c, act, net, front, 1)
                    relu_step(c, act, back, ["h3_turned"], f["hT"], psA, "h3T_made")
                    relu_step(c, act, front, ["n1_made"], f["h1"], normed, "h1_made")
                    relu_step(c, act, back, ["x0_done"], f["x0T"], psB, "x0T_made", bias=w["fc1_b"][:, 0:1], scale=1.0 / X0_SCALE)
                    take_root(c, act, net, front, 2)
                    relu_step(c, act, front, ["n2_made"], f["h2"], normed, "h2_made")
                    take_root(c, act, net, coming, 0)
                    relu_step(c, act, back, ["c3_done"], f["hT"], psA, "x3T_made")
                    copy_step(c, act, front, ["h2_turned"], f["hT"], psA, "h2T_made")
                    relu_step(c, act, front, ["u_done"], f["hT"], psA, "uT_made", bias=w["bu1"][:, 0:1])
                staggered(c, act, half)

            @block.tensor
            def _(pe):
                def project(g, weight, bias=None):
                    row_product(c, f["hT"][g], weight[:, 0:D], c.psB[g], net, bias)
                    return score_product(c, f["hT"][g], weight[:, D:WA], c.psA[g])

                def first_projection(part):
                    if part is None:
                        return
                    it, groups = groups_of(c, part)
                    for g in groups:
                        pe.wait_ge(c.sem["o_made"][g // c.per], at_value(c, it, g))
                        pe.wait_ge(c.sem["h0T_made"][g // c.per], at_value(c, it, g))
                        project(g, w["W1"]).then_inc(c.sem["xh1_done"][g // c.per], 1)

                def half(front, back, coming=None):
                    each_group(c, pe, front, ["n0_made"], lambda g: turn_group(c, net, f["n"][g], c.psA[g]), "h0_turned")
                    each_group(c, pe, back, ["uT_made"], lambda g: row_product(c, f["hT"][g], w["Wu2"][:, :], c.psB[g], net, "bu2"), "upd_done")
                    first_projection(front)
                    each_group(c, pe, front, ["t1_made"], lambda g: turn_group(c, net, f["t1"][g], c.psA[g]), "xh1_turned")
                    each_group(c, pe, front, ["h1T_made"], lambda g: project(g, w["W2"], "b2"), "xh2_done")
                    each_group(c, pe, back, ["n4_made"], lambda g: turn_group(c, net, f["n"][g], c.psA[g]), "h3_turned")
                    each_group(c, pe, back, ["h3T_made"], lambda g: column_product(c, f["hT"][g], w["fc1"][:, :], c.psB[g]), "x0_done")
                    each_group(c, pe, back, ["x0T_made"], lambda g: column_product(c, f["x0T"][g], w["conv_lone"][:, :], c.psA[g]), "c1_done")
                    each_group(c, pe, back, ["g1_made"], lambda g: column_product(c, f["hT"][g], w["conv1"][:, :], c.psB[g]), "c2_done")
                    each_group(c, pe, front, ["h2_made"], lambda g: turn_group(c, net, f["h2"][g], c.psA[g]), "h2_turned")
                    each_group(c, pe, back, ["g2_made"], lambda g: column_product(c, f["hT"][g], w["conv2"][:, :], c.psA[g]), "c3_done")
                    each_group(c, pe, front, ["h2T_made"], lambda g: column_product(c, f["hT"][g], w["Wu1a"][:, :], c.psA[g]), "u_done")
                    each_group(c, pe, back, ["x3T_made"], lambda g: row_product(c, f["hT"][g], w["fc2"][:, :], c.psB[g], net, "fc2_b"), "o_done")
                for s_ in c.sem["o_made"]:
                    pe.sem_inc(s_, c.per)
                staggered(c, pe, half)

            if on_pool is not None:
                @block.gpsimd
                def _(pool):
                    on_pool(pool)


def phase_index(nc, net, inp, out):
    s_ = net.S
    half_rows = T // 2
    with nc.cleanup_on_exit():
        sb = lambda name, shape, dt=F32: nc.alloc_sbuf_tensor(name, shape, dt)
        item = sb("sort_items", [P, T, 2], I32)
        key = sb("sort_key", [P, T])
        low = sb("sort_low", [P, T], I32)
        places = sb("sort_places", [P, T], I32)
        packed, tmp = sb("packed", [P, T, 5]), sb("so_tmp", [P, 3, T])
        ordered = sb("ordered", [P, 5, T])
        got = sb("own_src_got", [P, 3, T], I32)
        own_idx, own_val, dst_s = sb("own_src_idx", [P, T], I32), sb("own_src_val", [P, T, 1], I32), sb("dst_s", [P, T], I32)

        def low_digit(nc, v, link, digits):
            link(nc.vector.tensor_scalar(key[:, :], net.dst[:, :], float(N), float(N), ALU.is_equal, ALU.mult))
            link(nc.vector.tensor_tensor(key[:, :], key[:, :], net.src[:, :], ALU.add))
            link(nc.vector.tensor_copy(item[:, :, 0], key[:, :]))
            link(nc.vector.tensor_scalar(item[:, :, 1], net.own_row[:, :], -float(N), None, ALU.add))
            link(nc.vector.tensor_scalar(low[:, :], item[:, :, 0], R - 1, None, ALU.bitwise_and))
            link(nc.vector.tensor_copy(digits[:, :], low[:, :]))


        with nc.cleanup_on_exit():
            values = nc.alloc_sbuf_tensor("own_values", [P, 2, U], I32)
            claim_places = nc.alloc_sbuf_tensor("own_places", [P, 2, U], U32)
            copied = nc.alloc_semaphore("own_copied")
            claimed = [nc.alloc_semaphore(f"own_claimed{i}") for i in range(2)]
            qb = gather_buffers(nc, "q", 1, I32)

            def own_and_q(pool):
                claim_rows(nc, pool, net, claimed, copied, claim_places, values)
                fetch_columns(nc, pool, net.OWN, net.src, qb, lambda batch, half: nc.gpsimd.tensor_copy(
                    net.q[:, bass.ds(batch * U, U)], qb["ring"][:, half, :, 0]))
            phase_digit(nc, net, "low_digit", low_digit, places, own_and_q)

        with nc.cleanup_on_exit():
            b1 = scatter_buffers(nc, "low_items", 2)
            phase_nodes(nc, net, inp, out, "nodes_a", 0, NODE_SPLIT[0],
                        lambda pool: scatter_columns(nc, pool, net.J1, b1, places, item, EP - 1))

        with nc.cleanup_on_exit():
            back = nc.alloc_sbuf_tensor("sort_back", [half_rows, 2, P, 2], I32)
            back_f = nc.alloc_sbuf_tensor("sort_back_f", [half_rows, 2, 2, P], F32)
            ps = nc.alloc_psum_tensor("sort_turn", [P, 512], F32)
            loaded, split, turned, step = (nc.alloc_semaphore(f"sort_{x}") for x in ("loaded", "split", "turned", "step"))
            with nc.Block("turn") as block:
                @block.sync
                def _(sp):
                    sp.dma_start(back[:, :, :, :], net.J1.rearrange("(h t p) k -> t h p k", h=2, p=P)).then_inc(loaded, 16)

                @block.vector
                def _(v):
                    v.wait_ge(loaded, 16)
                    nc.vector.tensor_copy(back_f[:, :, :, :], back[:, :, :, :].rearrange("t h p k -> t h k p")).then_inc(split, 1)
                    v.wait_ge(turned, 1)
                    for h in range(2):
                        for k in range(2):
                            at = (h * 2 + k) * half_rows
                            last = nc.vector.tensor_copy(item[:, h * half_rows:(h + 1) * half_rows, k], ps[:, at:at + half_rows])
                    last.then_inc(step, 1)
                    v.wait_ge(step, 1)
                    steps = [1]

                    def link(ins):
                        steps[0] += 1
                        ins.then_inc(step, 1)
                        v.wait_ge(step, steps[0])
                    link(nc.vector.tensor_scalar(tmp[:, 0, :], net.dst[:, :], float(N), float(N), ALU.is_equal, ALU.mult))
                    link(nc.vector.tensor_tensor(packed[:, :, 0], tmp[:, 0, :], net.src[:, :], ALU.add))
                    nc.vector.tensor_copy(packed[:, :, 1], net.ew[:, :])
                    nc.vector.tensor_copy(packed[:, :, 2], net.r[:, :])
                    link(nc.vector.tensor_copy(packed[:, :, 3], net.q[:, :]))
                    link(nc.vector.tensor_copy(packed[:, :, 4], net.dst_idx[:, :]))

                @block.tensor
                def _(pe):
                    pe.wait_ge(split, 1)
                    for h in range(2):
                        for k in range(2):
                            at = (h * 2 + k) * half_rows
                            last = nc.tensor.transpose(ps[:, at:at + half_rows], back_f[:, h, k, :], net.ident[0:half_rows, 0:half_rows])
                    last.then_inc(turned, 1)


        def high_digit(nc, v, link, digits):
            link(nc.vector.tensor_scalar(low[:, :], item[:, :, 0], 8, None, ALU.logical_shift_right))
            link(nc.vector.tensor_copy(digits[:, :], low[:, :]))

        with nc.cleanup_on_exit():
            xb = gather_buffers(nc, "xd", D, freed_by=16)
            xd = net.XD.rearrange("(p t) d -> p t d", t=T)

            def store_xd(sp):
                with sp.Fori(0, NB // 2) as k:
                    for half in range(2):
                        sp.wait_ge(xb["arrived"][half], k * (16 * U) + 16 * U)
                        sp.dma_start(xd[:, bass.ds((k * 2 + half) * U, U), :], xb["ring"][:, half, :, :]).then_inc(xb["freed"][half], 16)
                for half in range(2):
                    sp.wait_ge(xb["freed"][half], NB // 2 * 16)
            phase_digit(nc, net, "high_digit", high_digit, places,
                        lambda pool: gather_columns(nc, pool, inp["x"], net.dst_idx, xb), store_xd)

        with nc.cleanup_on_exit():
            b2 = scatter_buffers(nc, "high_items", 2)
            pb = gather_buffers(nc, "packed", 5)
            perm2 = sb("perm2", [P, T, 2], I32)
            perm = sb("perm", [P, T], I32)
            stored, loaded_ = nc.alloc_semaphore("packed_stored"), nc.alloc_semaphore("perm_loaded")

            def order_edges(pool):
                pool.dma_start(net.PACK.rearrange("(p t) k -> p t k", t=T), packed[:, :, :]).then_inc(stored, 16)
                scatter_columns(nc, pool, net.J2, b2, places, item, EP - 1)
                pool.dma_start(perm2[:, :, :], net.J2.rearrange("(p t) k -> p t k", t=T)).then_inc(loaded_, 16)
                pool.wait_ge(stored, 16)
                pool.wait_ge(loaded_, 16)
                nc.gpsimd.tensor_copy(perm[:, :], perm2[:, :, 1]).then_inc(pb["staged"], 1)
                pool.wait_ge(pb["staged"], 1)
                pool.sem_clear(pb["staged"])
                fetch_columns(nc, pool, net.PACK, perm, pb, lambda batch, half: nc.gpsimd.tensor_copy(
                    ordered[:, :, bass.ds(batch * U, U)], pb["ring"][:, half, :, :].rearrange("p t k -> p k t")))
            phase_nodes(nc, net, inp, out, "nodes_b", NODE_SPLIT[0], NODE_SPLIT[1], order_edges)

        with nc.cleanup_on_exit():
            nxt = nc.alloc_sbuf_tensor("next_src", [P, 1], F32)
            diag = nc.alloc_sbuf_tensor("so_diag", [P, P], F32)
            ps = [nc.alloc_psum_tensor(f"so_ps{i}", [P, 512], F32) for i in range(2)]
            v_step, turned = nc.alloc_semaphore("so_v_step"), nc.alloc_semaphore("so_turned")
            with nc.Block("source_segments") as block:
                @block.vector
                def _(v):
                    steps = [0]

                    def link(ins):
                        steps[0] += 1
                        ins.then_inc(v_step, 1)
                        v.wait_ge(v_step, steps[0])
                    key = ordered[:, 0, :]
                    nc.vector.tensor_copy(s_.ew[:, :], ordered[:, 1, :])
                    nc.vector.tensor_copy(s_.r[:, :], ordered[:, 2, :])
                    nc.vector.tensor_copy(s_.q[:, :], ordered[:, 3, :])
                    nc.vector.tensor_copy(dst_s[:, :], ordered[:, 4, :])
                    nc.vector.memset(s_.cont[:, 0:1], 0.0)
                    nc.vector.tensor_tensor(s_.cont[:, 1:T], key[:, 1:T], key[:, 0:T - 1], ALU.is_equal)
                    nc.vector.tensor_tensor(tmp[:, 0, 0:T - 1], key[:, 1:T], key[:, 0:T - 1], ALU.not_equal)
                    nc.vector.tensor_scalar(s_.first[:, :], key, key[:, 0:1], None, ALU.is_equal)
                    link(nc.vector.tensor_scalar(diag[:, :], net.ident[:, :], key[:, 0:1], None, ALU.mult))
                    net.so_step = steps[0]
                    v.wait_ge(turned, 1)
                    nc.vector.tensor_copy(nxt[:, :], ps[0][:, 0:1])
                    link(nc.vector.tensor_scalar(s_.later[:, :], ps[1][:, 0:P], key[:, T - 1:T], None, ALU.is_equal))
                    nc.vector.tensor_tensor(tmp[:, 0, T - 1:T], key[:, T - 1:T], nxt[:, :], ALU.not_equal)
                    link(nc.vector.tensor_tensor(s_.later[:, :], s_.later[:, :], net.upper[:, :], ALU.mult))
                    end_of_first(nc, link, net, s_, tmp[:, 2, :])
                    link(nc.vector.tensor_scalar(tmp[:, 1, :], key, -float(SKIP), None, ALU.add))
                    link(nc.vector.tensor_tensor(tmp[:, 1, :], tmp[:, 1, :], tmp[:, 0, :], ALU.mult))
                    nc.vector.tensor_scalar(own_idx[:, :], tmp[:, 1, :], float(SKIP), None, ALU.add)
                    nc.vector.tensor_scalar(s_.own_idx[:, :], tmp[:, 1, :], float(SKIP), None, ALU.add)
                    link(nc.vector.tensor_scalar(own_val[:, :, 0], net.own_row[:, :], -float(N), None, ALU.add))

                @block.tensor
                def _(pe):
                    pe.wait_ge(v_step, net.so_step)
                    nc.tensor.matmul(ps[0][:, 0:1], net.shift[:, :], ordered[:, 0, 0:1], start=True, stop=True)
                    nc.tensor.matmul(ps[1][:, 0:P], net.ones[:, :], diag[:, :], start=True, stop=True).then_inc(turned, 1)


        with nc.cleanup_on_exit():
            sb_ = scatter_buffers(nc, "own_src", 1)
            ob = gather_buffers(nc, "own_src", 1, I32)
            none = nc.alloc_sbuf_tensor("no_row", [125, N // 125], I32)
            based = nc.alloc_semaphore("own_src_based")

            def source_rows_of(pool):
                nc.gpsimd.memset(none[:, :], EP).then_inc(ob["staged"], 1)
                pool.wait_ge(ob["staged"], 1)
                pool.sem_clear(ob["staged"])
                pool.dma_start(net.OWNS[0:N, :].rearrange("(p j) k -> p (j k)", p=125), none[:, :]).then_inc(based, 16)
                pool.wait_ge(based, 16)
                scatter_columns(nc, pool, net.OWNS, sb_, own_idx, own_val, N)
                for i, index in enumerate((dst_s, net.src, net.dst_idx)):
                    fetch_columns(nc, pool, net.OWNS, index, ob, lambda batch, half, i=i: nc.gpsimd.tensor_copy(
                        got[:, i, bass.ds(batch * U, U)], ob["ring"][:, half, :, 0]), i)
            phase_nodes(nc, net, inp, out, "nodes_c", sum(NODE_SPLIT[0:2]), NODE_SPLIT[2], source_rows_of)

        with nc.cleanup_on_exit():
            v_step = nc.alloc_semaphore("homes_step")
            with nc.Block("homes") as block:
                @block.vector
                def _(v):
                    steps = [0]

                    def link(ins):
                        steps[0] += 1
                        ins.then_inc(v_step, 1)
                        v.wait_ge(v_step, steps[0])
                    nc.vector.tensor_copy(s_.s[:, :], got[:, 0, :])
                    link(nc.vector.tensor_scalar(got[:, 1, :], got[:, 1, :], float(EP - 1), None, ALU.min))
                    nc.vector.tensor_copy(net.s[:, :], got[:, 1, :])
                    link(nc.vector.tensor_scalar(tmp[:, 0, :], got[:, 2, :], float(EP), None, ALU.is_lt))
                    link(nc.vector.tensor_tensor(tmp[:, 1, :], got[:, 2, :], net.r[:, :], ALU.subtract))
                    link(nc.vector.tensor_scalar(tmp[:, 1, :], tmp[:, 1, :], float(EP), None, ALU.add))
                    link(nc.vector.tensor_tensor(tmp[:, 1, :], tmp[:, 1, :], tmp[:, 0, :], ALU.mult))
                    link(nc.vector.tensor_tensor(tmp[:, 1, :], tmp[:, 1, :], net.r[:, :], ALU.add))
                    link(nc.vector.tensor_scalar(net.home2[:, :], tmp[:, 1, :], float(N), None, ALU.add))
                    link(nc.vector.tensor_scalar(tmp[:, 0, :], net.q[:, :], float(N), None, ALU.is_ge))
                    link(nc.vector.tensor_tensor(tmp[:, 1, :], net.q[:, :], got[:, 1, :], ALU.subtract))
                    link(nc.vector.tensor_scalar(tmp[:, 1, :], tmp[:, 1, :], -float(N + EP), None, ALU.add))
                    link(nc.vector.tensor_tensor(tmp[:, 1, :], tmp[:, 1, :], tmp[:, 0, :], ALU.mult))
                    link(nc.vector.tensor_tensor(tmp[:, 1, :], tmp[:, 1, :], got[:, 1, :], ALU.add))
                    link(nc.vector.tensor_scalar(net.home3[:, :], tmp[:, 1, :], float(EP), None, ALU.add))


    phase_nodes(nc, net, inp, out, "nodes_d", sum(NODE_SPLIT[0:3]), NODE_ITERS - sum(NODE_SPLIT[0:3]))


NODE_SPLIT = (2, 4, 9)



def fix_first_ends(nc, name, out, width):
    return dict(row=nc.alloc_sbuf_tensor(f"{name}_fix_row", [P, width], F32), at=nc.alloc_sbuf_tensor(f"{name}_fix_at", [P, 1], U32),
                carried=nc.alloc_semaphore(f"{name}_carried"), fetched=nc.alloc_semaphore(f"{name}_fix_fetched"),
                added=nc.alloc_semaphore(f"{name}_fix_added"), placed=nc.alloc_semaphore(f"{name}_fix_placed"),
                copied=nc.alloc_semaphore(f"{name}_fix_copied"))


def fix_pool(nc, pool, fix, out, order):
    nc.gpsimd.tensor_copy(fix["at"][:, :], order.first_end[:, :]).then_inc(fix["copied"], 1)
    pool.wait_ge(fix["copied"], 1)
    nc.gpsimd.indirect_dma_start(out=fix["row"][:, :], out_offset=None, in_=out,
                                 in_offset=bass.IndirectOffsetOnAxis(ap=fix["at"][:, 0:1], axis=0)).then_inc(fix["fetched"], 16)
    pool.wait_ge(fix["added"], 1)
    nc.gpsimd.indirect_dma_start(out=out, out_offset=bass.IndirectOffsetOnAxis(ap=fix["at"][:, 0:1], axis=0),
                                 in_=fix["row"][:, :], in_offset=None).then_inc(fix["placed"], 16)
    pool.wait_ge(fix["placed"], 16)


def fix_vector(nc, v, fix, ps, width):
    v.wait_ge(fix["fetched"], 16)
    v.wait_ge(fix["carried"], 1)
    nc.vector.tensor_tensor(fix["row"][:, :], fix["row"][:, :], ps[:, 0:width], ALU.add).then_inc(fix["added"], 1)


def phase_sum(nc, net, name, table, index, order, out, weight=None, relu_with=None):
    with nc.cleanup_on_exit():
        b = gather_buffers(nc, name, D)
        acc = nc.alloc_sbuf_tensor(f"{name}_acc", [P, 2, U, D], F32)
        other = nc.alloc_sbuf_tensor(f"{name}_other", [P, 2, U, D], F32) if relu_with is not None else None
        ps = nc.alloc_psum_tensor(f"{name}_ps", [P, 512], F32)
        chain, cleared = (nc.alloc_semaphore(f"{name}_{x}") for x in ("chain", "cleared"))
        summed, stored, loaded, used = ([nc.alloc_semaphore(f"{name}_{x}{i}") for i in range(2)] for x in ("summed", "stored", "loaded", "used"))
        fix = fix_first_ends(nc, name, out, D)
        view = out[0:EP, :].rearrange("(p t) d -> p t d", t=T)
        with nc.Block(name) as block:
            @block.gpsimd
            def _(pool):
                gather_columns(nc, pool, table, index, b)
                for half in range(2):
                    pool.wait_ge(stored[half], NB // 2 * 16 + 16)
                fix_pool(nc, pool, fix, out, order)

            @block.sync
            def _(sp):
                for half in range(2):
                    sp.sem_inc(stored[half], 16)
                with sp.Fori(0, NB // 2) as k:
                    for half in range(2):
                        sp.wait_ge(summed[half], k + 1)
                        sp.dma_start(view[:, bass.ds((k * 2 + half) * U, U), :], acc[:, half, :, :]).then_inc(stored[half], 16)
                for half in range(2):
                    sp.wait_ge(stored[half], NB // 2 * 16 + 16)

            if relu_with is not None:
                source = relu_with.rearrange("(p t) d -> p t d", t=T)

                @block.scalar
                def _(act):
                    for half in range(2):
                        act.dma_start(other[:, half, :, :], source[:, half * U:(half + 1) * U, :]).then_inc(loaded[half], 16)
                    with act.Fori(1, NB // 2) as k:
                        for half in range(2):
                            act.wait_ge(used[half], k)
                            act.dma_start(other[:, half, :, :], source[:, bass.ds((k * 2 + half) * U, U), :]).then_inc(loaded[half], 16)

            @block.vector
            def _(v):
                def chained(ins):
                    ins.then_inc(chain, 1)
                    v.wait_ge(chain, 1)
                    v.sem_clear(chain)
                chained(nc.vector.memset(acc[:, 1, U - 1, :], 0.0))
                with v.Fori(0, NB // 2) as k:
                    for half in range(2):
                        got = b["ring"][:, half, :, :]
                        v.wait_ge(b["arrived"][half], k * (16 * U) + 16 * U)
                        if relu_with is not None:
                            v.wait_ge(loaded[half], k * 16 + 16)
                            nc.vector.tensor_tensor(got, got, other[:, half, :, :], ALU.add).then_inc(used[half], 1)
                            v.wait_ge(used[half], k + 1)
                            chained(nc.vector.tensor_scalar(got, got, 0.0, None, ALU.max))
                        if weight is not None:
                            chained(nc.vector.tensor_tensor(got, got, weight[:, bass.ds((k * 2 + half) * U, U)].unsqueeze(2).to_broadcast([P, U, D]), ALU.mult))
                        v.wait_ge(stored[half], k * 16 + 16)
                        for u in range(U):
                            before = acc[:, half, u - 1, :] if u else acc[:, 1 - half, U - 1, :]
                            ins = nc.vector.scalar_tensor_tensor(out=acc[:, half, u, :], in0=before, scalar=order.cont[:, bass.ds((k * 2 + half) * U + u, 1)],
                                                                 in1=b["ring"][:, half, u, :], op0=ALU.mult, op1=ALU.add)
                            if u < U - 1:
                                chained(ins)
                        ins.then_inc(b["freed"][half], 1)
                        v.wait_ge(b["freed"][half], k + 1)
                        v.sem_inc(summed[half], 1)
                fix_vector(nc, v, fix, ps, D)

            @block.tensor
            def _(pe):
                pe.wait_ge(summed[1], NB // 2)
                nc.tensor.matmul(ps[:, 0:D], order.later[:, :], acc[:, 1, U - 1, :], start=True, stop=True).then_inc(fix["carried"], 1)



def phase_gat(nc, net, layer):
    with nc.cleanup_on_exit():
        Y = nc.alloc_sbuf_tensor(f"gat{layer + 1}_rows", [P, T, D + H], F32)
        if layer == 0:
            phase_own_projection(nc, net, Y)
        phase_attend(nc, net, layer, Y)


def phase_own_projection(nc, net, Y):
    w = net.w
    with nc.cleanup_on_exit():
        b = gather_buffers(nc, "gat1", WA)
        c = Pass(nc, "own_projection", EDGE_ITERS, EDGE_STEP, "edges", [("x", D), ("hT", D), ("t1", WA)], ["x", "AD1"],
                 ["n0_made", "turned", "h0T_made", "xh1_done", "t1_made", "ad_made"], norms=1)
        f = c.buf
        with nc.Block("own_projection") as block:
            @block.gpsimd
            def _(pool):
                fetch_columns(nc, pool, net.T1, net.src, b, lambda batch, half: nc.gpsimd.tensor_copy(
                    Y[:, bass.ds(batch * U, U), :], b["ring"][:, half, :, 0:D + H]))

            @block.sync
            def _(sp):
                prime(c, sp, ["AD1"])
                load_rows(c, sp, "x", f["x"], net.XD, 0)

                def iteration(it, more):
                    if more:
                        reload_rows(c, sp, "x", f["x"], net.XD, it, "turned")
                    store_rows(c, sp, "AD1", net.AD1, f["t1"], it, "t1_made")
                with sp.Fori(0, c.iters - 1) as it:
                    iteration(it, True)
                iteration(c.iters - 1, False)
                settle(c, sp, ["AD1"])

            @block.vector
            def _(v):
                with v.Fori(0, c.iters) as it:
                    take_statistics(c, v, it, 0, f["x"], ["x"])
                    normalize(c, v, it, 0, f["x"], f["x"], "n0_made")

            @block.scalar
            def _(act):
                with act.Fori(0, c.iters) as it:
                    take_root(c, act, net, it, 0)
                    relu_step(c, act, it, ["turned"], f["hT"], lambda g: c.psA[g][:, :], "h0T_made")
                    gat_rows_act(c, net, act, it, f["t1"], "t1_made", ["xh1_done"], "AD1")
                    each_group(c, act, it, [], lambda g: nc.scalar.activation(
                        net.ad[:, :, bass.ds(column_of(c, it, g), S)], c.psA[g][:, 0:S * 2 * H].rearrange("p (j k) -> p k j", j=S), ACT.Copy), "ad_made")

            @block.tensor
            def _(pe):
                for s_ in c.sem["ad_made"]:
                    pe.sem_inc(s_, c.per)
                with pe.Fori(0, c.iters) as it:
                    each_group(c, pe, it, ["ad_made", "n0_made"], lambda g: turn_group(c, net, f["x"][g], c.psA[g]), "turned")
                    for g in range(G):
                        pe.wait_ge(c.sem["h0T_made"][g // c.per], at_value(c, it, g))
                        row_product(c, f["hT"][g], w["W1"][:, 0:D], c.psB[g])
                        score_product(c, f["hT"][g], w["W1"][:, D:WA], c.psA[g]).then_inc(c.sem["xh1_done"][g // c.per], 1)


def phase_attend(nc, net, layer, Y):
    name = f"gat{layer + 1}"
    W_ = D + H
    with nc.cleanup_on_exit():
        b = gather_buffers(nc, name, WA) if layer == 1 else None
        alpha, of_owner, m = (nc.alloc_sbuf_tensor(f"{name}_{x}", [P, H, T], F32) for x in ("alpha", "of_owner", "max"))
        own, mask = nc.alloc_sbuf_tensor(f"{name}_own", [P, H, T], F32), nc.alloc_sbuf_tensor(f"{name}_mask", [P, T], F32)
        diag = nc.alloc_sbuf_tensor(f"{name}_diag", [P, H, P], F32)
        cm = nc.alloc_sbuf_tensor(f"{name}_carried_max", [P, H], F32)
        ps = [nc.alloc_psum_tensor(f"{name}_ps{i}", [P, 512], F32) for i in range(4)]
        step, t_step, a_step, out_done, scored = (nc.alloc_semaphore(f"{name}_{x}") for x in ("v_step", "t_step", "a_step", "stored", "scored"))
        fix = fix_first_ends(nc, name, net.RG, W_)
        value = {}
        with nc.Block(name) as block:
            @block.gpsimd
            def _(pool):
                if layer == 1:
                    gather_columns(nc, pool, net.T2, net.q, b)
                pool.wait_ge(out_done, 16)
                fix_pool(nc, pool, fix, net.RG, net)

            @block.sync
            def _(sp):
                sp.wait_ge(scored, 1)
                sp.dma_start(net.RG.rearrange("(p t) d -> p t d", t=T), Y[:, :, :]).then_inc(out_done, 16)
                sp.wait_ge(out_done, 16)

            @block.vector
            def _(v):
                steps = [0]

                def link(ins):
                    steps[0] += 1
                    ins.then_inc(step, 1)
                    v.wait_ge(step, steps[0])
                link(nc.vector.tensor_copy(own[:, :, :], net.ad[:, H:2 * H, :]))
                owner_scan(nc, link, net, own[:, :, :], of_owner)
                value["scores"] = steps[0]
                v.wait_ge(t_step, 1)
                owner_carry(nc, link, net, ps[0][:, 0:H], of_owner)
                a_edge, seg = net.a_edge[:, layer * H:(layer + 1) * H, :], net.seg[:, layer * H:(layer + 1) * H, :]
                link(nc.vector.tensor_tensor(of_owner[:, :, :], of_owner[:, :, :], a_edge, ALU.add))
                link(nc.vector.tensor_tensor(own[:, :, :], net.ad[:, 0:H, :], net.ad[:, H:2 * H, :], ALU.add))
                link(nc.vector.tensor_tensor(own[:, :, :], own[:, :, :], seg, ALU.add))
                link(nc.vector.scalar_tensor_tensor(out=own[:, :, :], in0=own[:, :, :], scalar=NEG_SLOPE, in1=own[:, :, :], op0=ALU.mult, op1=ALU.max))
                if layer == 1:
                    with v.Fori(0, NB // 2) as k:
                        for half in range(2):
                            v.wait_ge(b["arrived"][half], k * (16 * U) + 16 * U)
                            nc.vector.tensor_copy(Y[:, bass.ds((k * 2 + half) * U, U), :], b["ring"][:, half, :, 0:W_]).then_inc(b["freed"][half], 1)
                    for half in range(2):
                        v.wait_ge(b["freed"][half], NB // 2)
                scores_in = Y[:, :, D:W_].rearrange("p t h -> p h t")
                link(nc.vector.tensor_tensor(alpha[:, :, :], scores_in, of_owner[:, :, :], ALU.add))
                link(nc.vector.scalar_tensor_tensor(out=alpha[:, :, :], in0=alpha[:, :, :], scalar=NEG_SLOPE, in1=alpha[:, :, :], op0=ALU.mult, op1=ALU.max))
                link(nc.vector.tensor_scalar(mask[:, :], net.cont[:, :], -1.0, BIG, ALU.add, ALU.mult))
                for h in range(H):
                    last = nc.vector.tensor_tensor_scan(m[:, h, :], mask[:, :], alpha[:, h, :], 0.0, ALU.add, ALU.max)
                link(last)
                for h in range(H):
                    last = nc.vector.tensor_scalar(diag[:, h, :], net.ident[:, :], m[:, h, T - 1:T], None, ALU.mult)
                link(last)
                value["maxima"] = steps[0]
                v.wait_ge(t_step, 2)
                for h in range(H):
                    last = nc.vector.tensor_tensor(diag[:, h, :], ps[1][:, h * P:(h + 1) * P], net.earlier[:, :], ALU.mult)
                link(last)
                link(nc.vector.tensor_tensor(diag[:, :, :], diag[:, :, :], net.earlier_mask[:, :].unsqueeze(1).to_broadcast([P, H, P]), ALU.add))
                link(nc.vector.tensor_reduce(cm[:, :], diag[:, :, :], AX_X, ALU.max))
                link(nc.vector.tensor_scalar(mask[:, :], net.first[:, :], -1.0, BIG, ALU.add, ALU.mult))
                for h in range(H):
                    last = nc.vector.scalar_tensor_tensor(out=m[:, h, :], in0=mask[:, :], scalar=cm[:, h:h + 1], in1=m[:, h, :], op0=ALU.add, op1=ALU.max)
                link(last)
                link(nc.vector.tensor_tensor(m[:, :, :], m[:, :, :], own[:, :, :], ALU.max))
                link(nc.vector.tensor_tensor(own[:, :, :], own[:, :, :], m[:, :, :], ALU.subtract))
                value["own"] = steps[0]
                owner_scan(nc, link, net, m[:, :, :], of_owner)
                value["max"] = steps[0]
                v.wait_ge(t_step, 3)
                owner_carry(nc, link, net, ps[2][:, 0:H], of_owner)
                link(nc.vector.tensor_tensor(alpha[:, :, :], alpha[:, :, :], of_owner[:, :, :], ALU.subtract))
                value["alpha"] = steps[0]
                v.wait_ge(a_step, 2)
                for i in range(NB):
                    cols = slice(i * U, (i + 1) * U)
                    nc.vector.tensor_tensor(Y[:, cols, 0:D].rearrange("p t (h c) -> p t h c", h=H), Y[:, cols, 0:D].rearrange("p t (h c) -> p t h c", h=H),
                                            alpha[:, :, cols].rearrange("p h t -> p t h").unsqueeze(3).to_broadcast([P, U, H, CH]), ALU.mult)
                link(nc.vector.tensor_copy(scores_in, alpha[:, :, :]))
                for d in range(W_):
                    last = nc.vector.tensor_tensor_scan(Y[:, :, d], net.cont[:, :], Y[:, :, d], 0.0, ALU.mult, ALU.add)
                last.then_inc(scored, 1)
                fix_vector(nc, v, fix, ps[3], W_)

            @block.scalar
            def _(act):
                act.wait_ge(step, value["own"])
                nc.scalar.activation(net.pself[:, :, :], own[:, :, :], ACT.Exp).then_inc(a_step, 1)
                act.wait_ge(step, value["alpha"])
                nc.scalar.activation(alpha[:, :, :], alpha[:, :, :], ACT.Exp).then_inc(a_step, 1)

            @block.tensor
            def _(pe):
                pe.wait_ge(step, value["scores"])
                nc.tensor.matmul(ps[0][:, 0:H], net.earlier[:, :], of_owner[:, :, 0], start=True, stop=True).then_inc(t_step, 1)
                pe.wait_ge(step, value["maxima"])
                nc.tensor.matmul(ps[1][:, :], net.ones[:, :], diag[:, :, :].rearrange("p h q -> p (h q)"), start=True, stop=True).then_inc(t_step, 1)
                pe.wait_ge(step, value["max"])
                nc.tensor.matmul(ps[2][:, 0:H], net.earlier[:, :], of_owner[:, :, 0], start=True, stop=True).then_inc(t_step, 1)
                pe.wait_ge(scored, 1)
                nc.tensor.matmul(ps[3][:, 0:W_], net.later[:, :], Y[:, T - 1, :], start=True, stop=True).then_inc(fix["carried"], 1)


GAT_STEPS = ["den_made", "inv_made", "self_made", "num_made", "gat_made"]


def gat_divide(c, net, v, it):
    nc, f = c.nc, c.buf
    own = lambda g: net.pself[:, :, bass.ds(column_of(c, it, g), S)].rearrange("p h s -> p s h")
    heads = lambda buf: buf[:, :, 0:D].rearrange("p s (h c) -> p s h c", h=H)
    each_group(c, v, it, ["r"], lambda g: nc.vector.scalar_tensor_tensor(out=f["inv"][g][:, :, :], in0=f["r"][g][:, :, D:D + H], scalar=1e-16,
                                                                  in1=own(g), op0=ALU.add, op1=ALU.add), "den_made")
    each_group(c, v, it, ["den_made"], lambda g: nc.vector.reciprocal(f["inv"][g][:, :, :], f["inv"][g][:, :, :]), "inv_made")
    each_group(c, v, it, ["self_made"], lambda g: nc.vector.tensor_tensor(f["r"][g][:, :, 0:D], f["r"][g][:, :, 0:D], f["xh"][g][:, :, 0:D], ALU.add), "num_made")
    each_group(c, v, it, ["num_made", "inv_made"], lambda g: nc.vector.tensor_tensor(
        heads(f["r"][g]), heads(f["r"][g]), f["inv"][g][:, :, :].unsqueeze(3).to_broadcast([P, S, H, CH]), ALU.mult), "gat_made")


def gat_own(c, net, pool, it):
    nc, f = c.nc, c.buf
    own = lambda g: net.pself[:, :, bass.ds(column_of(c, it, g), S)].rearrange("p h s -> p s h")
    heads = lambda buf: buf[:, :, 0:D].rearrange("p s (h c) -> p s h c", h=H)
    each_group(c, pool, it, ["xh"], lambda g: nc.gpsimd.tensor_tensor(heads(f["xh"][g]), heads(f["xh"][g]), own(g).unsqueeze(3).to_broadcast([P, S, H, CH]), ALU.mult), "self_made")


def phase_gat1_rows(nc, net):
    w = net.w
    with nc.cleanup_on_exit():
        c = Pass(nc, "gat1_rows", EDGE_ITERS, EDGE_STEP, "edges", [("r", D + H), ("xh", WA), ("inv", H), ("hT", D), ("t2", WA)],
                 ["r", "xh", "T2"], GAT_STEPS + ["turned", "h1T_made", "xh2_done", "t2_made", "ad_made"])
        f = c.buf
        with nc.Block("gat1_rows") as block:
            @block.sync
            def _(sp):
                prime(c, sp, ["T2"])
                load_rows(c, sp, "r", f["r"], net.RG, 0)
                load_rows(c, sp, "xh", f["xh"], net.AD1, 0)

                def iteration(it, more):
                    if more:
                        reload_rows(c, sp, "xh", f["xh"], net.AD1, it, "num_made")
                        reload_rows(c, sp, "r", f["r"], net.RG, it, "turned")
                    store_rows(c, sp, "T2", net.T2, f["t2"], it, "t2_made", base=N)
                with sp.Fori(0, c.iters - 1) as it:
                    iteration(it, True)
                iteration(c.iters - 1, False)
                settle(c, sp, ["T2"])

            @block.vector
            def _(v):
                with v.Fori(0, c.iters) as it:
                    gat_divide(c, net, v, it)

            @block.scalar
            def _(act):
                with act.Fori(0, c.iters) as it:
                    each_group(c, act, it, ["turned"], lambda g: nc.scalar.activation(flat(f["hT"][g]), c.psA[g][:, :], ACT.Relu, bias=w["b1"][:, 0:1]), "h1T_made")
                    gat_rows_act(c, net, act, it, f["t2"], "t2_made", ["xh2_done"], "T2")
                    each_group(c, act, it, [], lambda g: nc.scalar.activation(
                        net.ad[:, :, bass.ds(column_of(c, it, g), S)], c.psA[g][:, 0:S * 2 * H].rearrange("p (j k) -> p k j", j=S), ACT.Copy), "ad_made")

            @block.tensor
            def _(pe):
                for s_ in c.sem["ad_made"]:
                    pe.sem_inc(s_, c.per)
                with pe.Fori(0, c.iters) as it:
                    each_group(c, pe, it, ["ad_made", "gat_made"], lambda g: turn_group(c, net, f["r"][g], c.psA[g]), "turned")
                    for g in range(G):
                        pe.wait_ge(c.sem["h1T_made"][g // c.per], at_value(c, it, g))
                        row_product(c, f["hT"][g], w["W2"][:, 0:D], c.psB[g], net, "b2")
                        score_product(c, f["hT"][g], w["W2"][:, D:WA], c.psA[g]).then_inc(c.sem["xh2_done"][g // c.per], 1)

            @block.gpsimd
            def _(pool):
                with pool.Fori(0, c.iters) as it:
                    gat_own(c, net, pool, it)


def phase_gat2_rows(nc, net):
    w = net.w
    with nc.cleanup_on_exit():
        c = Pass(nc, "gat2_rows", EDGE_ITERS, EDGE_STEP, "edges", [("r", D + H), ("xh", WA), ("inv", H), ("xd", D), ("x2", D), ("n", D), ("h1", D), ("o", D)],
                 ["r", "xh", "xd", "HD", "XHX"], GAT_STEPS + ["x1_made", "n1_made", "h1_made", "x2_made"], norms=2)
        f = c.buf
        with nc.Block("gat2_rows") as block:
            @block.sync
            def _(sp):
                prime(c, sp, ["HD", "XHX"])
                load_rows(c, sp, "r", f["r"], net.RG, 0)
                load_rows(c, sp, "xh", f["xh"], net.T2, 0, base=N)
                load_rows(c, sp, "xd", f["xd"], net.XD, 0)

                def iteration(it, more):
                    if more:
                        reload_rows(c, sp, "xh", f["xh"], net.T2, it, "num_made", base=N)
                        reload_rows(c, sp, "r", f["r"], net.RG, it, "x1_made")
                        reload_rows(c, sp, "xd", f["xd"], net.XD, it, "x1_made")
                    store_rows(c, sp, "HD", net.HD, f["h1"], it, "h1_made")
                    store_rows(c, sp, "XHX", net.XHX, f["o"], it, "x2_made", base=N)
                with sp.Fori(0, c.iters - 1) as it:
                    iteration(it, True)
                iteration(c.iters - 1, False)
                settle(c, sp, ["HD", "XHX"])

            @block.vector
            def _(v):
                with v.Fori(0, c.iters) as it:
                    gat_divide(c, net, v, it)
                    each_group(c, v, it, ["xd", "gat_made"], lambda g: nc.vector.tensor_tensor(
                        f["x2"][g][:, :, :], f["r"][g][:, :, 0:D], f["xd"][g][:, :, :], ALU.add), "x1_made")
                    take_statistics(c, v, it, 1, f["x2"], ["x1_made"])
                    normalize(c, v, it, 1, f["n"], f["x2"], "n1_made")

            @block.scalar
            def _(act):
                with act.Fori(0, c.iters) as it:
                    take_root(c, act, net, it, 1)
                    each_group(c, act, it, ["HD", "n1_made"], lambda g: nc.scalar.activation(flat(f["h1"][g]), flat(f["n"][g]), ACT.Relu), "h1_made")

            @block.gpsimd
            def _(pool):
                with pool.Fori(0, c.iters) as it:
                    gat_own(c, net, pool, it)
                    each_group(c, pool, it, ["XHX", "h1_made"], lambda g: nc.gpsimd.tensor_tensor(
                        flat(f["o"][g]), flat(f["x2"][g]), flat(f["h1"][g]), ALU.add), "x2_made")


def phase_source_rows(nc, net, out):
    w = net.w
    with nc.cleanup_on_exit():
        ios = ["XHX", "PS", "GT0", "GT1", "GT2"]
        c = Pass(nc, "source_rows", EDGE_ITERS, EDGE_STEP, "edges",
                 [(n_, D) for n_ in ("x2", "n", "hT", "h2", "x0T", "xT", "o", "xs", "c1", "c2", "c3", "p", "r0", "r1", "r2")],
                 ["xs", "c1", "c2", "c3"] + ios,
                 ["a_made", "b_made", "x2_made", "n2_made", "x2b_made", "h2_made", "h2_turned", "h2T_made", "p_done", "p_made",
                  "u_done", "uT_made", "upd_done", "y_made", "yg_made", "x3_made", "n4_made", "h3_turned", "h3T_made",
                  "x0_done", "x0T_made", "c1_done", "x1T_made", "g1_made", "c2_done", "x2T_made", "g2_made", "c3_done",
                  "x3T_made", "o_done", "o_made", "x0_turned", "r0_made", "x1_turned", "r1_made", "x2_turned", "r2_made"],
                 norms=5, streams=2, gathered=("xs",))
        f = c.buf
        places = scatter_stage(nc, c, "source_out")
        b = gather_stage(nc, "xs")
        p_complete = nc.alloc_semaphore("p_complete")
        loads = [("c1", net.C1), ("c2", net.C2), ("c3", net.C3)]
        with nc.Block("source_rows") as block:
            @block.sync
            def _(sp):
                prime(c, sp, ios)
                for n_, table in loads:
                    load_rows(c, sp, n_, f[n_], table, 0)

                def half(front, back, reload=()):
                    for part in reload:
                        for n_, table in loads:
                            reload_rows(c, sp, n_, f[n_], table, part, "x2_made")
                    store_rows(c, sp, "XHX", net.XHX, f["x2"], front, "x2_made", base=N + EP)
                    store_rows(c, sp, "GT0", net.GT[0], f["r0"], back, "r0_made", base=EP)
                    store_rows(c, sp, "PS", net.PS, f["p"], front, "p_made", noted=p_complete)
                    for k in range(1, 3):
                        store_rows(c, sp, f"GT{k}", net.GT[k], f[f"r{k}"], back, f"r{k}_made", base=EP)
                half((0, 0), None)
                with sp.Fori(0, c.iters - 1) as it:
                    half((it, 1), (it, 0), [(it, 0)])
                    half((it + 1, 0), (it, 1), [(it, 1)])
                half((c.iters - 1, 1), (c.iters - 1, 0))
                half(None, (c.iters - 1, 1))
                settle(c, sp, ios)

            @block.vector
            def _(v):
                add = lambda dst, a, b: nc.vector.tensor_tensor(flat(dst), a, b, ALU.add)

                def output(part):
                    if part is None:
                        return
                    it, groups = groups_of(c, part)
                    for g in groups:
                        v.wait_ge(places["free"][g // c.per], at_value(c, it, g))
                        v.wait_ge(c.sem["o_done"][g // c.per], at_value(c, it, g))
                        add(f["o"][g], c.psB[g][:, :], flat(f["x2"][g])).then_inc(c.sem["o_made"][g // c.per], 1)

                def half(front, back, coming=None):
                    each_group(c, v, front, ["a_made", "b_made"], lambda g: add(f["x2"][g], flat(f["c1"][g]), flat(f["c3"][g])), "x2_made")
                    take_statistics(c, v, front, 2, f["x2"], ["x2_made"])
                    normalize(c, v, front, 2, f["n"], f["x2"], "n2_made")
                    each_group(c, v, back, ["x1T_made"], lambda g: add(f["hT"][g], flat(f["xT"][g]), flat(f["x0T"][g])), "g1_made")
                    beta_step(c, net, v, front)
                    each_group(c, v, back, ["x2T_made"], lambda g: add(f["hT"][g], flat(f["xT"][g]), flat(f["x0T"][g])), "g2_made")
                    update_step(c, v, front)
                    layer_norm_affine(c, net, v, front)
                    output(back)
                    take_statistics(c, v, front, 4, f["x2"], ["x3_made"])
                    normalize(c, v, front, 4, f["n"], f["x2"], "n4_made")
                staggered(c, v, half)

            @block.scalar
            def _(act):
                psA, psB = (lambda g: c.psA[g][:, :]), (lambda g: c.psB[g][:, :])

                def half(front, back, coming=None):
                    relu_step(c, act, back, ["h3_turned"], f["hT"], psA, "h3T_made")
                    relu_step(c, act, back, ["x0_done"], f["x0T"], psB, "x0T_made", bias=w["fc1_b"][:, 0:1], scale=1.0 / X0_SCALE)
                    take_root(c, act, net, front, 2)
                    relu_step(c, act, back, ["c1_done"], f["xT"], psA, "x1T_made")
                    copy_step(c, act, back, ["GT0", "x0_turned"], f["r0"], psB, "r0_made", scale=X0_SCALE)
                    copy_step(c, act, back, ["GT1", "x1_turned"], f["r1"], psA, "r1_made")
                    relu_step(c, act, front, ["n2_made"], f["h2"], lambda g: flat(f["n"][g]), "h2_made")
                    copy_step(c, act, front, ["h2_turned"], f["hT"], psA, "h2T_made")
                    relu_step(c, act, back, ["c2_done"], f["xT"], psB, "x2T_made")
                    copy_step(c, act, front, ["PS", "p_done"], f["p"], psB, "p_made")
                    relu_step(c, act, front, ["u_done"], f["hT"], psA, "uT_made", bias=w["bu1"][:, 0:1])
                    copy_step(c, act, back, ["GT2", "x2_turned"], f["r2"], psB, "r2_made")
                    relu_step(c, act, back, ["c3_done"], f["hT"], psA, "x3T_made")
                    take_root(c, act, net, front, 3)
                    take_root(c, act, net, front, 4)
                staggered(c, act, half)

            @block.tensor
            def _(pe):
                turned = lambda src, ps: (lambda g: turn_group(c, net, f[src][g], ps[g]))

                def half(front, back, coming=None):
                    each_group(c, pe, back, ["n4_made"], turned("n", c.psA), "h3_turned")
                    each_group(c, pe, back, ["h3T_made"], lambda g: column_product(c, f["hT"][g], w["fc1"][:, :], c.psB[g]), "x0_done")
                    each_group(c, pe, back, ["x0T_made"], lambda g: column_product(c, f["x0T"][g], w["conv_lone"][:, :], c.psA[g]), "c1_done")
                    each_group(c, pe, back, [], turned("x0T", c.psB), "x0_turned")
                    each_group(c, pe, back, ["x1T_made"], turned("xT", c.psA), "x1_turned")
                    each_group(c, pe, front, ["h2_made"], turned("h2", c.psA), "h2_turned")
                    each_group(c, pe, back, ["g1_made", "r0_made"], lambda g: column_product(c, f["hT"][g], w["conv1"][:, :], c.psB[g]), "c2_done")
                    each_group(c, pe, front, ["o_made", "h2T_made"], lambda g: row_product(c, f["hT"][g], w["Wm1a"][:, :], c.psB[g]), "p_done")
                    each_group(c, pe, front, [], lambda g: column_product(c, f["hT"][g], w["Wu1a"][:, :], c.psA[g]), "u_done")
                    each_group(c, pe, back, ["x2T_made"], turned("xT", c.psB), "x2_turned")
                    each_group(c, pe, back, ["r1_made", "g2_made"], lambda g: column_product(c, f["hT"][g], w["conv2"][:, :], c.psA[g]), "c3_done")
                    each_group(c, pe, front, ["p_made", "uT_made"], lambda g: row_product(c, f["hT"][g], w["Wu2"][:, :], c.psB[g], net, "bu2"), "upd_done")
                    each_group(c, pe, back, ["r2_made", "x3T_made"], lambda g: row_product(c, f["hT"][g], w["fc2"][:, :], c.psB[g], net, "fc2_b"), "o_done")
                for s_ in c.sem["o_made"]:
                    pe.sem_inc(s_, c.per)
                staggered(c, pe, half)

            @block.gpsimd
            def _(pool):
                add = lambda dst, a: nc.gpsimd.tensor_tensor(flat(dst), flat(dst), flat(a), ALU.add)

                def half(front, back, coming=None, fetch=True):
                    each_group(c, pool, coming, ["c1", "c2"], lambda g: add(f["c1"][g], f["c2"][g]), "a_made")
                    each_group(c, pool, coming, ["c3", "xs"], lambda g: add(f["c3"][g], f["xs"][g]), "b_made")
                    if front is not None and fetch:
                        gather_rows(nc, pool, c, b, "xs", net.S.q, net.XHX[0:N + EP, :], f["xs"], front, freed="x2_made")
                    scatter_rows(nc, pool, c, places, back, net.S.own_idx, out, f["o"], "o_made")
                for s_ in places["free"]:
                    pool.sem_inc(s_, c.per)
                gather_rows(nc, pool, c, b, "xs", net.S.q, net.XHX[0:N + EP, :], f["xs"])
                last = c.iters - 1
                half(None, None, (0, 0))
                half((0, 0), None, (0, 1))
                with pool.Fori(0, last - 1) as it:
                    half((it, 1), (it, 0), (it + 1, 0))
                    half((it + 1, 0), (it, 1), (it + 1, 1))
                half((last - 1, 1), (last - 1, 0), (last, 0))
                half((last, 0), (last - 1, 1), (last, 1), fetch=False)
                half((last, 1), (last, 0), None, fetch=False)
                half(None, (last, 1), None)


def phase_message_rows(nc, net):
    w = net.w
    with nc.cleanup_on_exit():
        c = Pass(nc, "message_rows", EDGE_ITERS, EDGE_STEP, "edges", [("arriving", D), ("x", D), ("ea", KE64), ("n", D), ("h2", D), ("hT", D), ("eT", D), ("z", D)],
                 ["arriving", "ea", "X2D", "H2D", "Z"], ["x_made", "n2_made", "h2_made", "turned", "hT_made", "eT_made", "z_done", "z_made"], norms=1, gathered=("arriving",))
        f = c.buf
        b = gather_stage(nc, "x2")
        with nc.Block("message_rows") as block:
            @block.sync
            def _(sp):
                prime(c, sp, ["X2D", "H2D", "Z"])
                load_rows(c, sp, "ea", f["ea"], net.EA64, 0)

                def iteration(it, more):
                    if more:
                        reload_rows(c, sp, "ea", f["ea"], net.EA64, it, "turned")
                    store_rows(c, sp, "X2D", net.X2D, f["x"], it, "x_made")
                    store_rows(c, sp, "H2D", net.H2D, f["h2"], it, "h2_made")
                    store_rows(c, sp, "Z", net.Z, f["z"], it, "z_made", primed=c.per)
                with sp.Fori(0, c.iters - 1) as it:
                    iteration(it, True)
                iteration(c.iters - 1, False)
                settle(c, sp, ["X2D", "H2D", "Z"])

            @block.vector
            def _(v):
                with v.Fori(0, c.iters) as it:
                    take_statistics(c, v, it, 0, f["x"], ["x_made"])
                    normalize(c, v, it, 0, f["n"], f["x"], "n2_made")

            @block.scalar
            def _(act):
                with act.Fori(0, c.iters) as it:
                    copy_step(c, act, it, ["arriving", "X2D"], f["x"], lambda g: flat(f["arriving"][g]), "x_made")
                    take_root(c, act, net, it, 0)
                    each_group(c, act, it, ["H2D", "n2_made"], lambda g: nc.scalar.activation(flat(f["h2"][g]), flat(f["n"][g]), ACT.Relu), "h2_made")
                    each_group(c, act, it, ["turned"], lambda g: nc.scalar.activation(flat(f["hT"][g]), c.psA[g][:, :], ACT.Copy), "hT_made")
                    each_group(c, act, it, [], lambda g: nc.scalar.activation(f["eT"][g][0:KE64, :, :].rearrange("p j d -> p (j d)"),
                                                                                  c.psB[g][0:KE64, :], ACT.Copy), "eT_made")
                    each_group(c, act, it, ["Z", "z_done"], lambda g: nc.scalar.activation(flat(f["z"][g]), c.psB[g][:, :], ACT.Copy), "z_made")

            @block.tensor
            def _(pe):
                for s_ in c.sem["z_made"]:
                    pe.sem_inc(s_, c.per)

                def z_rows(g):
                    nc.tensor.matmul(c.psB[g][:, :], net.ones_b[:, :], net.parts["bm1"][:, :, :].rearrange("p j d -> p (j d)"), start=True, stop=False)
                    for j in range(S):
                        ps = c.psB[g][:, j * P:(j + 1) * P]
                        nc.tensor.matmul(ps, f["hT"][g][:, j, :], w["Wm1b"][:, :], start=False, stop=False)
                        last = nc.tensor.matmul(ps, f["eT"][g][0:KE64, j, :], w["Wm1c"][:, :], start=False, stop=j == S - 1)
                    return last
                with pe.Fori(0, c.iters) as it:
                    for g in range(G):
                        pe.wait_ge(c.sem["z_made"][g // c.per], at_value(c, it, g))
                        loaded(c, pe, "ea", it, g)
                        pe.wait_ge(c.sem["h2_made"][g // c.per], at_value(c, it, g))
                        turn_group(c, net, f["h2"][g], c.psA[g])
                        turn_group(c, net, f["ea"][g], c.psB[g], KE64).then_inc(c.sem["turned"][g // c.per], 1)
                    each_group(c, pe, it, ["hT_made", "eT_made"], z_rows, "z_done")

            @block.gpsimd
            def _(pool):
                gather_rows(nc, pool, c, b, "arriving", net.home2, net.XHX, f["arriving"])
                with pool.Fori(0, c.iters - 1) as it:
                    gather_rows(nc, pool, c, b, "arriving", net.home2, net.XHX, f["arriving"], it, freed="x_made")


def phase_update_rows(nc, net):
    w = net.w
    with nc.cleanup_on_exit():
        ios = ["X3D", "X0D", "GT0"]
        c = Pass(nc, "update_rows", EDGE_ITERS, EDGE_STEP, "edges",
                 [(n_, D) for n_ in ("h2", "x2", "r", "count", "hT", "rT", "n", "x0T", "x0", "g0")], ["h2", "x2", "r"] + ios,
                 ["count_made", "h2_turned", "h2T_made", "r_turned", "rT_made", "u_done", "uT_made", "upd_done", "x2b_made",
                  "y_made", "yg_made", "x3_made", "n4_made", "h3_turned", "h3T_made", "x0_done", "x0T_made", "x0_turned", "x0_made", "g0_made"], norms=5)
        f = c.buf
        loads = [("h2", net.H2D, "x3_made"), ("r", net.RM, "r_turned")]
        with nc.Block("update_rows") as block:
            @block.sync
            def _(sp):
                prime(c, sp, ios)
                for n_, table, _ in loads:
                    load_rows(c, sp, n_, f[n_], table, 0)
                load_rows(c, sp, "x2", f["x2"], net.X2D, 0)

                def iteration(it, more):
                    if more:
                        for n_, table, freed in reversed(loads):
                            reload_rows(c, sp, n_, f[n_], table, it, freed)
                    store_rows(c, sp, "X3D", net.X3D, f["x2"], it, "x3_made")
                    if more:
                        for g in range(G):
                            sp.wait_ge(c.io["X3D"][g], it * 16 + 32)
                        reload_rows(c, sp, "x2", f["x2"], net.X2D, it, "n4_made")
                    store_rows(c, sp, "X0D", net.X0D, f["x0"], it, "x0_made", primed=c.per)
                    store_rows(c, sp, "GT0", net.GT[0], f["g0"], it, "g0_made")
                with sp.Fori(0, c.iters - 1) as it:
                    iteration(it, True)
                iteration(c.iters - 1, False)
                settle(c, sp, ios)

            @block.vector
            def _(v):
                with v.Fori(0, c.iters) as it:
                    each_group(c, v, it, ["upd_done"], lambda g: nc.vector.tensor_tensor(flat(f["h2"][g]), c.psB[g][:, :], flat(f["h2"][g]), ALU.add), "y_made")
                    layer_norm_affine(c, net, v, it)
                    take_statistics(c, v, it, 4, f["x2"], ["x3_made"])
                    normalize(c, v, it, 4, f["n"], f["x2"], "n4_made")
                    for g in range(G):
                        stored(c, v, "GT0", it, g)
                        v.wait_ge(c.sem["x0_made"][g // c.per], at_value(c, it, g) + c.per)
                        for j in range(S):
                            last = nc.vector.tensor_scalar(f["g0"][g][:, j, :], f["x0"][g][:, j, :], net.dinv[:, bass.ds(column_of(c, it, g) + j, 1)], X0_SCALE, ALU.mult, ALU.mult)
                        last.then_inc(c.sem["g0_made"][g // c.per], 1)

            @block.scalar
            def _(act):
                relu = lambda dst, src, **kw: nc.scalar.activation(flat(dst), src, ACT.Relu, **kw)
                copy = lambda dst, src, **kw: nc.scalar.activation(flat(dst), src, ACT.Copy, **kw)
                with act.Fori(0, c.iters) as it:
                    each_group(c, act, it, ["h2_turned"], lambda g: copy(f["hT"][g], c.psA[g][:, :]), "h2T_made")
                    each_group(c, act, it, ["r_turned"], lambda g: copy(f["rT"][g], c.psB[g][:, :]), "rT_made")
                    each_group(c, act, it, ["u_done"], lambda g: relu(f["hT"][g], c.psA[g][:, :], bias=w["bu1"][:, 0:1]), "uT_made")
                    take_root(c, act, net, it, 3)
                    take_root(c, act, net, it, 4)
                    each_group(c, act, it, ["h3_turned"], lambda g: relu(f["hT"][g], c.psA[g][:, :]), "h3T_made")
                    each_group(c, act, it, ["x0_done"], lambda g: relu(f["x0T"][g], c.psB[g][:, :], bias=w["fc1_b"][:, 0:1], scale=1.0 / X0_SCALE), "x0T_made")
                    each_group(c, act, it, ["X0D", "x0_turned"], lambda g: copy(f["x0"][g], c.psA[g][:, :]), "x0_made")

            @block.tensor
            def _(pe):
                for s_ in c.sem["x0_made"]:
                    pe.sem_inc(s_, c.per)
                def update(g):
                    nc.tensor.matmul(c.psA[g][:, :], w["Wu1a"][:, :], flat(f["hT"][g]), start=True, stop=False)
                    nc.tensor.matmul(c.psA[g][:, :], w["Wm2u"][:, :], flat(f["rT"][g]), start=False, stop=False)
                    return nc.tensor.matmul(c.psA[g][:, :], w["bm2u"][:, :], flat(f["count"][g]), start=False, stop=True)
                with pe.Fori(0, c.iters) as it:
                    for g in range(G):
                        pe.wait_ge(c.sem["x0_made"][g // c.per], at_value(c, it, g))
                        loaded(c, pe, "h2", it, g)
                        turn_group(c, net, f["h2"][g], c.psA[g]).then_inc(c.sem["h2_turned"][g // c.per], 1)
                    each_group(c, pe, it, ["r"], lambda g: turn_group(c, net, f["r"][g], c.psB[g]), "r_turned")
                    each_group(c, pe, it, ["h2T_made", "rT_made", "count_made"], update, "u_done")
                    each_group(c, pe, it, ["uT_made"], lambda g: row_product(c, f["hT"][g], w["Wu2"][:, :], c.psB[g], net, "bu2"), "upd_done")
                    each_group(c, pe, it, ["n4_made"], lambda g: turn_group(c, net, f["n"][g], c.psA[g]), "h3_turned")
                    each_group(c, pe, it, ["h3T_made"], lambda g: column_product(c, f["hT"][g], w["fc1"][:, :], c.psB[g]), "x0_done")
                    each_group(c, pe, it, ["x0T_made"], lambda g: turn_group(c, net, f["x0T"][g], c.psA[g]), "x0_turned")

            @block.gpsimd
            def _(pool):
                counts = lambda g, it: net.seg[:, 2 * H, bass.ds(column_of(c, it, g), S)].unsqueeze(2).to_broadcast([P, S, D])
                with pool.Fori(0, c.iters) as it:
                    each_group(c, pool, it, ["h2"], lambda g: nc.gpsimd.tensor_tensor(
                        f["count"][g][:, :, :], slots(net.ident), counts(g, it), ALU.mult), "count_made")
                    each_group(c, pool, it, ["x2"], lambda g: nc.gpsimd.tensor_tensor(
                        f["x2"][g][:, :, :], f["x2"][g][:, :, :], slots(w["beta"]), ALU.add), "x2b_made")


def phase_gcn_rows(nc, net, i, out):
    w = net.w
    last_layer = i == GCN_LAYERS - 1
    with nc.cleanup_on_exit():
        c = Pass(nc, f"gcn_rows{i}", EDGE_ITERS, EDGE_STEP, "edges",
                 [(n_, D) for n_ in ("r", "g", "x0", "h", "hT", "o") + (("x3", "xT") if last_layer else ())],
                 ["r", "g", "x0", "x3", "GT"], ["s_made", "h_made", "turned", "hT_made", "x_done", "xT_made", "o_done", "o_made"])
        f = c.buf
        loads = [("g", net.GT[i], "s_made"), ("r", net.RC[i], "h_made"), ("x0", net.X0D, "h_made")]
        places = scatter_stage(nc, c, f"gcn_out{i}") if last_layer else None
        with nc.Block(f"gcn_rows{i}") as block:
            @block.sync
            def _(sp):
                prime(c, sp, ["GT"])
                for n_, table, _ in loads:
                    load_rows(c, sp, n_, f[n_], table, 0)
                if last_layer:
                    load_rows(c, sp, "x3", f["x3"], net.X3D, 0)

                def iteration(it, more):
                    if more:
                        for n_, table, freed in loads:
                            reload_rows(c, sp, n_, f[n_], table, it, freed)
                        if last_layer:
                            reload_rows(c, sp, "x3", f["x3"], net.X3D, it, "o_made", primed=c.per)
                    if not last_layer:
                        store_rows(c, sp, "GT", net.GT[i + 1], f["o"], it, "o_made", primed=c.per)
                with sp.Fori(0, c.iters - 1) as it:
                    iteration(it, True)
                iteration(c.iters - 1, False)
                if not last_layer:
                    settle(c, sp, ["GT"])

            @block.vector
            def _(v):
                with v.Fori(0, c.iters) as it:
                    if last_layer:
                        each_group(c, v, it, ["r", "g"], lambda g: nc.vector.tensor_tensor(flat(f["r"][g]), flat(f["r"][g]), flat(f["g"][g]), ALU.add), "s_made")
                    for g in range(G):
                        loaded(c, v, "x0", it, g)
                        v.wait_ge(c.sem["s_made"][g // c.per], at_value(c, it, g))
                        for j in range(S):
                            last = nc.vector.scalar_tensor_tensor(out=f["h"][g][:, j, :], in0=f["r"][g][:, j, :], scalar=net.dinv[:, bass.ds(column_of(c, it, g) + j, 1)],
                                                                  in1=f["x0"][g][:, j, :], op0=ALU.mult, op1=ALU.add)
                        last.then_inc(c.sem["h_made"][g // c.per], 1)
                    if last_layer:
                        for g in range(G):
                            v.wait_ge(places["free"][g // c.per], at_value(c, it, g))
                            loaded(c, v, "x3", it, g)
                            v.wait_ge(c.sem["o_done"][g // c.per], at_value(c, it, g))
                            nc.vector.tensor_tensor(flat(f["o"][g]), c.psA[g][:, :], flat(f["x3"][g]), ALU.add).then_inc(c.sem["o_made"][g // c.per], 1)
                    else:
                        for g in range(G):
                            stored(c, v, "GT", it, g)
                            v.wait_ge(c.sem["x_done"][g // c.per], at_value(c, it, g))
                            for j in range(S):
                                last = nc.vector.tensor_scalar(f["o"][g][:, j, :], c.psB[g][:, j * P:(j + 1) * P], 0.0,
                                                               net.dinv[:, bass.ds(column_of(c, it, g) + j, 1)], ALU.max, ALU.mult)
                            last.then_inc(c.sem["o_made"][g // c.per], 1)

            @block.scalar
            def _(act):
                with act.Fori(0, c.iters) as it:
                    each_group(c, act, it, ["turned"], lambda g: nc.scalar.activation(flat(f["hT"][g]), c.psA[g][:, :], ACT.Copy), "hT_made")
                    if last_layer:
                        each_group(c, act, it, ["x_done"], lambda g: nc.scalar.activation(flat(f["xT"][g]), c.psB[g][:, :], ACT.Relu), "xT_made")

            @block.tensor
            def _(pe):
                for s_ in c.sem["o_made"]:
                    pe.sem_inc(s_, c.per)
                with pe.Fori(0, c.iters) as it:
                    each_group(c, pe, it, ["o_made", "h_made"], lambda g: turn_group(c, net, f["h"][g], c.psA[g]), "turned")
                    if last_layer:
                        each_group(c, pe, it, ["hT_made"], lambda g: column_product(c, f["hT"][g], w[f"conv{i}"][:, :], c.psB[g]), "x_done")
                        each_group(c, pe, it, ["xT_made"], lambda g: row_product(c, f["xT"][g], w["fc2"][:, :], c.psA[g], net, "fc2_b"), "o_done")
                    else:
                        each_group(c, pe, it, ["hT_made"], lambda g: row_product(c, f["hT"][g], w[f"conv{i}"][:, :], c.psB[g]), "x_done")

            @block.gpsimd
            def _(pool):
                if last_layer:
                    for s_ in places["free"]:
                        pool.sem_inc(s_, c.per)
                with pool.Fori(0, c.iters) as it:
                    if not last_layer:
                        each_group(c, pool, it, ["r", "g"], lambda g: nc.gpsimd.tensor_tensor(flat(f["r"][g]), flat(f["r"][g]), flat(f["g"][g]), ALU.add), "s_made")
                    else:
                        scatter_rows(nc, pool, c, places, it, net.own_idx, out, f["o"], "o_made")


_INS = ["x", "src", "dst", "edge_attr_16", "edge_attr_64", "edge_weight", "L0_gnn_W1", "L0_gnn_att_src1", "L0_gnn_att_dst1",
        "L0_gnn_W_edge1", "L0_gnn_att_edge1", "L0_gnn_bias1", "L0_gnn_W2", "L0_gnn_att_src2", "L0_gnn_att_dst2",
        "L0_gnn_W_edge2", "L0_gnn_att_edge2", "L0_gnn_bias2", "L2_gnn_Wm1", "L2_gnn_bm1", "L2_gnn_Wm2", "L2_gnn_bm2",
        "L2_gnn_Wu1", "L2_gnn_bu1", "L2_gnn_Wu2", "L2_gnn_bu2", "L2_gnn_gamma", "L2_gnn_beta", "L3_gnn_fc1_w",
        "L3_gnn_fc1_b", "L3_gnn_fc2_w", "L3_gnn_fc2_b", "L3_gnn_conv_w"]


def gnn_kernel(nc, inp, out):
    net = Net()
    allocate(nc, net)
    phase_setup(nc, net, inp)
    phase_own_rows(nc, net)
    phase_index(nc, net, inp, out)
    phase_gat(nc, net, 0)
    phase_gat1_rows(nc, net)
    phase_gat(nc, net, 1)
    phase_gat2_rows(nc, net)
    s_ = net.S
    phase_sum(nc, net, "light1", net.HD, s_.r, s_, net.C1, weight=s_.ew)
    phase_sum(nc, net, "light2", net.C1, s_.s, s_, net.C2, weight=s_.ew)
    phase_sum(nc, net, "light3", net.C2, s_.s, s_, net.C3, weight=s_.ew)
    phase_source_rows(nc, net, out)
    phase_message_rows(nc, net)
    phase_sum(nc, net, "messages", net.PS, net.s, net, net.RM, relu_with=net.Z)
    phase_update_rows(nc, net)
    for i in range(GCN_LAYERS):
        phase_sum(nc, net, f"gcn{i}", net.GT[i], net.home3, net, net.RC[i])
        phase_gcn_rows(nc, net, i, out)


def kernel(**inputs):
    import numpy as _np
    import concourse.bacc as _bacc
    from concourse import mybir as _mybir
    from concourse.bass_utils import run_bass_kernel_spmd as _run

    nc = _bacc.Bacc("TRN2", target_bir_lowering=False, num_devices=1)
    arrays, aps = {}, {}
    for name in _INS:
        a = _np.ascontiguousarray(inputs[name])
        arrays[f"in_{name}"] = a
        aps[name] = nc.dram_tensor(f"in_{name}", a.shape, _mybir.dt.from_np(a.dtype), kind="ExternalInput").ap()
    out = nc.dram_tensor("out", (N, D), F32, kind="ExternalOutput").ap()
    gnn_kernel(nc, aps, out)
    return _run(nc, [arrays], core_ids=[0]).results[0]["out"]
```
